# Optimizing a Trainium2 kernel written in Bass

```python
import numpy as np
import jax
import jax.numpy as jnp

def _softmax(x, axis=-1):
    return jax.nn.softmax(x, axis=axis)

def _gelu(x):
    return jax.nn.gelu(x, approximate=True)

def _silu(x):
    return jax.nn.silu(x)

def _sigmoid(x):
    return jax.nn.sigmoid(x)

def _layernorm(x, axis=-1, eps=1e-05):
    m = jnp.mean(x, axis=axis, keepdims=True)
    v = jnp.var(x, axis=axis, keepdims=True)
    return (x - m) / jnp.sqrt(v + eps)

def _scatter_add(tgt, idx, src, axis=0):
    return tgt.at[idx].add(src)

def _segment_sum(src, seg, n):
    return jax.ops.segment_sum(src, seg, n)
kernel_name = 'mk_recurrent_d2_jaxref_r8_157833'

def setup_inputs(seed: int=0):
    np.random.seed(seed)
    _w = jnp.asarray

    def _L0_attn_setup():
        import jax, jax.numpy as jnp
        import numpy as np
        H = 16
        CHUNK = 32
        TOPK = 4
        THETA = 10000.0
        EPS = 1e-06
        NEG = -1e+30
        POS = 1e+30

        def _rope(x, cos, sin):
            d2 = x.shape[-1] // 2
            x1, x2 = (x[..., :d2], x[..., d2:])
            return jnp.concatenate([x1 * cos - x2 * sin, x2 * cos + x1 * sin], axis=-1)
        key = jax.random.key(seed)
        ks = jax.random.split(key, 6)
        B, S, D = (1, 256, 256)
        scale = 0.02
        return {'hidden_states': jax.random.normal(ks[0], (B, S, D), jnp.float32), 'Wq': jax.random.normal(ks[1], (D, D), jnp.float32) * scale, 'Wk': jax.random.normal(ks[2], (D, D), jnp.float32) * scale, 'Wv': jax.random.normal(ks[3], (D, D), jnp.float32) * scale, 'Wo': jax.random.normal(ks[4], (D, D), jnp.float32) * scale, 'o_norm_w': jnp.ones((D // H,), jnp.float32)}
    _L0_attn_in = _L0_attn_setup()

    def _L0_ffn_setup():
        import jax, jax.numpy as jnp
        import numpy as np
        B, S, D = (4, 64, 256)
        E, K, H = (8, 2, 176)
        HS = 2 * 176
        ALPHA = 0.001
        W_SCALE = 0.02

        def _moe_forward(hidden_states, gate_w, w_gate, w_up, w_down, sw_gate, sw_up, sw_down):
            b, s, d = hidden_states.shape
            x = hidden_states.reshape(-1, d)
            T = x.shape[0]
            logits = x @ gate_w
            scores = jax.nn.softmax(logits, axis=-1)
            topk_w, topk_idx = jax.lax.top_k(scores, K)
            mask = jax.nn.one_hot(topk_idx, E, dtype=scores.dtype).sum(axis=1)
            ce = mask.mean(axis=0)
            Pi = scores.mean(axis=0)
            aux_loss = (Pi * ce * E).sum() * ALPHA
            comb = jnp.zeros((T, E), dtype=x.dtype)
            comb = comb.at[jnp.arange(T)[:, None], topk_idx].add(topk_w)
            g = jax.nn.silu(jnp.einsum('td,edh->teh', x, w_gate)) * jnp.einsum('td,edh->teh', x, w_up)
            routed = jnp.einsum('teh,ehd,te->td', g, w_down, comb)
            shared = jax.nn.silu(x @ sw_gate) * (x @ sw_up) @ sw_down
            out = (routed + shared).reshape(b, s, d)
            return (out, aux_loss)
        key = jax.random.key(seed)
        ks = jax.random.split(key, 8)
        rn = lambda k, sh: jax.random.normal(k, sh, dtype=jnp.float32)
        return {'hidden_states': rn(ks[0], (B, S, D)), 'gate_w': rn(ks[1], (D, E)) * W_SCALE, 'w_gate': rn(ks[2], (E, D, H)) * W_SCALE, 'w_up': rn(ks[3], (E, D, H)) * W_SCALE, 'w_down': rn(ks[4], (E, H, D)) * W_SCALE, 'sw_gate': rn(ks[5], (D, HS)) * W_SCALE, 'sw_up': rn(ks[6], (D, HS)) * W_SCALE, 'sw_down': rn(ks[7], (HS, D)) * W_SCALE}
    _L0_ffn_in = _L0_ffn_setup()

    def _L1_attn_setup():
        import jax, jax.numpy as jnp
        import numpy as np
        IN_DIM, HID, OUT_DIM = (256, 320, 256)
        KERNEL = 4
        C_RGLRU = 8.0

        def _rg_lru(u, Wa, ba, Wi, bi, lam):
            r = jax.nn.sigmoid(jnp.einsum('bsh,hk->bsk', u, Wa) + ba)
            i = jax.nn.sigmoid(jnp.einsum('bsh,hk->bsk', u, Wi) + bi)
            log_a = -C_RGLRU * jax.nn.softplus(-lam) * r
            a = jnp.exp(log_a)
            beta = jnp.sqrt(jnp.maximum(1.0 - jnp.exp(2.0 * log_a), 1e-12))
            drive = beta * (i * u)

            def step(h, ab):
                a_t, d_t = ab
                h = a_t * h + d_t
                return (h, h)
            h0 = jnp.zeros((u.shape[0], u.shape[2]), u.dtype)
            _, hs = jax.lax.scan(step, h0, (a.transpose(1, 0, 2), drive.transpose(1, 0, 2)))
            return hs.transpose(1, 0, 2)
        key = jax.random.key(seed)
        ks = jax.random.split(key, 16)
        s = 0.02
        return {'x': jax.random.normal(ks[0], (4, 256, IN_DIM), jnp.float32), 'Wl': jax.random.normal(ks[1], (IN_DIM, HID), jnp.float32) * s, 'bl': jnp.zeros((HID,), jnp.float32), 'Wr': jax.random.normal(ks[2], (IN_DIM, HID), jnp.float32) * s, 'br': jnp.zeros((HID,), jnp.float32), 'conv_w': jax.random.normal(ks[3], (KERNEL, 1, HID), jnp.float32) * 0.1, 'conv_b': jnp.zeros((HID,), jnp.float32), 'Wa': jax.random.normal(ks[4], (HID, HID), jnp.float32) * s, 'ba': jnp.zeros((HID,), jnp.float32), 'Wi': jax.random.normal(ks[5], (HID, HID), jnp.float32) * s, 'bi': jnp.zeros((HID,), jnp.float32), 'lam': jax.random.normal(ks[6], (HID,), jnp.float32) + 2.0, 'Wo': jax.random.normal(ks[7], (HID, OUT_DIM), jnp.float32) * s, 'bo': jnp.zeros((OUT_DIM,), jnp.float32)}
    _L1_attn_in = _L1_attn_setup()

    def _L1_ffn_setup():
        import jax, jax.numpy as jnp
        import numpy as np
        B, T, D = (4, 128, 256)
        N, S, H = (8, 8, 8)
        ETA = 1.0
        key = jax.random.key(seed)
        ks = jax.random.split(key, 9)
        return {'x': jax.random.normal(ks[0], (B, T, D), jnp.float32), 'select_weight': jax.random.normal(ks[1], (N, D, S), jnp.float32) / D, 'select_mean_diff': jax.random.normal(ks[2], (N, D), jnp.float32) / D, 'imp_center': jax.random.normal(ks[3], (N,), jnp.float32), 'imp_slope': jax.random.normal(ks[4], (N,), jnp.float32) * 5.0, 'lora_update': jax.random.normal(ks[5], (N, D, H), jnp.float32) * 0.02, 'lora_degen': jax.random.normal(ks[6], (N, D, H), jnp.float32) * 0.02, 'bias_w': jax.random.normal(ks[7], (N, D), jnp.float32) * 0.02, 'debias_w': jax.random.normal(ks[8], (N, D), jnp.float32) * 0.02}
    _L1_ffn_in = _L1_ffn_setup()
    _d = {'L0_attn_hidden_states': _L0_attn_in['hidden_states'], 'L0_attn_Wq': _L0_attn_in['Wq'], 'L0_attn_Wk': _L0_attn_in['Wk'], 'L0_attn_Wv': _L0_attn_in['Wv'], 'L0_attn_Wo': _L0_attn_in['Wo'], 'L0_attn_o_norm_w': _L0_attn_in['o_norm_w'], 'L0_ffn_gate_w': _L0_ffn_in['gate_w'], 'L0_ffn_w_gate': _L0_ffn_in['w_gate'], 'L0_ffn_w_up': _L0_ffn_in['w_up'], 'L0_ffn_w_down': _L0_ffn_in['w_down'], 'L0_ffn_sw_gate': _L0_ffn_in['sw_gate'], 'L0_ffn_sw_up': _L0_ffn_in['sw_up'], 'L0_ffn_sw_down': _L0_ffn_in['sw_down'], 'L1_attn_Wl': _L1_attn_in['Wl'], 'L1_attn_bl': _L1_attn_in['bl'], 'L1_attn_Wr': _L1_attn_in['Wr'], 'L1_attn_br': _L1_attn_in['br'], 'L1_attn_conv_w': _L1_attn_in['conv_w'], 'L1_attn_conv_b': _L1_attn_in['conv_b'], 'L1_attn_Wa': _L1_attn_in['Wa'], 'L1_attn_ba': _L1_attn_in['ba'], 'L1_attn_Wi': _L1_attn_in['Wi'], 'L1_attn_bi': _L1_attn_in['bi'], 'L1_attn_lam': _L1_attn_in['lam'], 'L1_attn_Wo': _L1_attn_in['Wo'], 'L1_attn_bo': _L1_attn_in['bo'], 'L1_ffn_select_weight': _L1_ffn_in['select_weight'], 'L1_ffn_select_mean_diff': _L1_ffn_in['select_mean_diff'], 'L1_ffn_imp_center': _L1_ffn_in['imp_center'], 'L1_ffn_imp_slope': _L1_ffn_in['imp_slope'], 'L1_ffn_lora_update': _L1_ffn_in['lora_update'], 'L1_ffn_lora_degen': _L1_ffn_in['lora_degen'], 'L1_ffn_bias_w': _L1_ffn_in['bias_w'], 'L1_ffn_debias_w': _L1_ffn_in['debias_w']}
    _x0 = _d['L0_attn_hidden_states']
    _d['L0_attn_hidden_states'] = jax.random.normal(jax.random.fold_in(jax.random.key(seed), 1), (2, 512, 256), dtype=_x0.dtype)
    del _x0
    return _d

def reference(L0_attn_hidden_states, L0_attn_Wq, L0_attn_Wk, L0_attn_Wv, L0_attn_Wo, L0_attn_o_norm_w, L0_ffn_gate_w, L0_ffn_w_gate, L0_ffn_w_up, L0_ffn_w_down, L0_ffn_sw_gate, L0_ffn_sw_up, L0_ffn_sw_down, L1_attn_Wl, L1_attn_bl, L1_attn_Wr, L1_attn_br, L1_attn_conv_w, L1_attn_conv_b, L1_attn_Wa, L1_attn_ba, L1_attn_Wi, L1_attn_bi, L1_attn_lam, L1_attn_Wo, L1_attn_bo, L1_ffn_select_weight, L1_ffn_select_mean_diff, L1_ffn_imp_center, L1_ffn_imp_slope, L1_ffn_lora_update, L1_ffn_lora_degen, L1_ffn_bias_w, L1_ffn_debias_w):

    def _L0_attn_ref(hidden_states, Wq, Wk, Wv, Wo, o_norm_w):
        import jax, jax.numpy as jnp
        import numpy as np
        H = 16
        CHUNK = 32
        TOPK = 4
        THETA = 10000.0
        EPS = 1e-06
        NEG = -1e+30
        POS = 1e+30

        def _rope(x, cos, sin):
            d2 = x.shape[-1] // 2
            x1, x2 = (x[..., :d2], x[..., d2:])
            return jnp.concatenate([x1 * cos - x2 * sin, x2 * cos + x1 * sin], axis=-1)
        B, S, D = hidden_states.shape
        d = D // H
        nblk = S // CHUNK
        q = (hidden_states @ Wq.T).reshape(B, S, H, d)
        k = (hidden_states @ Wk.T).reshape(B, S, H, d)
        v = (hidden_states @ Wv.T).reshape(B, S, H, d)
        pos = jnp.arange(S)
        inv_freq = 1.0 / THETA ** (jnp.arange(0, d, 2).astype(jnp.float32) / d)
        freqs = pos[:, None].astype(jnp.float32) * inv_freq
        cos = jnp.cos(freqs)[None, :, None, :]
        sin = jnp.sin(freqs)[None, :, None, :]
        q = _rope(q, cos, sin)
        k = _rope(k, cos, sin)
        km = k.reshape(B, nblk, CHUNK, H, d).mean(axis=2)
        gate = jnp.einsum('bshd,bnhd->bhsn', q, km)
        blk_q = pos // CHUNK
        blk_ids = jnp.arange(nblk)
        future = blk_ids[None, :] > blk_q[:, None]
        selfb = blk_ids[None, :] == blk_q[:, None]
        gate = jnp.where(future, NEG, gate)
        gate = jnp.where(selfb, POS, gate)
        vals, idx = jax.lax.top_k(gate, TOPK)
        valid = (vals > NEG / 2).astype(jnp.float32)
        sel = (jax.nn.one_hot(idx, nblk, dtype=jnp.float32) * valid[..., None]).sum(axis=-2) > 0
        sel_tok = jnp.repeat(sel, CHUNK, axis=-1)
        causal = pos[None, :] <= pos[:, None]
        mask = sel_tok & causal
        scores = jnp.einsum('bihd,bjhd->bhij', q, k) * d ** (-0.5)
        scores = jnp.where(mask, scores, NEG)
        p = jax.nn.softmax(scores, axis=-1)
        o = jnp.einsum('bhij,bjhd->bihd', p, v)
        o = o * jax.lax.rsqrt(jnp.mean(o * o, axis=-1, keepdims=True) + EPS) * o_norm_w
        return o.reshape(B, S, D) @ Wo.T

    def _L0_ffn_ref(hidden_states, gate_w, w_gate, w_up, w_down, sw_gate, sw_up, sw_down):
        import jax, jax.numpy as jnp
        import numpy as np
        B, S, D = (4, 64, 256)
        E, K, H = (8, 2, 176)
        HS = 2 * 176
        ALPHA = 0.001
        W_SCALE = 0.02

        def _moe_forward(hidden_states, gate_w, w_gate, w_up, w_down, sw_gate, sw_up, sw_down):
            b, s, d = hidden_states.shape
            x = hidden_states.reshape(-1, d)
            T = x.shape[0]
            logits = x @ gate_w
            scores = jax.nn.softmax(logits, axis=-1)
            topk_w, topk_idx = jax.lax.top_k(scores, K)
            mask = jax.nn.one_hot(topk_idx, E, dtype=scores.dtype).sum(axis=1)
            ce = mask.mean(axis=0)
            Pi = scores.mean(axis=0)
            aux_loss = (Pi * ce * E).sum() * ALPHA
            comb = jnp.zeros((T, E), dtype=x.dtype)
            comb = comb.at[jnp.arange(T)[:, None], topk_idx].add(topk_w)
            g = jax.nn.silu(jnp.einsum('td,edh->teh', x, w_gate)) * jnp.einsum('td,edh->teh', x, w_up)
            routed = jnp.einsum('teh,ehd,te->td', g, w_down, comb)
            shared = jax.nn.silu(x @ sw_gate) * (x @ sw_up) @ sw_down
            out = (routed + shared).reshape(b, s, d)
            return (out, aux_loss)
        out, _aux = _moe_forward(hidden_states, gate_w, w_gate, w_up, w_down, sw_gate, sw_up, sw_down)
        return out

    def _L1_attn_ref(x, Wl, bl, Wr, br, conv_w, conv_b, Wa, ba, Wi, bi, lam, Wo, bo):
        import jax, jax.numpy as jnp
        import numpy as np
        IN_DIM, HID, OUT_DIM = (256, 320, 256)
        KERNEL = 4
        C_RGLRU = 8.0

        def _rg_lru(u, Wa, ba, Wi, bi, lam):
            r = jax.nn.sigmoid(jnp.einsum('bsh,hk->bsk', u, Wa) + ba)
            i = jax.nn.sigmoid(jnp.einsum('bsh,hk->bsk', u, Wi) + bi)
            log_a = -C_RGLRU * jax.nn.softplus(-lam) * r
            a = jnp.exp(log_a)
            beta = jnp.sqrt(jnp.maximum(1.0 - jnp.exp(2.0 * log_a), 1e-12))
            drive = beta * (i * u)

            def step(h, ab):
                a_t, d_t = ab
                h = a_t * h + d_t
                return (h, h)
            h0 = jnp.zeros((u.shape[0], u.shape[2]), u.dtype)
            _, hs = jax.lax.scan(step, h0, (a.transpose(1, 0, 2), drive.transpose(1, 0, 2)))
            return hs.transpose(1, 0, 2)
        left = jax.nn.gelu(jnp.einsum('bsd,dh->bsh', x, Wl) + bl)
        r_in = jnp.einsum('bsd,dh->bsh', x, Wr) + br
        conv = jax.lax.conv_general_dilated(r_in, conv_w, window_strides=(1,), padding=[(KERNEL - 1, 0)], dimension_numbers=('NWC', 'WIO', 'NWC'), feature_group_count=HID) + conv_b
        right = _rg_lru(conv, Wa, ba, Wi, bi, lam)
        return jnp.einsum('bsh,ho->bso', left * right, Wo) + bo

    def _L1_ffn_ref(x, select_weight, select_mean_diff, imp_center, imp_slope, lora_update, lora_degen, bias_w, debias_w):
        import jax, jax.numpy as jnp
        import numpy as np
        B, T, D = (4, 128, 256)
        N, S, H = (8, 8, 8)
        ETA = 1.0
        x_diff = x[:, None, :, :] - select_mean_diff[None, :, None, :]
        x_diff = x_diff / jnp.linalg.norm(x_diff, axis=3, keepdims=True)
        cont = jnp.einsum('nds,bntd->bnts', select_weight, x_diff) ** 2
        score = cont.sum(axis=-1)
        gate = jax.nn.sigmoid(imp_slope[None, :, None] * (score - imp_center[None, :, None]))
        sel_scale = gate.max(axis=1)[..., None]
        sel_idx = gate.argmax(axis=1)
        debias = jnp.take(debias_w, sel_idx, axis=0)
        bias = jnp.take(bias_w, sel_idx, axis=0)
        upd = jnp.take(lora_update, sel_idx, axis=0)
        dgn = jnp.take(lora_degen, sel_idx, axis=0)
        x_debias = x - debias
        mod_x = jnp.einsum('btdh,btd->bth', upd, x_debias)
        degen_up = jnp.einsum('btdh,bth->btd', dgn, mod_x)
        mod_x_bias = ETA * (bias + degen_up)
        return (1.0 - sel_scale) * x + sel_scale * mod_x_bias
    x = L0_attn_hidden_states
    xn = _layernorm(x, axis=-1)
    s = _L0_attn_ref(xn, L0_attn_Wq, L0_attn_Wk, L0_attn_Wv, L0_attn_Wo, L0_attn_o_norm_w)
    g = _silu(_L0_ffn_ref(xn, L0_ffn_gate_w, L0_ffn_w_gate, L0_ffn_w_up, L0_ffn_w_down, L0_ffn_sw_gate, L0_ffn_sw_up, L0_ffn_sw_down))
    x = x + s * g
    xn = _layernorm(x, axis=-1)
    s = _L1_attn_ref(xn, L1_attn_Wl, L1_attn_bl, L1_attn_Wr, L1_attn_br, L1_attn_conv_w, L1_attn_conv_b, L1_attn_Wa, L1_attn_ba, L1_attn_Wi, L1_attn_bi, L1_attn_lam, L1_attn_Wo, L1_attn_bo)
    g = _silu(_L1_ffn_ref(xn, L1_ffn_select_weight, L1_ffn_select_mean_diff, L1_ffn_imp_center, L1_ffn_imp_slope, L1_ffn_lora_update, L1_ffn_lora_degen, L1_ffn_bias_w, L1_ffn_debias_w))
    x = x + s * g
    return x

_drawn_inputs = setup_inputs


def setup_inputs(seed=0):
    import zlib

    import numpy as np

    out = dict(_drawn_inputs(seed))
    spreads = {'L0_attn_o_norm_w': (1.0, 0.6),
     'L1_attn_bl': (0.0, 0.8),
     'L1_attn_br': (0.0, 0.8),
     'L1_attn_conv_b': (0.0, 0.8),
     'L1_attn_ba': (0.0, 2.0),
     'L1_attn_bi': (0.0, 2.0),
     'L1_attn_bo': (0.0, 2.0)}
    factors = {'L0_attn_Wq': 8.0,
     'L0_attn_Wk': 8.0,
     'L0_attn_Wv': 8.0,
     'L0_attn_Wo': 8.0,
     'L0_ffn_gate_w': 8.0,
     'L0_ffn_w_gate': 8.0,
     'L0_ffn_w_up': 8.0,
     'L0_ffn_w_down': 8.0,
     'L0_ffn_sw_gate': 8.0,
     'L0_ffn_sw_up': 8.0,
     'L0_ffn_sw_down': 8.0,
     'L1_attn_Wl': 8.0,
     'L1_attn_Wr': 8.0,
     'L1_attn_conv_w': 8.0,
     'L1_attn_Wa': 8.0,
     'L1_attn_Wi': 8.0,
     'L1_attn_lam': 8.0,
     'L1_attn_Wo': 8.0,
     'L1_ffn_select_weight': 8.0,
     'L1_ffn_imp_center': 8.0,
     'L1_ffn_imp_slope': 8.0,
     'L1_ffn_lora_update': 8.0,
     'L1_ffn_lora_degen': 8.0,
     'L1_ffn_bias_w': 8.0,
     'L1_ffn_debias_w': 8.0}
    for name, (base, spread) in spreads.items():
        noise = np.random.default_rng([zlib.crc32(name.encode()), seed]).standard_normal(out[name].shape)
        drawn = base * np.exp(spread * noise) if base else spread * noise
        out[name] = jnp.asarray(drawn.astype(out[name].dtype))
    for name, factor in factors.items():
        out[name] = (out[name] * factor).astype(out[name].dtype)
    return out
```

```python
from contextlib import ExitStack

import numpy as np

import concourse.bass as bass
from concourse import mybir

ALU = mybir.AluOpType
ACT = mybir.ActivationFunctionType
AX = mybir.AxisListType
F32 = mybir.dt.float32
F32R = mybir.dt.float32r
BF16 = mybir.dt.bfloat16

P = 128
B, S, D = 2, 512, 256
T = B * S // P
TB = S // P
KD = D // P
LN_EPS = 1e-5
NEG = -1e30

H, DH, BLK, TOPK = 16, 16, 32, 4
NBLK = S // BLK
GATE_ROW = NBLK + TOPK
HG = 4
NG = H // HG
RMS_EPS = 1e-6
E, EK, EH, SH = 8, 2, 176, 352
ECH = E * EH // P
SCH = -(-SH // P)
CH = ECH + SCH
EROW = E + 8 - EK
HALVES = 2
STEPS = HALVES * CH
SENT, SENT_TEST = 3e38, 1e38
STACK = [(0, 0), (0, 1), (1, 0), (1, 1), (0, 2), (2, 0)]
R_BIAS = len(STACK) * DH
R_MAX = R_BIAS + NBLK
R_ALL = R_MAX + 3
A_STEPS, B_STEPS = (4, 8), 12

HID = 320
HT = -(-HID // P)
HP = HT * P
TAPS = 4
N_SEL, S_SEL, H_SEL = 8, 8, 8
FW = N_SEL * S_SEL + N_SEL * H_SEL + N_SEL
OW = N_SEL * H_SEL + N_SEL


def unit_loads(g):
    heads = list(range(HG * g, HG * g + HG))
    loads = [(0, heads), (1, heads[:2]), (1, heads[2:])]
    loads += [(i, [h]) for i in (2, 3) for h in heads]
    return loads


LOADS = len(unit_loads(0))


def spread(ap, axis, n):
    v = ap.unsqueeze(axis)
    shape = list(v.shape)
    shape[axis] = n
    return v.broadcast_to(shape)


class Mem:
    def __init__(self, nc, ctx):
        self.nc, self.ctx = nc, ctx

    def sb(self, name, shape, dt=F32):
        return self.ctx.enter_context(self.nc.sbuf_tensor(name, shape, dt))

    def ps(self, name, dt=F32):
        return self.ctx.enter_context(self.nc.psum_tensor(name, [P, 2048 // (4 if dt == F32 else 2)], dt))

    def sem(self, name):
        return self.ctx.enter_context(self.nc.semaphore(name))


def chain(eng, sem):
    done = [0]

    def link(ins):
        done[0] += 1
        ins.then_inc(sem, 1)
        eng.wait_ge(sem, done[0])
    return link


def split_matmul(pe, out, l_hi, l_lo, r_hi, r_lo, start, stop, skip=False):
    pe.matmul(out, l_hi, r_hi, start=start, stop=False, skip_group_check=skip)
    pe.matmul(out, l_hi, r_lo, start=False, stop=False, skip_group_check=skip)
    return pe.matmul(out, l_lo, r_hi, start=False, stop=stop, skip_group_check=skip)


def layer0(nc, a, x1, cst):
    ctx = ExitStack()
    with ctx:
        m = Mem(nc, ctx)
        ident, ident_b = cst["ident"], cst["ident_b"]
        tri = m.sb("tri", [P, 2, P], BF16)
        ksel = m.sb("ksel", [64, ECH, P], BF16)
        onorm = m.sb("onorm", [P, DH])
        mhalf = m.sb("mhalf", [P, P])
        xn = x1
        xh = m.sb("xh", [P, KD, T * P], F32R)
        xl = m.sb("xl", [P, KD, T * P], F32R)
        bias = m.sb("bias", [P, T, H, NBLK], BF16)
        biasT = m.sb("biasT", [P, 4, 512], BF16)
        QS = m.sb("QS", [P, H, T * P], BF16)
        KS = m.sb("KS", [P, H, T * P], BF16)
        V = m.sb("V", [P, T, H, 32])
        mx = m.sb("mx", [P, T, H])
        mr = m.sb("mr", [P, 2, TB, H])
        ms = m.sb("ms", [P, T, 3, H], BF16)
        lg = m.sb("lg", [P, T, E])
        rt = m.sb("rt", [P, 4, T, E])
        rm = m.sb("rm", [P, 3, T])
        sc = m.sb("sc", [P, T, EROW])
        cs = m.sb("cs", [P, T, 64], BF16)
        combT = m.sb("combT", [64, T * P], BF16)
        wr = m.sb("wr", [P, 2, 3, 256])
        wh = m.sb("wh", [P, 2, 3, 256], F32R)
        wl = m.sb("wl", [P, 2, 3, 256], F32R)

        early_ctx = ExitStack()
        early = Mem(nc, early_ctx)
        x = early.sb("x", [P, T, D])
        wp = early.sb("wp", [P, KD, 776])
        wp_h = early.sb("wp_h", [P, KD, 776], F32R)
        wp_l = early.sb("wp_l", [P, KD, 776], F32R)
        rot_a = early.sb("rot_a", [P, 512])
        rot_b = early.sb("rot_b", [P, 512])
        qkr = early.sb("qkr", [P, TB, 512])
        X = early.sb("X", [P, 4, 512])
        R1 = early.sb("R1", [P, 2, 512])
        parts = early.sb("parts", [P, 2, 3, 512], BF16)
        gates = early.sb("gates", [P, 2, H, GATE_ROW])
        top = early.sb("top", [P, H, 8])
        picked = early.sb("picked", [P, H, GATE_ROW])
        km = early.sb("km", [P, 4, NBLK])
        kmb = early.sb("kmb", [P, 4, 8, NBLK])
        cos = early.sb("cos", [P, TB, DH])
        sin = early.sb("sin", [P, TB, DH])
        gate_add = early.sb("gate_add", [P, TB, NBLK])
        future = early.sb("future", [P, NBLK])
        headmask = early.sb("headmask", [P, 8, NBLK])
        st = early.sb("st", [P, T, 6])
        mv = early.sb("mv", [P, T, 2])
        ve = early.sb("ve", [P, T])
        rstd = early.sb("rstd", [P, T])
        rpick = early.sb("rpick", [P, T, EROW])
        rtop = early.sb("rtop", [P, T, 8])
        early_ctx.close()
        PT = m.sb("PT", [P, 8, 512])
        oT = m.sb("oT", [P, 512])
        th = m.sb("th", [P, 512])
        s2 = m.sb("s2", [P, 512])
        uv = m.sb("uv", [P, 512])
        gb = m.sb("gb", [P, 512])
        gh = m.sb("gh", [P, 2, 512], F32R)
        gl = m.sb("gl", [P, 2, 512], F32R)
        y = m.sb("y", [P, T, D])
        ob = m.sb("ob", [P, T, H, DH + 1])
        small = m.sb("small", [P, 3, TB * H])
        msT = m.sb("msT", [48, 2, 512], BF16)
        wo = m.sb("wo", [P, KD, D])
        wo_h = m.sb("wo_h", [P, KD, D], F32R)
        wo_l = m.sb("wo_l", [P, KD, D], F32R)

        bank = [m.ps(f"bank{i}") for i in range(8)]
        bank_b = [bank[i][:, :].bitcast(BF16) for i in range(8)]

        parts_dram = nc.dram_tensor("parts_dram", (B, 2, 3, D, S), BF16, kind="Internal").ap()
        bias_dram = nc.dram_tensor("bias_dram", (B, D, S), BF16, kind="Internal").ap()
        max_dram = nc.dram_tensor("max_dram", (B, 3 * H, S), BF16, kind="Internal").ap()

        x_in = [m.sem(f"x_in{b}") for b in range(B)]
        sem_wp, sem_wo, sem_const, x_again = (m.sem(n) for n in ("wp_in", "wo_in", "const_in", "x_again"))
        init_done = m.sem("init_done")
        half_done = m.sem("half_done")
        var_ready, rstd_ready, xn_ready = m.sem("var_ready"), m.sem("rstd_ready"), m.sem("xn_ready")
        xT_ready, xh_ready, xl_ready = m.sem("xT_ready"), m.sem("xh_ready"), m.sem("xl_ready")
        wph_ready, wpl_ready, woh_ready, wol_ready = (m.sem(n) for n in ("wph", "wpl", "woh", "wol"))
        qk_ready, vg_ready, qk_read, vg_read = (m.sem(n) for n in ("qk_ready", "vg_ready", "qk_read", "vg_read"))
        rope_ready = m.sem("rope_ready")
        qkT_ready, X_ready, H_ready, R1_ready, M_ready, L_ready = (
            m.sem(n) for n in ("qkT_ready", "X_ready", "H_ready", "R1_ready", "M_ready", "L_ready"))
        parts_out = [m.sem(f"parts_out{i}") for i in range(2)]
        q_stacked = [m.sem(f"q_stacked{b}") for b in range(B)]
        k_stacked = [m.sem(f"k_stacked{b}") for b in range(B)]
        kconst_ready = m.sem("kconst_ready")
        kmb_ready, gate_ready, gate_read, bias_ready = (
            m.sem(n) for n in ("kmb_ready", "gate_ready", "gate_read", "bias_ready"))
        biasT_ready, biasT_read, bias_out = m.sem("biasT_ready"), m.sem("biasT_read"), m.sem("bias_out")
        e_in, e_out, comb_ready, combT_ready, combT_read = (
            m.sem(n) for n in ("e_in", "e_out", "comb_ready", "combT_ready", "combT_read"))
        w_in = [m.sem("w_in0"), m.sem("w_in1")]
        wh_ready, wl_ready = m.sem("wh_ready"), m.sem("wl_ready")
        G_ready, U_ready, th_ready, G_read, g_ready, gh_ready, gl_ready, down_done = (
            m.sem(n) for n in ("G_ready", "U_ready", "th_ready", "G_read", "g_ready", "gh_ready", "gl_ready",
                               "down_done"))
        y_read = m.sem("y_read")
        A_ready, A_read, max_ready, maxT_ready, maxT_read, max_out = (
            m.sem(n) for n in ("A_ready", "A_read", "max_ready", "maxT_ready", "maxT_read", "max_out"))
        B_ready, P_ready, PV_done, oT_ready, oTT_ready, ob_ready = (
            m.sem(n) for n in ("B_ready", "P_ready", "PV_done", "oT_ready", "oTT_ready", "ob_ready"))
        rms_in, rms_out, on_ready, onT_ready, onh_ready, onl_ready = (
            m.sem(n) for n in ("rms_in", "rms_out", "on_ready", "onT_ready", "onh_ready", "onl_ready"))
        yth_ready, s_ready, x1_ready = m.sem("yth_ready"), m.sem("s_ready"), m.sem("x1_ready")
        dve_step, act_step, pool_step = m.sem("dve_step"), m.sem("act_step"), m.sem("pool_step")

        def tokens(t, n=1):
            return slice(t * P, (t + n) * P)

        def unit_of(u):
            return u // (NG * TB), (u // TB) % NG, u % TB

        xr = KS[:, 8:12, :].bitcast(F32).rearrange("p a (b d) -> p (a b) d", d=D)
        yth = QS[:, 0:4, :].bitcast(F32).rearrange("p a (b d) -> p (a b) d", d=D)
        sq = KS[:, 0:2, :].bitcast(F32).rearrange("p a (c d) -> p (a c) d", d=DH)

        block = ctx.enter_context(nc.Block())

        @block.sync
        def _(sp):
            for b in range(B):
                sp.dma_start(x[:, b * TB:(b + 1) * TB, :],
                             a["x"].rearrange("(t p) d -> p t d", p=P)[:, b * TB:(b + 1) * TB, :]).then_inc(x_in[b], 16)
            sp.dma_start(cst["ident"][:, :], a["c_ident"]).then_inc(cst["ident_in"], 16)
            sp.dma_start(wp[:, :, :], a["w_proj"].rearrange("(k p) n -> p k n", p=P)).then_inc(sem_wp, 16)
            for dst, src in ((cos[:, :, :], a["c_cos"]), (sin[:, :, :], a["c_sin"]),
                             (gate_add[:, :, :], a["c_gate_add"]), (future[:, :], a["c_future"]),
                             (headmask[:, :, :], a["c_headmask"]), (tri[:, :, :], a["c_tri"]),
                             (ksel[:, :, :], a["c_ksel"]), (ident_b[:, :], a["c_ident_b"]),
                             (onorm[:, :], a["L0_attn_o_norm_w"].unsqueeze(0).broadcast_to([P, DH]))):
                sp.dma_start(dst, src).then_inc(sem_const, 16)
            sp.dma_start(KS[R_BIAS:R_ALL, :, :], spread(a["c_kconst"], 1, H)).then_inc(kconst_ready, 16)

            def load_chunk(s):
                c = s % CH
                if s >= 2:
                    sp.wait_ge(wh_ready, s - 1)
                    sp.wait_ge(wl_ready, s - 1)
                sp.dma_start(wr[:, s % 2, :, :], a["w_chunks"][c]).then_inc(w_in[s % 2], 16)

            load_chunk(0)
            load_chunk(1)
            for b in range(B):
                for k in range(4):
                    n = 4 * b + k
                    which, half = k // 2, k % 2
                    sp.wait_ge(H_ready, n + 1)
                    sp.wait_ge(M_ready, n + 1)
                    sp.wait_ge(L_ready, n + 1)
                    sp.dma_start(parts_dram[b, which, :, half * P:(half + 1) * P, :].rearrange("l p t -> p l t"),
                                 parts[:, n % 2, :, :]).then_inc(parts_out[n % 2], 16)
                    if half == 0:
                        continue
                    sp.wait_ge(parts_out[0], 16 * (n // 2 + 1))
                    sp.wait_ge(parts_out[1], 16 * (n // 2 + 1))
                    dst, done = ((QS, q_stacked), (KS, k_stacked))[which]
                    for r, pair in enumerate(STACK):
                        sp.dma_start(dst[r * DH:(r + 1) * DH, :, b * S:(b + 1) * S],
                                     parts_dram[b, which, pair[which]].rearrange("(h d) t -> d h t", d=DH)
                                     ).then_inc(done[b], 16)
                sp.wait_ge(biasT_read, 2 * (b + 1))
                sp.dma_start(bias_dram[b].rearrange("(f p) t -> p f t", p=P),
                             biasT[:, 2 * b:2 * b + 2, :]).then_inc(bias_out, 16)
                sp.wait_ge(bias_out, 16 * (b + 1))
                sp.dma_start(QS[R_BIAS:R_MAX, :, b * S:(b + 1) * S],
                             bias_dram[b].rearrange("(h n) t -> n h t", n=NBLK)).then_inc(q_stacked[b], 16)
            sp.wait_ge(combT_read, 1)
            sp.dma_start(wo[:, :, :], a["w_o"].rearrange("(k p) n -> p k n", p=P)).then_inc(sem_wo, 16)
            for s in range(2, STEPS):
                load_chunk(s)
                for b in range(B):
                    if s == A_STEPS[b] + NG + 2:
                        sp.wait_ge(maxT_read, b + 1)
                        sp.dma_start(max_dram[b], msT[:, b, :]).then_inc(max_out, 16)
                        sp.wait_ge(max_out, 16 * (b + 1))
                        sp.dma_start(QS[R_MAX:R_ALL, :, b * S:(b + 1) * S],
                                     max_dram[b].rearrange("(l h) t -> l h t", l=3)).then_inc(q_stacked[b], 16)
            sp.wait_ge(PV_done, B * NG * TB)
            sp.dma_start(xr[:, :, :], a["x"].rearrange("(t p) d -> p t d", p=P)).then_inc(x_again, 16)

        @block.gpsimd
        def _(pool):
            link = chain(pool, pool_step)
            pool.memset(mhalf[:, :], -0.5).then_inc(half_done, 1)
            link(pool.memset(V[:, :, :, :], 0.0))
            link(pool.memset(V[:, :, :, DH:DH + 1], 1.0))
            link(pool.memset(gates[:, :, :, NBLK:GATE_ROW], SENT))
            link(pool.memset(sc[:, :, E:EROW], SENT))
            pool.memset(cs[:, :, :], 0.0).then_inc(init_done, 1)
            pool.wait_ge(half_done, 1)
            for b in range(B):
                tb = slice(b * TB, (b + 1) * TB)
                pool.wait_ge(var_ready, b + 1)
                pool.tensor_tensor(rstd[:, tb], ve[:, tb], mhalf[:, 0:TB], ALU.pow).then_inc(rstd_ready, 1)
            pool.wait_ge(wph_ready, 1)
            pool.tensor_tensor(wp_l[:, :, :], wp[:, :, :], wp_h[:, :, :].bitcast(F32), ALU.subtract).then_inc(wpl_ready, 1)

            def split_chunk(s):
                pool.wait_ge(wh_ready, s + 1)
                if s >= 2:
                    pool.wait_ge(down_done, s - 1)
                pool.tensor_tensor(wl[:, s % 2, :, :], wr[:, s % 2, :, :], wh[:, s % 2, :, :].bitcast(F32),
                                   ALU.subtract).then_inc(wl_ready, 1)

            def third_parts(b):
                for k in range(4):
                    n = 4 * b + k
                    pool.wait_ge(M_ready, n + 1)
                    pool.wait_ge(R1_ready, n + 1)
                    if n >= 2:
                        pool.wait_ge(parts_out[n % 2], 16 * (n // 2))
                    pool.tensor_tensor(parts[:, n % 2, 2, :], R1[:, n % 2, :], parts[:, n % 2, 1, :],
                                       ALU.subtract).then_inc(L_ready, 1)

            for t in range(T):
                pool.wait_ge(qk_read, t + 1)
                if t >= TB:
                    pool.wait_ge(qkT_ready, 4)
                pool.tensor_tensor(qkr[:, t % TB, :], rot_a[:, :], rot_b[:, :],
                                   ALU.add).then_inc(rope_ready, 1)
                if t == TB - 1:
                    third_parts(0)
            third_parts(1)
            split_chunk(0)
            for s in range(STEPS):
                if s + 1 < STEPS:
                    split_chunk(s + 1)
                pool.wait_ge(gh_ready, s + 1)
                if s >= 2:
                    pool.wait_ge(down_done, s - 1)
                pool.tensor_tensor(gl[:, s % 2, :], gb[:, :], gh[:, s % 2, :].bitcast(F32),
                                   ALU.subtract).then_inc(gl_ready, 1)
            pool.wait_ge(woh_ready, 1)
            pool.tensor_tensor(wo_l[:, :, :], wo[:, :, :], wo_h[:, :, :].bitcast(F32), ALU.subtract).then_inc(wol_ready, 1)
            for b in range(B):
                pool.wait_ge(rms_in, b + 1)
                pool.tensor_tensor(small[:, 2, :], small[:, 1, :], mhalf[:, 0:TB * H], ALU.pow).then_inc(rms_out, 1)

        @block.scalar
        def _(act):
            act.wait_ge(sem_wp, 16)
            act.copy(wp_h[:, :, :], wp[:, :, :]).then_inc(wph_ready, 1)
            for n in range(2 * B):
                b, c = n // 2, n % 2
                act.wait_ge(xT_ready, n + 1)
                act.copy(xh[:, c, b * S:(b + 1) * S], bank[n][:, :]).then_inc(xh_ready, 1)

            def values(t):
                act.wait_ge(vg_ready, t + 1)
                act.wait_ge(init_done, 1)
                vg = bank[6 + t % 2]
                act.copy(V[:, t, :, 0:DH], vg[:, 0:D].rearrange("p (h d) -> p h d", d=DH))
                act.copy(lg[:, t, :], vg[:, D:D + E]).then_inc(vg_read, 1)

            def first_parts(b):
                for k in range(4):
                    n = 4 * b + k
                    act.wait_ge(X_ready, n + 1)
                    if n >= 2:
                        act.wait_ge(parts_out[n % 2], 16 * (n // 2))
                    act.copy(parts[:, n % 2, 0, :], X[:, n % 4, :]).then_inc(H_ready, 1)
                    act.wait_ge(R1_ready, n + 1)
                    act.copy(parts[:, n % 2, 1, :], R1[:, n % 2, :]).then_inc(M_ready, 1)

            def split_chunk(s):
                act.wait_ge(w_in[s % 2], 16 * (s // 2 + 1))
                if s >= 2:
                    act.wait_ge(down_done, s - 1)
                act.copy(wh[:, s % 2, :, :], wr[:, s % 2, :, :]).then_inc(wh_ready, 1)

            def bias_rows(b):
                for f in range(2):
                    act.wait_ge(biasT_ready, 2 * b + f + 1)
                    act.copy(biasT[:, 2 * b + f, :], bank_b[6 + f][:, 0:512]).then_inc(biasT_read, 1)

            for t in range(TB):
                values(t)
            first_parts(0)
            for t in range(TB, T):
                values(t)
            bias_rows(0)
            act.wait_ge(e_in, 1)
            act.activation(rt[:, 1, :, :], rt[:, 0, :, :], ACT.Exp).then_inc(e_out, 1)
            first_parts(1)
            split_chunk(0)
            bias_rows(1)
            act.wait_ge(combT_ready, 1)
            act.copy(combT[:, :], bank_b[4][0:64, :]).then_inc(combT_read, 1)

            def exps(u):
                b, g, j = unit_of(u)
                n = S - j * P
                for c in range(HG):
                    k = HG * u + c
                    act.wait_ge(B_ready, k + 1)
                    if k >= 8:
                        act.wait_ge(PV_done, u - 1)
                    act.activation(PT[:, k % 8, 0:n], bank[k % 2][:, 0:n], ACT.Exp,
                                   scale=float(DH) ** -0.5).then_inc(P_ready, 1)

            for s in range(STEPS):
                act.wait_ge(G_ready, s + 1)
                if s >= 1:
                    act.wait_ge(G_read, s)
                act.activation(th[:, :], bank[3][:, :], ACT.Tanh, scale=0.5).then_inc(th_ready, 1)
                if s >= B_STEPS:
                    exps(2 * (s - B_STEPS))
                if s + 1 < STEPS:
                    split_chunk(s + 1)
                act.wait_ge(g_ready, s + 1)
                if s >= 2:
                    act.wait_ge(down_done, s - 1)
                act.copy(gh[:, s % 2, :], gb[:, :]).then_inc(gh_ready, 1)
                for b in range(B):
                    if s == A_STEPS[b] + NG:
                        act.wait_ge(maxT_ready, b + 1)
                        act.copy(msT[:, b, :], bank_b[2][0:48, 0:512]).then_inc(maxT_read, 1)
                if s >= B_STEPS:
                    exps(2 * (s - B_STEPS) + 1)
            act.wait_ge(sem_wo, 16)
            act.copy(wo_h[:, :, :], wo[:, :, :]).then_inc(woh_ready, 1)
            act.wait_ge(PV_done, B * NG * TB)
            act.wait_ge(y_read, 4)
            act.activation(yth, y[:, :, :], ACT.Tanh, scale=0.5).then_inc(yth_ready, 1)
            for n in range(2 * B):
                act.wait_ge(onT_ready, n + 1)
                act.copy(xh[:, n % 2, (n // 2) * S:(n // 2 + 1) * S], bank[n][:, :]).then_inc(onh_ready, 1)

        @block.vector
        def _(dve):
            link = chain(dve, dve_step)
            for b in range(B):
                dve.wait_ge(x_in[b], 16)
                for t in range(b * TB, (b + 1) * TB):
                    ins = dve.bn_stats(st[:, t, :], x[:, t, :])
                link(ins)
                for t in range(b * TB, (b + 1) * TB):
                    ins = dve.bn_aggr(mv[:, t, :], st[:, t, :])
                link(ins)
                tb = slice(b * TB, (b + 1) * TB)
                dve.tensor_scalar(ve[:, tb], mv[:, tb, 1], LN_EPS, None, ALU.add).then_inc(var_ready, 1)
            for b in range(B):
                dve.wait_ge(rstd_ready, b + 1)
                for t in range(b * TB, (b + 1) * TB):
                    dve.tensor_scalar(xn[:, t, :], x[:, t, :], mv[:, t, 0:1], rstd[:, t:t + 1],
                                      ALU.subtract, ALU.mult).then_inc(xn_ready, 1)
            for n in range(2 * B):
                b, c = n // 2, n % 2
                dve.wait_ge(xh_ready, n + 1)
                dve.tensor_tensor(xl[:, c, b * S:(b + 1) * S], bank[n][:, :],
                                  xh[:, c, b * S:(b + 1) * S].bitcast(F32), ALU.subtract).then_inc(xl_ready, 1)
            dve.wait_ge(sem_const, 16 * 9)

            def rotate(t):
                i = t % TB
                dve.wait_ge(qk_ready, t + 1)
                if t:
                    dve.wait_ge(rope_ready, t)
                qk = bank[4 + t % 2][:, :].rearrange("p (h s e) -> p h s e", s=2, e=DH // 2)
                rb = rot_b[:, :].rearrange("p (h s e) -> p h s e", s=2, e=DH // 2)
                dve.tensor_tensor(rot_a[:, :].rearrange("p (h d) -> p h d", d=DH),
                                  bank[4 + t % 2][:, :].rearrange("p (h d) -> p h d", d=DH),
                                  spread(cos[:, i, :], 1, 2 * H), ALU.mult)
                dve.tensor_tensor(rb[:, :, 0, :], qk[:, :, 1, :], spread(sin[:, i, 0:DH // 2], 1, 2 * H), ALU.mult)
                dve.tensor_tensor(rb[:, :, 1, :], qk[:, :, 0, :], spread(sin[:, i, DH // 2:DH], 1, 2 * H),
                                  ALU.mult).then_inc(qk_read, 1)

            def key_means_and_rests(b):
                for k in range(4):
                    n = 4 * b + k
                    dve.wait_ge(qkT_ready, n + 1)
                    if n >= 4:
                        dve.wait_ge(gate_ready, TB)
                        dve.wait_ge(H_ready, n - 3)
                    dve.tensor_copy(X[:, k, :], bank[k][:, :]).then_inc(X_ready, 1)
                    dve.wait_ge(H_ready, n + 1)
                    if n >= 2:
                        dve.wait_ge(L_ready, n - 1)
                    dve.tensor_tensor(R1[:, n % 2, :], X[:, k, :], parts[:, n % 2, 0, :],
                                      ALU.subtract).then_inc(R1_ready, 1)
                    if k >= 2:
                        w = 2 * b + k - 2
                        link(dve.tensor_reduce(km[:, w, :], X[:, k, :].rearrange("p (n e) -> p n e", e=BLK),
                                               AX.X, ALU.add))
                        dve.scalar_tensor_tensor(out=kmb[:, w, :, :], in0=spread(km[:, w, :], 1, 8),
                                                 scalar=1.0 / BLK, in1=headmask[:, :, :], op0=ALU.mult,
                                                 op1=ALU.mult).then_inc(kmb_ready, 1)

            def select(t):
                i = t % TB
                dve.wait_ge(gate_ready, t + 1)
                dve.wait_ge(init_done, 1)
                if t:
                    dve.wait_ge(bias_ready, t)
                link(dve.tensor_tensor(gates[:, t % 2, :, 0:NBLK],
                                       bank[4 + t % 2][:, 0:H * NBLK].rearrange("p (h n) -> p h n", n=NBLK),
                                       spread(gate_add[:, i, :], 1, H), ALU.add))
                if i == 0:
                    dve.tensor_copy(bias[:, t, :, :], spread(future[:, :], 1, H)).then_inc(bias_ready, 1)
                    return
                for h in range(H):
                    ins = dve.max(top[:, h, :], gates[:, t % 2, h, :])
                link(ins)
                for h in range(H):
                    ins = dve.match_replace(picked[:, h, :], top[:, h, :], gates[:, t % 2, h, :], SENT)
                link(ins)
                dve.tensor_scalar(bias[:, t, :, :], picked[:, :, 0:NBLK], SENT_TEST, NEG, ALU.is_lt,
                                  ALU.mult).then_inc(bias_ready, 1)

            def router_in():
                dve.wait_ge(vg_read, T)
                link(dve.tensor_reduce(rm[:, 0, :], lg[:, :, :], AX.X, ALU.max))
                dve.tensor_tensor(rt[:, 0, :, :], lg[:, :, :], spread(rm[:, 0, :], 2, E), ALU.subtract).then_inc(e_in, 1)

            def router_out():
                dve.wait_ge(e_out, 1)
                dve.wait_ge(init_done, 1)
                link(dve.tensor_reduce(rm[:, 1, :], rt[:, 1, :, :], AX.X, ALU.add))
                link(dve.reciprocal(rm[:, 2, :], rm[:, 1, :]))
                link(dve.tensor_tensor(sc[:, :, 0:E], rt[:, 1, :, :], spread(rm[:, 2, :], 2, E), ALU.mult))
                for t in range(T):
                    ins = dve.max(rtop[:, t, :], sc[:, t, :])
                link(ins)
                for t in range(T):
                    ins = dve.match_replace(rpick[:, t, :], rtop[:, t, :], sc[:, t, :], SENT)
                link(ins)
                link(dve.scalar_tensor_tensor(out=rt[:, 2, :, :], in0=rpick[:, :, 0:E], scalar=SENT_TEST,
                                              in1=sc[:, :, 0:E], op0=ALU.is_ge, op1=ALU.mult))
                link(dve.tensor_copy(cs[:, :, 0:E], rt[:, 2, :, :]))
                link(dve.tensor_tensor(rt[:, 3, :, :], rt[:, 2, :, :], cs[:, :, 0:E], ALU.subtract))
                link(dve.tensor_copy(cs[:, :, E:2 * E], rt[:, 3, :, :]))
                dve.tensor_tensor(cs[:, :, 2 * E:3 * E], rt[:, 3, :, :], cs[:, :, E:2 * E],
                                  ALU.subtract).then_inc(comb_ready, 1)

            def head_maxima(b, g):
                for r, (i, heads) in enumerate(unit_loads(g)):
                    k = (b * NG + g) * LOADS + r
                    n = (i + 1) * P
                    dve.wait_ge(A_ready, k + 1)
                    dve.tensor_reduce(mx[:, b * TB + i, heads[0]:heads[-1] + 1],
                                      bank[k % 2][:, 0:len(heads) * n].rearrange("p (h n) -> p h n", n=n),
                                      AX.X, ALU.max).then_inc(A_read, 1)

            def maxima_parts(b):
                tb = slice(b * TB, (b + 1) * TB)
                dve.wait_ge(A_read, (b + 1) * NG * LOADS)
                link(dve.tensor_scalar(mr[:, 0, :, :], mx[:, tb, :], -1.0, None, ALU.mult))
                link(dve.tensor_copy(ms[:, tb, 0, :], mr[:, 0, :, :]))
                link(dve.tensor_tensor(mr[:, 1, :, :], mr[:, 0, :, :], ms[:, tb, 0, :], ALU.subtract))
                link(dve.tensor_copy(ms[:, tb, 1, :], mr[:, 1, :, :]))
                dve.tensor_tensor(ms[:, tb, 2, :], mr[:, 1, :, :], ms[:, tb, 1, :],
                                  ALU.subtract).then_inc(max_ready, 1)

            def head_out(q):
                b, g = q // NG, q % NG
                dve.wait_ge(PV_done, (q + 1) * TB)
                if q >= 1:
                    dve.wait_ge(oTT_ready, q)
                dve.tensor_copy(oT[:, :], bank[2][:, :]).then_inc(oT_ready, 1)
                dve.wait_ge(oTT_ready, q + 1)
                for i in range(TB):
                    dve.tensor_copy(ob[:, b * TB + i, g * HG:(g + 1) * HG, :],
                                    bank[5][:, i * P:(i + 1) * P].rearrange("p (h d) -> p h d", d=32)[:, :, 0:DH + 1]
                                    ).then_inc(ob_ready, 1)

            for t in range(TB):
                rotate(t)
            key_means_and_rests(0)
            for t in range(TB, T):
                rotate(t)
            for t in range(TB):
                select(t)
            router_in()
            key_means_and_rests(1)
            router_out()
            for t in range(TB, T):
                select(t)

            for s in range(STEPS):
                n, c = s // CH, s % CH
                dve.wait_ge(th_ready, s + 1)
                if s >= 1:
                    dve.wait_ge(g_ready, s)
                dve.scalar_tensor_tensor(out=s2[:, :], in0=th[:, :], scalar=1.0, in1=bank[3][:, :],
                                         op0=ALU.add, op1=ALU.mult).then_inc(G_read, 1)
                dve.wait_ge(U_ready, s + 1)
                dve.wait_ge(G_read, s + 1)
                if s >= 1:
                    dve.wait_ge(gh_ready, s)
                    dve.wait_ge(gl_ready, s)
                if c < ECH:
                    link(dve.scalar_tensor_tensor(out=uv[:, :], in0=s2[:, :], scalar=0.5, in1=bank[4][:, :],
                                                  op0=ALU.mult, op1=ALU.mult))
                    dve.tensor_tensor(gb[:, :], uv[:, :], bank[5][:, :], ALU.mult).then_inc(g_ready, 1)
                else:
                    dve.scalar_tensor_tensor(out=gb[:, :], in0=s2[:, :], scalar=0.5, in1=bank[4][:, :],
                                             op0=ALU.mult, op1=ALU.mult).then_inc(g_ready, 1)
                for b in range(B):
                    if A_STEPS[b] <= s < A_STEPS[b] + NG:
                        head_maxima(b, s - A_STEPS[b])
                    if s == A_STEPS[b] + NG - 1:
                        maxima_parts(b)
                if c == CH - 1:
                    dve.wait_ge(down_done, s + 1)
                    for k in range(2):
                        dve.tensor_copy(y[:, n * TB + 2 * k:n * TB + 2 * k + 2, :],
                                        bank[6 + k][:, :].rearrange("p (t d) -> p t d", d=D)).then_inc(y_read, 1)
                if s > B_STEPS and (s - B_STEPS) % 2 == 0:
                    head_out((s - B_STEPS) // 2 - 1)
            head_out(B * NG - 1)
            for b in range(B):
                tb = slice(b * TB, (b + 1) * TB)
                o = ob[:, tb, :, 0:DH].rearrange("p t h d -> p (t h) d")
                l = ob[:, tb, :, DH].rearrange("p t h -> p (t h)")
                dve.wait_ge(ob_ready, NG * TB * B)
                if b == 1:
                    dve.wait_ge(rms_out, 1)
                link(dve.tensor_tensor(sq, o, o, ALU.mult))
                link(dve.tensor_reduce(small[:, 0, :], sq, AX.X, ALU.add))
                link(dve.tensor_tensor(small[:, 1, :], l, l, ALU.mult))
                link(dve.scalar_tensor_tensor(out=small[:, 0, :], in0=small[:, 1, :], scalar=DH * RMS_EPS,
                                              in1=small[:, 0, :], op0=ALU.mult, op1=ALU.add))
                dve.tensor_scalar(small[:, 1, :], small[:, 0, :], 1.0 / DH, None, ALU.mult).then_inc(rms_in, 1)
                dve.wait_ge(rms_out, b + 1)
                link(dve.tensor_tensor(sq, o, spread(small[:, 2, :], 2, DH), ALU.mult))
                dve.tensor_tensor(xn[:, tb, :].rearrange("p t (h d) -> p (t h) d", d=DH), sq,
                                  spread(onorm[:, :], 1, TB * H), ALU.mult).then_inc(on_ready, 1)
                if b == 0:
                    dve.wait_ge(on_ready, 1)
            for n in range(2 * B):
                dve.wait_ge(onh_ready, n + 1)
                part = (slice(None), n % 2, slice((n // 2) * S, (n // 2 + 1) * S))
                dve.tensor_tensor(xl[part], bank[n][:, :], xh[part].bitcast(F32), ALU.subtract).then_inc(onl_ready, 1)
            dve.wait_ge(yth_ready, 1)
            link(dve.scalar_tensor_tensor(out=y[:, :, :], in0=yth, scalar=1.0, in1=y[:, :, :], op0=ALU.add,
                                          op1=ALU.mult))
            for t in range(T):
                dve.wait_ge(s_ready, t + 1)
                link(dve.scalar_tensor_tensor(out=y[:, t, :], in0=y[:, t, :], scalar=0.5,
                                              in1=bank[4 + t % 2][:, 0:D], op0=ALU.mult, op1=ALU.mult))
                if t == 0:
                    dve.wait_ge(x_again, 16)
                    dve.wait_ge(onT_ready, 2 * B)
                dve.tensor_tensor(x1[:, t, :], xr[:, t, :], y[:, t, :], ALU.add).then_inc(x1_ready, 1)

        @block.tensor
        def _(pe):
            pe.wait_ge(cst["ident_in"], 16)
            for n in range(2 * B):
                b, c = n // 2, n % 2
                for i in range(TB):
                    pe.wait_ge(xn_ready, b * TB + i + 1)
                    ins = pe.transpose(bank[n][:, i * P:(i + 1) * P], xn[:, b * TB + i, c * P:(c + 1) * P], ident[:, :])
                ins.then_inc(xT_ready, 1)
            pe.wait_ge(wph_ready, 1)
            pe.wait_ge(wpl_ready, 1)

            def project(t):
                pe.wait_ge(xl_ready, 2 * (t // TB + 1))
                if t >= 2:
                    pe.wait_ge(qk_read, t - 1)
                    pe.wait_ge(vg_read, t - 1)
                for c in range(KD):
                    ins = split_matmul(pe, bank[4 + t % 2][:, :], xh[:, c, tokens(t)], xl[:, c, tokens(t)],
                                       wp_h[:, c, 0:512], wp_l[:, c, 0:512], c == 0, c == KD - 1)
                ins.then_inc(qk_ready, 1)
                for c in range(KD):
                    ins = split_matmul(pe, bank[6 + t % 2][:, 0:264], xh[:, c, tokens(t)], xl[:, c, tokens(t)],
                                       wp_h[:, c, 512:776], wp_l[:, c, 512:776], c == 0, c == KD - 1)
                ins.then_inc(vg_ready, 1)

            def transpose_qk(b):
                pe.wait_ge(rope_ready, (b + 1) * TB)
                pe.wait_ge(xl_ready, 2 * B)
                for k in range(4):
                    if b:
                        pe.wait_ge(X_ready, k + 1)
                    for i in range(TB):
                        ins = pe.transpose(bank[k][:, i * P:(i + 1) * P], qkr[:, i, k * P:(k + 1) * P], ident[:, :])
                    ins.then_inc(qkT_ready, 1)

            def block_gates(b):
                pe.wait_ge(kmb_ready, 2 * (b + 1))
                pe.wait_ge(qk_read, T)
                for t in range(b * TB, (b + 1) * TB):
                    if t >= 2:
                        pe.wait_ge(bias_ready, t - 1)
                    for f in range(2):
                        ins = pe.matmul(bank[4 + t % 2][:, f * P:(f + 1) * P], X[:, f, (t % TB) * P:(t % TB + 1) * P],
                                        kmb[:, 2 * b + f, :, :], start=True, stop=True)
                    ins.then_inc(gate_ready, 1)

            def transpose_bias(b):
                pe.wait_ge(bias_ready, (b + 1) * TB)
                pe.wait_ge(sem_const, 16 * 9)
                pe.wait_ge(vg_read, T)
                for f in range(2):
                    if b:
                        pe.wait_ge(biasT_read, f + 1)
                    for i in range(TB):
                        ins = pe.transpose(bank_b[6 + f][:, i * P:(i + 1) * P],
                                           bias[:, b * TB + i, f * 8:(f + 1) * 8, :], ident_b[:, :])
                    ins.then_inc(biasT_ready, 1)

            for t in range(TB):
                project(t)
            transpose_qk(0)
            for t in range(TB, T):
                project(t)
            block_gates(0)
            transpose_bias(0)
            transpose_qk(1)
            block_gates(1)
            transpose_bias(1)
            pe.wait_ge(comb_ready, 1)
            for t in range(T):
                ins = pe.transpose(bank_b[4][0:64, t * P:(t + 1) * P], cs[:, t, :], ident_b[:, :])
            ins.then_inc(combT_ready, 1)
            pe.wait_ge(combT_read, 1)
            pe.wait_ge(X_ready, 8)

            def score_maxima(b, g):
                if g == 0:
                    pe.wait_ge(q_stacked[b], 16 * (len(STACK) + 1))
                    pe.wait_ge(k_stacked[b], 16 * len(STACK))
                    pe.wait_ge(kconst_ready, 16)
                for r, (i, heads) in enumerate(unit_loads(g)):
                    k = (b * NG + g) * LOADS + r
                    n = (i + 1) * P
                    if k >= 2:
                        pe.wait_ge(A_read, k - 1)
                    for o, h in enumerate(heads):
                        out = bank[k % 2][:, o * n:(o + 1) * n]
                        pe.matmul(out, QS[0:R_MAX, h, b * S + i * P:b * S + (i + 1) * P],
                                  KS[0:R_MAX, h, b * S:b * S + n], start=True, stop=False)
                        ins = pe.matmul(out[:, n - P:n], ident_b[:, :], tri[:, 0, :], start=False, stop=True)
                    ins.then_inc(A_ready, 1)

            def score_exps(u):
                b, g, j = unit_of(u)
                n = S - j * P
                if g == 0 and j == 0:
                    pe.wait_ge(q_stacked[b], 16 * (len(STACK) + 2))
                for c in range(HG):
                    k = HG * u + c
                    h = HG * g + c
                    if k == 0:
                        pe.wait_ge(A_read, B * NG * LOADS)
                    if k >= 2:
                        pe.wait_ge(P_ready, k - 1)
                    out = bank[k % 2]
                    pe.matmul(out[:, 0:n], KS[0:R_ALL, h, b * S + j * P:b * S + (j + 1) * P],
                              QS[0:R_ALL, h, b * S + j * P:(b + 1) * S], start=True, stop=False)
                    pe.matmul(out[:, 0:P], ident_b[:, :], tri[:, 1, :], start=False, stop=True).then_inc(B_ready, 1)

            def values_sum(u):
                b, g, j = unit_of(u)
                q = u // TB
                pe.wait_ge(P_ready, HG * (u + 1))
                if j == 0 and q >= 1:
                    pe.wait_ge(oT_ready, q)
                if u == 0:
                    pe.wait_ge(maxT_read, B)
                for c in range(HG):
                    k = HG * u + c
                    ins = pe.matmul(bank[2][32 * c:32 * (c + 1), j * P:S], V[:, b * TB + j, HG * g + c, :],
                                    PT[:, k % 8, 0:S - j * P], start=(j == 0), stop=(j == TB - 1))
                ins.then_inc(PV_done, 1)

            def transpose_out(q):
                pe.wait_ge(oT_ready, q + 1)
                for i in range(TB):
                    ins = pe.transpose(bank[5][:, i * P:(i + 1) * P], oT[:, i * P:(i + 1) * P], ident[:, :])
                ins.then_inc(oTT_ready, 1)

            def up(s):
                n, c = s // CH, s % CH
                part = slice(n * S, (n + 1) * S)
                w = s % 2
                pe.wait_ge(wl_ready, s + 1)
                if s >= 1:
                    pe.wait_ge(G_read, s)
                for k in range(KD):
                    ins = split_matmul(pe, bank[3][:, :], wh[:, w, k, 0:P], wl[:, w, k, 0:P],
                                       xh[:, k, part], xl[:, k, part], k == 0, k == KD - 1)
                ins.then_inc(G_ready, 1)
                if s >= 1:
                    pe.wait_ge(g_ready, s)
                for k in range(KD):
                    ins = split_matmul(pe, bank[4][:, :], wh[:, w, k, P:2 * P], wl[:, w, k, P:2 * P],
                                       xh[:, k, part], xl[:, k, part], k == 0, k == KD - 1)
                if c < ECH:
                    ins = pe.matmul(bank[5][:, :], ksel[:, c, :], combT[:, part], start=True, stop=True)
                ins.then_inc(U_ready, 1)

            def down(s):
                n, c = s // CH, s % CH
                w = s % 2
                pe.wait_ge(gl_ready, s + 1)
                if s == 0:
                    pe.wait_ge(biasT_read, 4)
                if c == 0 and n:
                    pe.wait_ge(y_read, 2)
                for i in range(TB):
                    ins = split_matmul(pe, bank[6 + i // 2][:, (i % 2) * D:(i % 2 + 1) * D],
                                       gh[:, w, tokens(i)], gl[:, w, tokens(i)], wh[:, w, 2, :], wl[:, w, 2, :],
                                       c == 0 and i % 2 == 0, c == CH - 1, skip=True)
                ins.then_inc(down_done, 1)

            for s in range(STEPS):
                up(s)
                for b in range(B):
                    if A_STEPS[b] <= s < A_STEPS[b] + NG:
                        score_maxima(b, s - A_STEPS[b])
                    if s == A_STEPS[b] + NG:
                        pe.wait_ge(max_ready, b + 1)
                        if b:
                            pe.wait_ge(maxT_read, b)
                        for i in range(TB):
                            ins = pe.transpose(bank_b[2][0:48, i * P:(i + 1) * P],
                                               ms[:, b * TB + i, :, :].rearrange("p l h -> p (l h)"), ident_b[:, :])
                        ins.then_inc(maxT_ready, 1)
                if s >= 1 and s % CH:
                    down(s - 1)
                if s >= B_STEPS:
                    u = 2 * (s - B_STEPS)
                    score_exps(u)
                    if u >= 1:
                        values_sum(u - 1)
                    if u and u % TB == 0:
                        pe.wait_ge(g_ready, s + 1)
                        transpose_out(u // TB - 1)
                        pe.wait_ge(ob_ready, TB * (u // TB))
                    score_exps(u + 1)
                    values_sum(u)
                if s % CH == CH - 1:
                    down(s)
            values_sum(B * NG * TB - 1)
            transpose_out(B * NG - 1)
            for n in range(2 * B):
                b, c = n // 2, n % 2
                pe.wait_ge(on_ready, b + 1)
                for i in range(TB):
                    ins = pe.transpose(bank[n][:, i * P:(i + 1) * P], xn[:, b * TB + i, c * P:(c + 1) * P], ident[:, :])
                ins.then_inc(onT_ready, 1)
            pe.wait_ge(woh_ready, 1)
            pe.wait_ge(wol_ready, 1)
            for t in range(T):
                pe.wait_ge(onl_ready, 2 * (t // TB + 1))
                if t >= 2:
                    pe.wait_ge(x1_ready, t - 1)
                for c in range(KD):
                    ins = split_matmul(pe, bank[4 + t % 2][:, 0:D], xh[:, c, tokens(t)], xl[:, c, tokens(t)],
                                       wo_h[:, c, :], wo_l[:, c, :], c == 0, c == KD - 1)
                ins.then_inc(s_ready, 1)


def layer1(nc, a, x1, out, cst):
    ctx = ExitStack()
    with ctx:
        m = Mem(nc, ctx)
        ident = cst["ident"]
        w_lr = m.sb("w_lr", [P, KD, 2 * HP])
        w_lr_h = m.sb("w_lr_h", [P, KD, 2 * HP], F32R)
        w_lr_l = m.sb("w_lr_l", [P, KD, 2 * HP], F32R)
        w_ai = m.sb("w_ai", [P, HT, 2 * HP])
        w_ai_h = m.sb("w_ai_h", [P, HT, 2 * HP], F32R)
        w_ai_l = m.sb("w_ai_l", [P, HT, 2 * HP], F32R)
        w_o = m.sb("w_o", [P, HT, D])
        w_o_h = m.sb("w_o_h", [P, HT, D], F32R)
        w_o_l = m.sb("w_o_l", [P, HT, D], F32R)
        w_f = m.sb("w_f", [P, KD, FW])
        md = m.sb("md", [P, KD, 2 * N_SEL])
        w_g = m.sb("w_g", [OW, D])
        vec = m.sb("vec", [P, 10, HT])
        vec2 = m.sb("vec2", [P, 10, HT])
        sel_vec = m.sb("sel_vec", [P, 3, N_SEL])
        bo = m.sb("bo", [P, D])
        fmask = m.sb("fmask", [2 * N_SEL, FW])
        ones16 = m.sb("ones16", [2 * N_SEL, P])
        st = m.sb("st1", [P, T, 6])
        mv = m.sb("mv1", [P, T, 2])
        ve = m.sb("ve1", [P, T])
        mhalf = m.sb("mhalf1", [P, T])
        rstd = m.sb("rstd1", [P, T])
        xn = m.sb("xn1", [P, T, D])
        xsq = m.sb("xsq", [P, D])
        nsq = m.sb("nsq", [P, T])
        xh = m.sb("xh1", [P, KD, T * P], F32R)
        xl = m.sb("xl1", [P, KD, T * P], F32R)
        xT = m.sb("xT1", [P, KD, T * P])
        rin = m.sb("rin", [P, 2, TAPS - 1 + S])
        cv = m.sb("cv", [P, 2, S])
        u = m.sb("u", [P, HT, S])
        uh = m.sb("uh", [P, HT, S], F32R)
        ul = m.sb("ul", [P, HT, S], F32R)
        left = m.sb("left", [P, HT, S])
        ta = m.sb("ta", [P, HT, S])
        ti = m.sb("ti", [P, HT, S])
        dec = m.sb("dec", [P, HT, S])
        sqd = m.sb("sqd", [P, HT, S])
        drv = m.sb("drv", [P, HT, S])
        Y = m.sb("Y", [P, T, FW])
        fc = m.sb("fc", [2 * N_SEL, FW])
        fcm = m.sb("fcm", [2 * N_SEL, FW])
        fb = m.sb("fb", [P, FW])
        f1 = m.sb("f1", [P, T, N_SEL * S_SEL])
        z = m.sb("z", [P, 6, T, N_SEL])
        zm = m.sb("zm", [P, 3, T])
        ZO = m.sb("ZO", [P, T, OW])
        ZT = m.sb("ZT", [OW, T * P])
        ed = m.sb("ed", [P, T, D])
        o1 = m.sb("o1", [P, T, D])

        bank = [m.ps(f"lbank{i}") for i in range(8)]

        sems = {}

        def sem(name):
            if name not in sems:
                sems[name] = m.sem("l1_" + name)
            return sems[name]

        w_in = {n: m.sem("in_" + n) for n in ("lr", "ai", "o", "f", "vec", "selc")}
        var_ready, rstd_ready, xn_ready, nsq_ready = (sem(n) for n in ("var", "rstd", "xn", "nsq"))
        xT_ready, xh_ready, xl_ready = sem("xT"), sem("xh"), sem("xl")
        wh_ready, wl_ready = sem("wh"), sem("wl")
        R_ready, rin_ready, u_ready, uh_ready, ul_ready = (
            sem(n) for n in ("R", "rin", "u", "uh", "ul"))
        vec_ready, vec_exp, vec_dve, vec_ln, half_done = (sem(n) for n in ("vecr", "vexp", "vdve", "vln", "half"))
        A_ready, I_ready, ta_ready, ti_ready, dec_ready, sqd_ready, om_ready, beta_ready = (
            sem(n) for n in ("A", "I", "ta", "ti", "dec", "sqd", "om", "beta"))
        L_ready, left_ready, prod_ready, ph_ready, pl_ready, O_ready = (
            sem(n) for n in ("L", "left", "prod", "ph", "pl", "O"))
        F_ready, F_read, fc_ready, fcm_ready, fb_ready, fb_read = (
            sem(n) for n in ("F", "Fread", "fc", "fcm", "fb", "fbread"))
        z_ready, ez_ready, ZO_ready, ZT_ready, ZT_read, D_ready, ed_ready, eth_ready, out_ready = (
            sem(n) for n in ("z", "ez", "ZO", "ZT", "ZTread", "Dg", "ed", "eth", "out"))
        o_read = sem("o_read")
        dve_step, act_step, pool_step, stored = sem("dve_step"), sem("act_step"), sem("pool_step"), sem("stored")

        def tokens(t):
            return slice(t * P, (t + 1) * P)

        block = ctx.enter_context(nc.Block())

        @block.sync
        def _(sp):
            def load(dst, src, s):
                sp.dma_start(dst, src).then_inc(w_in[s], 16)
            load(w_lr[:, :, :], a["w_lr"].rearrange("(k p) n -> p k n", p=P), "lr")
            load(w_f[:, :, :], a["w_f"].rearrange("(k p) n -> p k n", p=P), "f")
            load(md[:, :, :], a["w_md"].rearrange("(k p) n -> p k n", p=P), "f")
            load(fmask[:, :], a["c_fmask"], "f")
            load(ones16[:, :], a["c_ones16"], "f")
            load(vec[:, :, :], a["vecs"], "vec")
            load(w_ai[:, :, :], a["w_ai"].rearrange("(k p) n -> p k n", p=P), "ai")
            load(w_o[:, :, :], a["w_o1"].rearrange("(k p) n -> p k n", p=P), "o")
            load(w_g[:, :], a["w_g"], "selc")
            load(sel_vec[:, 0, :], a["L1_ffn_imp_center"].unsqueeze(0).broadcast_to([P, N_SEL]), "selc")
            load(sel_vec[:, 1, :], a["L1_ffn_imp_slope"].unsqueeze(0).broadcast_to([P, N_SEL]), "selc")
            load(sel_vec[:, 2, :], a["c_rank"], "selc")
            load(bo[:, :], a["L1_attn_bo"].unsqueeze(0).broadcast_to([P, D]), "selc")
            dst = out.rearrange("(t p) d -> p t d", p=P)
            for t in range(T):
                sp.wait_ge(out_ready, t + 1)
                sp.dma_start(dst[:, t, :], ed[:, t, :]).then_inc(stored, 16)
            sp.wait_ge(stored, 16 * T)

        @block.gpsimd
        def _(pool):
            pool.memset(mhalf[:, :], -0.5).then_inc(half_done, 1)
            pool.memset(rin[:, :, 0:TAPS - 1], 0.0).then_inc(half_done, 1)
            pool.wait_ge(half_done, 1)
            for b in range(B):
                tb = slice(b * TB, (b + 1) * TB)
                pool.wait_ge(var_ready, b + 1)
                pool.tensor_tensor(rstd[:, tb], ve[:, tb], mhalf[:, tb], ALU.pow).then_inc(rstd_ready, 1)
            for k, (lo, raw, hi) in enumerate(((w_lr_l, w_lr, w_lr_h), (w_ai_l, w_ai, w_ai_h), (w_o_l, w_o, w_o_h))):
                pool.wait_ge(wh_ready, k + 1)
                pool.tensor_tensor(lo[:, :, :], raw[:, :, :], hi[:, :, :].bitcast(F32), ALU.subtract).then_inc(wl_ready, 1)
            for b in range(B):
                pool.wait_ge(uh_ready, b + 1)
                if b:
                    pool.wait_ge(O_ready, TB)
                pool.tensor_tensor(ul[:, :, :], u[:, :, :], uh[:, :, :].bitcast(F32), ALU.subtract).then_inc(ul_ready, 1)
                pool.wait_ge(ph_ready, b + 1)
                pool.wait_ge(I_ready, (b + 1) * HT)
                pool.tensor_tensor(ul[:, :, :], drv[:, :, :], uh[:, :, :].bitcast(F32), ALU.subtract).then_inc(pl_ready, 1)

        @block.scalar
        def _(act):
            link = chain(act, act_step)
            act.wait_ge(w_in["lr"], 16)
            act.copy(w_lr_h[:, :, :], w_lr[:, :, :]).then_inc(wh_ready, 1)
            act.wait_ge(vec_dve, 1)
            act.activation(vec2[:, 1, :], vec2[:, 0, :], ACT.Exp, scale=-1.0).then_inc(vec_exp, 1)
            act.wait_ge(vec_dve, 2)
            act.activation(vec2[:, 3, :], vec2[:, 2, :], ACT.Ln).then_inc(vec_ln, 1)
            for t in range(T):
                act.wait_ge(xn_ready, t + 1)
                if t:
                    act.wait_ge(nsq_ready, t)
                act.activation(xsq[:, :], xn[:, t, :], ACT.Square, accum_out=nsq[:, t:t + 1]).then_inc(nsq_ready, 1)
            for n in range(2 * B):
                b, c = n // 2, n % 2
                act.wait_ge(xT_ready, n + 1)
                act.copy(xh[:, c, b * S:(b + 1) * S], bank[n][:, :]).then_inc(xh_ready, 1)
            act.wait_ge(w_in["ai"], 16)
            act.copy(w_ai_h[:, :, :], w_ai[:, :, :]).then_inc(wh_ready, 1)
            act.wait_ge(w_in["o"], 16)
            act.copy(w_o_h[:, :, :], w_o[:, :, :]).then_inc(wh_ready, 1)
            act.wait_ge(half_done, 2)
            for b in range(B):
                for p in range(HT):
                    n = b * HT + p
                    act.wait_ge(R_ready, n + 1)
                    if n >= 2:
                        act.wait_ge(u_ready, n - 1)
                    act.activation(rin[:, n % 2, TAPS - 1:], bank[4 + n % 2][:, :], ACT.Identity,
                                   bias=vec[:, 1, p:p + 1]).then_inc(rin_ready, 1)
                act.wait_ge(u_ready, (b + 1) * HT)
                if b:
                    act.wait_ge(O_ready, TB)
                act.copy(uh[:, :, :], u[:, :, :]).then_inc(uh_ready, 1)
                act.wait_ge(vec_ready, 1)
                if b:
                    act.wait_ge(prod_ready, 1)
                for p in range(HT):
                    act.wait_ge(A_ready, b * HT + p + 1)
                    act.activation(ta[:, p, :], bank[0][:, :], ACT.Tanh, scale=0.5,
                                   bias=vec2[:, 4, p:p + 1]).then_inc(ta_ready, 1)
                    act.wait_ge(I_ready, b * HT + p + 1)
                    act.activation(ti[:, p, :], bank[1][:, :], ACT.Tanh, scale=0.5,
                                   bias=vec2[:, 5, p:p + 1]).then_inc(ti_ready, 1)
                    act.wait_ge(ta_ready, b * HT + p + 1)
                    act.activation(dec[:, p, :], ta[:, p, :], ACT.Exp, scale=vec2[:, 6, p:p + 1],
                                   bias=vec2[:, 6, p:p + 1]).then_inc(dec_ready, 1)
                    act.activation(sqd[:, p, :], ta[:, p, :], ACT.Exp, scale=vec2[:, 7, p:p + 1],
                                   bias=vec2[:, 7, p:p + 1]).then_inc(sqd_ready, 1)
                act.wait_ge(om_ready, b + 1)
                act.activation(sqd[:, :, :], sqd[:, :, :], ACT.Sqrt, scale=-1.0).then_inc(beta_ready, 1)
                for p in range(HT):
                    act.wait_ge(L_ready, b * HT + p + 1)
                    act.activation(left[:, p, :], bank[2 + (b * HT + p) % 2][:, :], ACT.Gelu_apprx_tanh,
                                   bias=vec[:, 0, p:p + 1]).then_inc(left_ready, 1)
                act.wait_ge(prod_ready, b + 1)
                act.wait_ge(I_ready, (b + 1) * HT)
                act.copy(uh[:, :, :], drv[:, :, :]).then_inc(ph_ready, 1)
            act.wait_ge(z_ready, 1)
            act.activation(z[:, 2, :, :], z[:, 1, :, :], ACT.Exp, scale=-1.0).then_inc(ez_ready, 1)
            for t in range(T):
                act.wait_ge(ZT_ready, t + 1)
                act.copy(ZT[:, tokens(t)], bank[6][0:OW, 0:P]).then_inc(ZT_read, 1)
            for t in range(T):
                act.wait_ge(ed_ready, t + 1)
                act.activation(xn[:, t, :], ed[:, t, :], ACT.Tanh, scale=0.5).then_inc(eth_ready, 1)

        @block.vector
        def _(dve):
            link = chain(dve, dve_step)
            for b in range(B):
                for t in range(b * TB, (b + 1) * TB):
                    ins = dve.bn_stats(st[:, t, :], x1[:, t, :])
                link(ins)
                for t in range(b * TB, (b + 1) * TB):
                    ins = dve.bn_aggr(mv[:, t, :], st[:, t, :])
                link(ins)
                tb = slice(b * TB, (b + 1) * TB)
                dve.tensor_scalar(ve[:, tb], mv[:, tb, 1], LN_EPS, None, ALU.add).then_inc(var_ready, 1)
            for b in range(B):
                dve.wait_ge(rstd_ready, b + 1)
                for t in range(b * TB, (b + 1) * TB):
                    dve.tensor_scalar(xn[:, t, :], x1[:, t, :], mv[:, t, 0:1], rstd[:, t:t + 1],
                                      ALU.subtract, ALU.mult).then_inc(xn_ready, 1)
            dve.wait_ge(w_in["vec"], 16)
            link(dve.tensor_scalar(vec2[:, 8, :], vec[:, 5, :], -1.0, None, ALU.mult))
            dve.tensor_tensor(vec2[:, 0, :], vec[:, 5, :], vec2[:, 8, :], ALU.max).then_inc(vec_dve, 1)
            dve.wait_ge(vec_exp, 1)
            dve.tensor_scalar(vec2[:, 2, :], vec2[:, 1, :], 1.0, None, ALU.add).then_inc(vec_dve, 1)
            dve.wait_ge(vec_dve, 2)
            link(dve.tensor_scalar(vec2[:, 6, :], vec2[:, 2, :], 1.0, None, ALU.subtract))
            link(dve.tensor_scalar(vec2[:, 7, :], vec2[:, 6, :], 0.0, None, ALU.is_equal))
            link(dve.tensor_tensor(vec2[:, 6, :], vec2[:, 6, :], vec2[:, 7, :], ALU.add))
            link(dve.reciprocal(vec2[:, 6, :], vec2[:, 6, :]))
            dve.wait_ge(vec_ln, 1)
            link(dve.tensor_tensor(vec2[:, 6, :], vec2[:, 6, :], vec2[:, 3, :], ALU.mult))
            link(dve.tensor_tensor(vec2[:, 6, :], vec2[:, 6, :], vec2[:, 7, :], ALU.add))
            link(dve.tensor_tensor(vec2[:, 6, :], vec2[:, 6, :], vec2[:, 1, :], ALU.mult))
            link(dve.scalar_tensor_tensor(out=vec2[:, 8, :], in0=vec2[:, 8, :], scalar=0.0, in1=vec2[:, 6, :],
                                          op0=ALU.max, op1=ALU.add))
            dve.tensor_scalar(vec2[:, 6, :], vec2[:, 8, :], -4.0, None, ALU.mult)
            dve.tensor_scalar(vec2[:, 7, :], vec2[:, 8, :], -8.0, None, ALU.mult)
            dve.tensor_scalar(vec2[:, 4:6, :], vec[:, 3:5, :], 0.5, None, ALU.mult).then_inc(vec_ready, 1)
            for n in range(2 * B):
                b, c = n // 2, n % 2
                part = (slice(None), c, slice(b * S, (b + 1) * S))
                dve.wait_ge(xh_ready, n + 1)
                dve.tensor_copy(xT[part], bank[n][:, :])
                dve.tensor_tensor(xl[part], bank[n][:, :], xh[part].bitcast(F32), ALU.subtract).then_inc(xl_ready, 1)

            def conv(b, p):
                n = b * HT + p
                dve.wait_ge(rin_ready, n + 1)
                if n:
                    dve.wait_ge(u_ready, n)
                if b and p == 0:
                    dve.wait_ge(ul_ready, 1)
                r = rin[:, n % 2, :]
                link(dve.tensor_scalar(cv[:, 0, :], r[:, 0:S], vec[:, 6, p:p + 1], vec[:, 2, p:p + 1],
                                       ALU.mult, ALU.add))
                link(dve.scalar_tensor_tensor(out=cv[:, 1, :], in0=r[:, 1:S + 1], scalar=vec[:, 7, p:p + 1],
                                              in1=cv[:, 0, :], op0=ALU.mult, op1=ALU.add))
                link(dve.scalar_tensor_tensor(out=cv[:, 0, :], in0=r[:, 2:S + 2], scalar=vec[:, 8, p:p + 1],
                                              in1=cv[:, 1, :], op0=ALU.mult, op1=ALU.add))
                dve.scalar_tensor_tensor(out=u[:, p, :], in0=r[:, 3:S + 3], scalar=vec[:, 9, p:p + 1],
                                         in1=cv[:, 0, :], op0=ALU.mult, op1=ALU.add).then_inc(u_ready, 1)

            def edit_in():
                dve.wait_ge(fc_ready, 1)
                dve.tensor_tensor(fcm[:, :], bank[6][0:2 * N_SEL, 0:FW], fmask[:, :], ALU.mult).then_inc(fcm_ready, 1)
                dve.wait_ge(fb_ready, 1)
                dve.tensor_copy(fb[:, :], bank[6][:, 0:FW]).then_inc(fb_read, 1)
                for t in range(T):
                    dve.wait_ge(F_ready, t + 1)
                    dve.tensor_copy(Y[:, t, :], bank[6 + t % 2][:, 0:FW]).then_inc(F_read, 1)
                dve.wait_ge(F_read, T)
                dve.wait_ge(fb_read, 1)
                dve.wait_ge(nsq_ready, T)
                NS = N_SEL * S_SEL
                link(dve.tensor_tensor(f1[:, :, :], Y[:, :, 0:NS], spread(fb[:, 0:NS], 1, T), ALU.subtract))
                link(dve.tensor_tensor(f1[:, :, :], f1[:, :, :], f1[:, :, :], ALU.mult))
                link(dve.tensor_reduce(z[:, 0, :, :].rearrange("p t n -> p (t n)"),
                                       f1[:, :, :].rearrange("p t (n s) -> p (t n) s", s=S_SEL), AX.X, ALU.add))
                link(dve.scalar_tensor_tensor(out=z[:, 1, :, :], in0=Y[:, :, 2 * NS:FW], scalar=-2.0,
                                              in1=spread(fb[:, 2 * NS:FW], 1, T), op0=ALU.mult, op1=ALU.add))
                link(dve.tensor_tensor(z[:, 1, :, :], z[:, 1, :, :], spread(nsq[:, :], 2, N_SEL), ALU.add))
                link(dve.reciprocal(z[:, 2, :, :], z[:, 1, :, :]))
                link(dve.tensor_tensor(z[:, 0, :, :], z[:, 0, :, :], z[:, 2, :, :], ALU.mult))
                dve.wait_ge(w_in["selc"], 16 * 5)
                link(dve.tensor_tensor(z[:, 0, :, :], z[:, 0, :, :], spread(sel_vec[:, 0, :], 1, T), ALU.subtract))
                link(dve.tensor_tensor(z[:, 1, :, :], z[:, 0, :, :], spread(sel_vec[:, 1, :], 1, T), ALU.mult))
                dve.tensor_scalar(z[:, 1, :, :], z[:, 1, :, :], -88.0, None, ALU.max).then_inc(z_ready, 1)

            def edit_select():
                NS = N_SEL * S_SEL
                dve.wait_ge(ez_ready, 1)
                link(dve.tensor_scalar(z[:, 3, :, :], z[:, 2, :, :], 1.0, None, ALU.add))
                link(dve.reciprocal(z[:, 0, :, :], z[:, 3, :, :]))
                link(dve.tensor_reduce(zm[:, 1, :], z[:, 0, :, :], AX.X, ALU.max))
                link(dve.tensor_tensor(z[:, 3, :, :], z[:, 0, :, :], spread(zm[:, 1, :], 2, N_SEL), ALU.is_equal))
                link(dve.tensor_tensor(z[:, 4, :, :], z[:, 3, :, :], spread(sel_vec[:, 2, :], 1, T), ALU.mult))
                link(dve.tensor_reduce(zm[:, 2, :], z[:, 4, :, :], AX.X, ALU.max))
                link(dve.tensor_tensor(ZO[:, :, NS:OW], z[:, 4, :, :], spread(zm[:, 2, :], 2, N_SEL), ALU.is_equal))
                link(dve.tensor_tensor(f1[:, :, :], Y[:, :, NS:2 * NS], spread(fb[:, NS:2 * NS], 1, T), ALU.subtract))
                for t in range(T):
                    ins = dve.tensor_tensor(ZO[:, t, 0:NS].rearrange("p (n h) -> p n h", h=H_SEL),
                                            f1[:, t, :].rearrange("p (n h) -> p n h", h=H_SEL),
                                            spread(ZO[:, t, NS:OW], 2, H_SEL), ALU.mult)
                ins.then_inc(ZO_ready, 1)

            for p in range(HT):
                conv(0, p)
            edit_in()
            for b in range(B):
                if b:
                    for p in range(HT):
                        conv(1, p)
                dve.wait_ge(sqd_ready, (b + 1) * HT)
                dve.tensor_scalar(sqd[:, :, :], sqd[:, :, :], 1.0, -1e-12, ALU.subtract, ALU.min).then_inc(om_ready, 1)
                dve.wait_ge(ti_ready, (b + 1) * HT)
                if b:
                    dve.wait_ge(pl_ready, 1)
                link(dve.scalar_tensor_tensor(out=ti[:, :, :], in0=ti[:, :, :], scalar=1.0, in1=u[:, :, :],
                                              op0=ALU.add, op1=ALU.mult))
                dve.wait_ge(beta_ready, b + 1)
                link(dve.scalar_tensor_tensor(out=drv[:, :, :], in0=ti[:, :, :], scalar=0.5, in1=sqd[:, :, :],
                                              op0=ALU.mult, op1=ALU.mult))
                dve.wait_ge(dec_ready, (b + 1) * HT)
                for p in range(HT):
                    ins = dve.tensor_tensor_scan(ti[:, p, :], dec[:, p, :], drv[:, p, :], 0.0, ALU.mult, ALU.add)
                link(ins)
                dve.wait_ge(left_ready, (b + 1) * HT)
                dve.tensor_tensor(drv[:, :, :], ti[:, :, :], left[:, :, :], ALU.mult).then_inc(prod_ready, 1)
                for t in range(b * TB, (b + 1) * TB):
                    dve.wait_ge(O_ready, t + 1)
                    dve.tensor_tensor(o1[:, t, :], bank[6 + t % 2][:, 0:D], bo[:, :], ALU.add).then_inc(o_read, 1)
            dve.wait_ge(o_read, T)
            edit_select()
            for t in range(T):
                dve.wait_ge(D_ready, t + 1)
                link(dve.tensor_tensor(ed[:, t, :], bank[4 + t % 2][:, 0:D], xn[:, t, :], ALU.subtract))
                dve.scalar_tensor_tensor(out=ed[:, t, :], in0=ed[:, t, :], scalar=zm[:, 1, t:t + 1],
                                         in1=xn[:, t, :], op0=ALU.mult, op1=ALU.add).then_inc(ed_ready, 1)
            for t in range(T):
                dve.wait_ge(eth_ready, t + 1)
                link(dve.scalar_tensor_tensor(out=ed[:, t, :], in0=xn[:, t, :], scalar=1.0, in1=ed[:, t, :],
                                              op0=ALU.add, op1=ALU.mult))
                link(dve.scalar_tensor_tensor(out=xn[:, t, :], in0=o1[:, t, :], scalar=0.5, in1=ed[:, t, :],
                                              op0=ALU.mult, op1=ALU.mult))
                dve.tensor_tensor(ed[:, t, :], xn[:, t, :], x1[:, t, :], ALU.add).then_inc(out_ready, 1)

        @block.tensor
        def _(pe):
            for n in range(2 * B):
                b, c = n // 2, n % 2
                for i in range(TB):
                    pe.wait_ge(xn_ready, b * TB + i + 1)
                    ins = pe.transpose(bank[n][:, i * P:(i + 1) * P], xn[:, b * TB + i, c * P:(c + 1) * P], ident[:, :])
                ins.then_inc(xT_ready, 1)

            def right_in(b):
                pe.wait_ge(wl_ready, 1)
                pe.wait_ge(xl_ready, 2 * (b + 1))
                for p in range(HT):
                    n = b * HT + p
                    if n >= 2:
                        pe.wait_ge(rin_ready, n - 1)
                    for k in range(KD):
                        w = slice(HP + p * P, HP + (p + 1) * P)
                        ins = split_matmul(pe, bank[4 + n % 2][:, :], w_lr_h[:, k, w], w_lr_l[:, k, w],
                                           xh[:, k, b * S:(b + 1) * S], xl[:, k, b * S:(b + 1) * S],
                                           k == 0, k == KD - 1)
                    ins.then_inc(R_ready, 1)

            def left_in(b):
                for p in range(HT):
                    n = b * HT + p
                    if n >= 2:
                        pe.wait_ge(left_ready, n - 1)
                    w = slice(p * P, (p + 1) * P)
                    for k in range(KD):
                        ins = split_matmul(pe, bank[2 + n % 2][:, :], w_lr_h[:, k, w], w_lr_l[:, k, w],
                                           xh[:, k, b * S:(b + 1) * S], xl[:, k, b * S:(b + 1) * S],
                                           k == 0, k == KD - 1)
                    ins.then_inc(L_ready, 1)

            def gates(b):
                pe.wait_ge(wl_ready, 2)
                pe.wait_ge(ul_ready, b + 1)
                for p in range(HT):
                    n = b * HT + p
                    if n:
                        pe.wait_ge(ta_ready, n)
                    for g, done in ((0, A_ready), (1, I_ready)):
                        if g and n:
                            pe.wait_ge(ti_ready, n)
                        w = slice(g * HP + p * P, g * HP + (p + 1) * P)
                        for k in range(HT):
                            ins = split_matmul(pe, bank[g][:, :], w_ai_h[:, k, w], w_ai_l[:, k, w],
                                               uh[:, k, :], ul[:, k, :], k == 0, k == HT - 1)
                        ins.then_inc(done, 1)

            def mix_out(b):
                pe.wait_ge(wl_ready, 3)
                pe.wait_ge(pl_ready, b + 1)
                for i in range(TB):
                    t = b * TB + i
                    if t >= 2:
                        pe.wait_ge(o_read, t - 1)
                    if t == 0:
                        pe.wait_ge(F_read, T)
                    for k in range(HT):
                        ins = split_matmul(pe, bank[6 + t % 2][:, 0:D],
                                           uh[:, k, tokens(i)], ul[:, k, tokens(i)], w_o_h[:, k, :], w_o_l[:, k, :],
                                           k == 0, k == HT - 1)
                    ins.then_inc(O_ready, 1)

            def edit_products():
                pe.wait_ge(w_in["f"], 64)
                for k in range(KD):
                    ins = pe.matmul(bank[6][0:2 * N_SEL, 0:FW], md[:, k, :], w_f[:, k, :],
                                    start=(k == 0), stop=(k == KD - 1))
                ins.then_inc(fc_ready, 1)
                pe.wait_ge(fcm_ready, 1)
                pe.matmul(bank[6][:, 0:FW], ones16[:, :], fcm[:, :], start=True, stop=True).then_inc(fb_ready, 1)
                pe.wait_ge(fb_read, 1)
                for t in range(T):
                    if t >= 2:
                        pe.wait_ge(F_read, t - 1)
                    for k in range(KD):
                        ins = pe.matmul(bank[6 + t % 2][:, 0:FW], xT[:, k, tokens(t)], w_f[:, k, :],
                                        start=(k == 0), stop=(k == KD - 1))
                    ins.then_inc(F_ready, 1)

            right_in(0)
            pe.wait_ge(xl_ready, 2 * B)
            edit_products()
            gates(0)
            left_in(0)
            right_in(1)
            mix_out(0)
            gates(1)
            left_in(1)
            mix_out(1)
            pe.wait_ge(ZO_ready, 1)
            pe.wait_ge(o_read, T)
            for t in range(T):
                if t:
                    pe.wait_ge(ZT_read, t)
                pe.transpose(bank[6][0:OW, 0:P], ZO[:, t, :], ident[:, :]).then_inc(ZT_ready, 1)
            pe.wait_ge(w_in["selc"], 16 * 5)
            pe.wait_ge(ZT_read, T)
            for t in range(T):
                if t >= 2:
                    pe.wait_ge(ed_ready, t - 1)
                pe.matmul(bank[4 + t % 2][:, 0:D], ZT[:, tokens(t)], w_g[:, :], start=True, stop=True).then_inc(D_ready, 1)


_OUTS = [((2, 512, 256), 'float32')]


def _constants():
    f, bf = np.float32, np.dtype("bfloat16")
    pos = np.arange(S, dtype=f)
    inv = (1.0 / 10000.0 ** (np.arange(0, DH, 2).astype(f) / f(DH))).astype(f)
    ang = (pos[:, None] * inv).astype(f)
    cos, sin = np.cos(ang).astype(f), np.sin(ang).astype(f)
    tok = np.arange(P)

    def by_tile(v):
        return np.ascontiguousarray(v.reshape(TB, P, -1).transpose(1, 0, 2))
    own = np.arange(S)[:, None] // BLK
    blk = np.arange(NBLK)[None, :]
    gate_add = np.where(blk > own, f(NEG), np.where(blk == own, f(-NEG), f(0))).astype(f)
    later = (tok[None, :] > tok[:, None])
    ksel = np.zeros((64, ECH, P), f)
    unit = np.arange(ECH * P).reshape(ECH, P)
    for level in range(3):
        for e in range(E):
            ksel[level * E + e] = (unit // EH == e)
    kconst = np.ones((R_ALL - R_BIAS, T * P), f)
    kconst[:NBLK] = (np.arange(T * P)[None, :] % S // BLK) == np.arange(NBLK)[:, None]
    fmask = np.zeros((2 * N_SEL, FW), f)
    for n in range(N_SEL):
        fmask[n, n * S_SEL:(n + 1) * S_SEL] = 1
        fmask[N_SEL + n, N_SEL * S_SEL + n * H_SEL:N_SEL * S_SEL + (n + 1) * H_SEL] = 1
        fmask[n, 2 * N_SEL * S_SEL + n] = 1
    return {
        "c_ident": np.eye(P, dtype=f),
        "c_cos": by_tile(np.concatenate([cos, cos], 1)),
        "c_sin": by_tile(np.concatenate([-sin, sin], 1)),
        "c_gate_add": by_tile(gate_add),
        "c_future": np.where(blk > tok[:, None] // BLK, f(NEG), f(0)).astype(f),
        "c_headmask": np.repeat((tok[:, None] // DH == np.arange(8)[None, :]).astype(f)[:, :, None], NBLK, 2),
        "c_tri": np.stack([np.where(later, f(NEG), f(0)), np.where(later.T, f(NEG), f(0))], 1).astype(bf),
        "c_ksel": ksel.astype(bf),
        "c_kconst": kconst.astype(bf),
        "c_ident_b": np.eye(P, dtype=f).astype(bf),
        "c_fmask": fmask,
        "c_ones16": np.ones((2 * N_SEL, P), f),
        "c_rank": np.tile(np.arange(N_SEL, 0, -1, dtype=f), (P, 1)),
    }


def _layout(v):
    def pad(w, rows, cols):
        return np.pad(w, ((0, rows - w.shape[0]), (0, cols - w.shape[1])))

    def wide(w):
        return w.transpose(1, 0, 2).reshape(D, E * EH)
    gate = np.concatenate([wide(v["L0_ffn_w_gate"]), pad(v["L0_ffn_sw_gate"], D, SCH * P)], 1)
    up = np.concatenate([wide(v["L0_ffn_w_up"]), pad(v["L0_ffn_sw_up"], D, SCH * P)], 1)
    down = np.concatenate([v["L0_ffn_w_down"].reshape(E * EH, D), pad(v["L0_ffn_sw_down"], SCH * P, D)], 0)
    chunks = np.empty((CH, P, 3, 2 * P), np.float32)
    for w, o in ((gate, 0), (up, P)):
        chunks[:, :, 0:KD, o:o + P] = w.reshape(KD, P, CH, P).transpose(2, 1, 0, 3)
    chunks[:, :, 2, :] = down.reshape(CH, P, D)
    vecs = [v["L1_attn_" + n] for n in ("bl", "br", "conv_b", "ba", "bi", "lam")] + list(v["L1_attn_conv_w"][:, 0])
    vecs = np.stack([np.pad(w, (0, HP - HID)).reshape(HT, P) for w in vecs])

    def side(w):
        return w.transpose(1, 0, 2).reshape(D, -1)
    return {
        "x": v["L0_attn_hidden_states"].reshape(B * S, D),
        "w_proj": np.concatenate([v["L0_attn_Wq"].T, v["L0_attn_Wk"].T, v["L0_attn_Wv"].T, v["L0_ffn_gate_w"]], 1),
        "w_o": v["L0_attn_Wo"].T,
        "w_chunks": chunks,
        "w_lr": np.concatenate([pad(v["L1_attn_Wl"], D, HP), pad(v["L1_attn_Wr"], D, HP)], 1),
        "w_ai": np.concatenate([pad(v["L1_attn_Wa"], HP, HP), pad(v["L1_attn_Wi"], HP, HP)], 1),
        "w_o1": pad(v["L1_attn_Wo"], HP, D),
        "w_f": np.concatenate([side(v["L1_ffn_select_weight"]), side(v["L1_ffn_lora_update"]),
                               v["L1_ffn_select_mean_diff"].T], 1),
        "w_md": np.concatenate([v["L1_ffn_select_mean_diff"].T, v["L1_ffn_debias_w"].T], 1),
        "w_g": np.concatenate([v["L1_ffn_lora_degen"].transpose(0, 2, 1).reshape(N_SEL * H_SEL, D),
                               v["L1_ffn_bias_w"]], 0),
        "vecs": vecs.transpose(2, 0, 1),
        "L0_attn_o_norm_w": v["L0_attn_o_norm_w"],
        "L1_ffn_imp_center": v["L1_ffn_imp_center"],
        "L1_ffn_imp_slope": v["L1_ffn_imp_slope"],
        "L1_attn_bo": v["L1_attn_bo"],
    }


def program(nc, a, out):
    with ExitStack() as ctx:
        m = Mem(nc, ctx)
        x1 = m.sb("x1", [P, T, D])
        cst = {"ident": m.sb("ident", [P, P]), "ident_b": m.sb("ident_b", [P, P], BF16),
               "ident_in": m.sem("ident_in")}
        layer0(nc, a, x1, cst)
        layer1(nc, a, x1, out, cst)


def kernel(**inputs):
    import numpy as _np
    import concourse.bacc as _bacc
    from concourse import mybir as _mybir
    from concourse.bass_utils import run_bass_kernel_spmd as _run

    nc = _bacc.Bacc("TRN2", target_bir_lowering=False, num_devices=1)
    data = _layout({k: _np.asarray(v) for k, v in inputs.items()})
    data.update(_constants())
    arrays, args = {}, {}
    for name, v in data.items():
        v = _np.ascontiguousarray(v)
        arrays[f"in_{name}_dram"] = v
        args[name] = nc.dram_tensor(f"in_{name}_dram", v.shape, _mybir.dt.from_np(v.dtype), kind="ExternalInput").ap()
    (shape, dtype), = _OUTS
    out = nc.dram_tensor("out_0_dram", shape, _mybir.dt.from_np(_np.dtype(dtype)), kind="ExternalOutput").ap()
    program(nc, args, out.rearrange("b s d -> (b s) d"))
    r = _run(nc, [arrays], core_ids=[0])
    return r.results[0]["out_0_dram"]
```

```python
from contextlib import ExitStack

import numpy as np

import concourse.bass as bass
from concourse import mybir

ALU = mybir.AluOpType
ACT = mybir.ActivationFunctionType
AX = mybir.AxisListType
F32 = mybir.dt.float32
F32R = mybir.dt.float32r
BF16 = mybir.dt.bfloat16

P = 128
B, S, D = 2, 512, 256
T = B * S // P
TB = S // P
KD = D // P
LN_EPS = 1e-5
NEG = -1e30

H, DH, BLK, TOPK = 16, 16, 32, 4
NBLK = S // BLK
GATE_ROW = NBLK + TOPK
HG = 4
NG = H // HG
RMS_EPS = 1e-6
E, EK, EH, SH = 8, 2, 176, 352
ECH = E * EH // P
SCH = -(-SH // P)
CH = ECH + SCH
EROW = E + 8 - EK
HALVES = 2
STEPS = HALVES * CH
SENT, SENT_TEST = 3e38, 1e38
STACK = [(0, 0), (0, 1), (1, 0), (1, 1), (0, 2), (2, 0)]
R_BIAS = len(STACK) * DH
R_MAX = R_BIAS + NBLK
R_ALL = R_MAX + 3
SLOTS = 4

HID = 320
HT = -(-HID // P)
HP = HT * P
TAPS = 4
N_SEL, S_SEL, H_SEL = 8, 8, 8
FW = N_SEL * S_SEL + N_SEL * H_SEL + N_SEL
OW = N_SEL * H_SEL + N_SEL


def unit_loads(g):
    heads = list(range(HG * g, HG * g + HG))
    loads = [(0, heads), (1, heads[:2]), (1, heads[2:])]
    loads += [(i, [h]) for i in (2, 3) for h in heads]
    return loads


LOADS = len(unit_loads(0))
A_SLOTS = B * NG * LOADS // 2
B_SLOT = A_SLOTS + 2
B_SLOTS = B * NG * TB * HG // 2
YTH_STEP = (B_SLOT + B_SLOTS // 2) // SLOTS + 2
UNIT_SLOTS = TB * HG // 2
MAX_SLOTS = [A_SLOTS // B, A_SLOTS]
BIAS_STEP = TB - 1


def out_unit(q, lag):
    v = q - B_SLOT - UNIT_SLOTS - lag
    return v // UNIT_SLOTS if v >= 0 and v % UNIT_SLOTS == 0 and v // UNIT_SLOTS < B * NG else None


def spread(ap, axis, n):
    v = ap.unsqueeze(axis)
    shape = list(v.shape)
    shape[axis] = n
    return v.broadcast_to(shape)


class Mem:
    def __init__(self, nc, ctx):
        self.nc, self.ctx = nc, ctx

    def sb(self, name, shape, dt=F32):
        return self.ctx.enter_context(self.nc.sbuf_tensor(name, shape, dt))

    def ps(self, name, dt=F32):
        return self.ctx.enter_context(self.nc.psum_tensor(name, [P, 2048 // (4 if dt == F32 else 2)], dt))

    def sem(self, name):
        return self.ctx.enter_context(self.nc.semaphore(name))


def chain(eng, sem):
    done = [0]

    def link(ins):
        done[0] += 1
        ins.then_inc(sem, 1)
        eng.wait_ge(sem, done[0])
    return link


def split_matmul(pe, out, l_hi, l_lo, r_hi, r_lo, start, stop, skip=False):
    pe.matmul(out, l_hi, r_hi, start=start, stop=False, skip_group_check=skip)
    pe.matmul(out, l_hi, r_lo, start=False, stop=False, skip_group_check=skip)
    return pe.matmul(out, l_lo, r_hi, start=False, stop=stop, skip_group_check=skip)


def layer0(nc, a, x1, cst):
    ctx = ExitStack()
    with ctx:
        m = Mem(nc, ctx)
        ident, ident_b = cst["ident"], cst["ident_b"]
        tri = m.sb("tri", [P, 2, P], BF16)
        ksel = m.sb("ksel", [64, ECH, P], BF16)
        onorm = m.sb("onorm", [P, DH])
        mhalf = m.sb("mhalf", [P, P])
        xn = x1
        xh = m.sb("xh", [P, KD, T * P], F32R)
        xl = m.sb("xl", [P, KD, T * P], F32R)
        bias = m.sb("bias", [P, T, H, NBLK], BF16)
        biasT = m.sb("biasT", [P, 2, 512], BF16)
        QS = m.sb("QS", [P, H, T * P], BF16)
        KS = m.sb("KS", [P, H, T * P], BF16)
        V = m.sb("V", [P, T, H, 32])
        mx = m.sb("mx", [P, T, H])
        mr = m.sb("mr", [P, 2, TB, H])
        ms = m.sb("ms", [P, T, 3, H], BF16)
        lg = m.sb("lg", [P, T, E])
        rt = m.sb("rt", [P, 4, T, E])
        rm = m.sb("rm", [P, 3, T])
        sc = m.sb("sc", [P, T, EROW])
        cs = m.sb("cs", [P, T, 64], BF16)
        combT = m.sb("combT", [64, T * P], BF16)
        wr = m.sb("wr", [P, 2, 3, 256])
        wh = m.sb("wh", [P, 3, 3, 256], F32R)
        wl = m.sb("wl", [P, 3, 3, 256], F32R)
        gates = m.sb("gates", [P, TB - 1, H, GATE_ROW])
        top = m.sb("top", [P, H, 8])
        picked = m.sb("picked", [P, H, GATE_ROW])

        early_ctx = ExitStack()
        early = Mem(nc, early_ctx)
        x = early.sb("x", [P, T, D])
        wp = early.sb("wp", [P, KD, 776])
        wp_h = early.sb("wp_h", [P, KD, 776], F32R)
        wp_l = early.sb("wp_l", [P, KD, 776], F32R)
        rot_a = early.sb("rot_a", [P, 512])
        rot_b = early.sb("rot_b", [P, 512])
        qkr = early.sb("qkr", [P, TB, 512])
        X = early.sb("X", [P, 4, 512])
        R1 = wp[:, :, 0:512]
        parts = early.sb("parts", [P, 2, 3, 512], BF16)
        km = early.sb("km", [P, 4, NBLK])
        kmb = early.sb("kmb", [P, 4, 8, NBLK])
        cos = early.sb("cos", [P, TB, DH])
        sin = early.sb("sin", [P, TB, DH])
        gate_add = early.sb("gate_add", [P, TB, NBLK])
        future = early.sb("future", [P, NBLK])
        headmask = early.sb("headmask", [P, 8, NBLK])
        st = early.sb("st", [P, T, 6])
        mv = early.sb("mv", [P, T, 2])
        ve = early.sb("ve", [P, T])
        rstd = early.sb("rstd", [P, T])
        rpick = early.sb("rpick", [P, T, EROW])
        rtop = early.sb("rtop", [P, T, 8])
        early_ctx.close()
        PT = m.sb("PT", [P, 8, 512])
        oT = m.sb("oT", [P, 512])
        th = m.sb("th", [P, 512])
        s2 = m.sb("s2", [P, 512])
        uv = m.sb("uv", [P, 512])
        gb = m.sb("gb", [P, 512])
        gh = m.sb("gh", [P, 2, 512], F32R)
        gl = m.sb("gl", [P, 2, 512], F32R)
        y = m.sb("y", [P, T, D])
        ob = m.sb("ob", [P, T, H, DH + 1])
        small = m.sb("small", [P, 3, TB, HG])
        msT = m.sb("msT", [48, 2, 512], BF16)
        wo = PT[:, 0, :].rearrange("p (k n) -> p k n", n=D)
        wo_h = m.sb("wo_h", [P, KD, D], F32R)
        wo_l = m.sb("wo_l", [P, KD, D], F32R)

        bank = [m.ps(f"bank{i}") for i in range(8)]
        bank_b = [bank[i][:, :].bitcast(BF16) for i in range(8)]

        parts_dram = nc.dram_tensor("parts_dram", (B, 2, 3, D, S), BF16, kind="Internal").ap()
        bias_dram = nc.dram_tensor("bias_dram", (B, D, S), BF16, kind="Internal").ap()
        max_dram = nc.dram_tensor("max_dram", (B, 3 * H, S), BF16, kind="Internal").ap()

        x_in = [m.sem(f"x_in{b}") for b in range(B)]
        sem_wp, sem_wo, sem_const, x_again = (m.sem(n) for n in ("wp_in", "wo_in", "const_in", "x_again"))
        init_done = m.sem("init_done")
        half_done = m.sem("half_done")
        var_ready, rstd_ready, xn_ready = m.sem("var_ready"), m.sem("rstd_ready"), m.sem("xn_ready")
        xT_ready, xh_ready, xl_ready = m.sem("xT_ready"), m.sem("xh_ready"), m.sem("xl_ready")
        wph_ready, wpl_ready, woh_ready, wol_ready = (m.sem(n) for n in ("wph", "wpl", "woh", "wol"))
        qk_ready, vg_ready, qk_read, vg_read = (m.sem(n) for n in ("qk_ready", "vg_ready", "qk_read", "vg_read"))
        rope_ready = m.sem("rope_ready")
        qkT_ready, X_ready, H_ready, R1_ready, M_ready, L_ready = (
            m.sem(n) for n in ("qkT_ready", "X_ready", "H_ready", "R1_ready", "M_ready", "L_ready"))
        parts_out = [m.sem(f"parts_out{i}") for i in range(2)]
        q_stacked = [m.sem(f"q_stacked{b}") for b in range(B)]
        k_stacked = [m.sem(f"k_stacked{b}") for b in range(B)]
        kconst_ready = m.sem("kconst_ready")
        kmb_ready, gate_ready, gate_read, bias_ready = (
            m.sem(n) for n in ("kmb_ready", "gate_ready", "gate_read", "bias_ready"))
        biasT_ready, biasT_read, bias_out = m.sem("biasT_ready"), m.sem("biasT_read"), m.sem("bias_out")
        e_in, e_out, comb_ready, combT_ready, combT_read = (
            m.sem(n) for n in ("e_in", "e_out", "comb_ready", "combT_ready", "combT_read"))
        w_in = [m.sem("w_in0"), m.sem("w_in1")]
        wh_ready, wl_ready = m.sem("wh_ready"), m.sem("wl_ready")
        G_ready, U_ready, th_ready, G_read, g_ready, gh_ready, gl_ready, down_done = (
            m.sem(n) for n in ("G_ready", "U_ready", "th_ready", "G_read", "g_ready", "gh_ready", "gl_ready",
                               "down_done"))
        y_read = m.sem("y_read")
        A_ready, A_read, max_ready, maxT_ready, maxT_read, max_out = (
            m.sem(n) for n in ("A_ready", "A_read", "max_ready", "maxT_ready", "maxT_read", "max_out"))
        B_ready, P_ready, PV_done, oT_ready, oTT_ready, ob_ready = (
            m.sem(n) for n in ("B_ready", "P_ready", "PV_done", "oT_ready", "oTT_ready", "ob_ready"))
        rms_in, rms_out, on_ready, onT_ready, onh_ready, onl_ready = (
            m.sem(n) for n in ("rms_in", "rms_out", "on_ready", "onT_ready", "onh_ready", "onl_ready"))
        yth_ready, s_ready, x1_ready = m.sem("yth_ready"), m.sem("s_ready"), m.sem("x1_ready")
        dve_step, act_step, pool_step = m.sem("dve_step"), m.sem("act_step"), m.sem("pool_step")

        def tokens(t, n=1):
            return slice(t * P, (t + n) * P)

        def unit_of(u):
            return u // (NG * TB), (u // TB) % NG, u % TB

        xr = KS[:, 4:12, 0:S].bitcast(F32)
        yth = QS[:, 0:8, 0:S].bitcast(F32)
        sq = KS[:, 0, 0:S].bitcast(F32).rearrange("p (i h d) -> p i h d", i=TB, d=DH)

        block = ctx.enter_context(nc.Block())

        @block.sync
        def _(sp):
            for b in range(B):
                sp.dma_start(x[:, b * TB:(b + 1) * TB, :],
                             a["x"].rearrange("(t p) d -> p t d", p=P)[:, b * TB:(b + 1) * TB, :]).then_inc(x_in[b], 16)
            sp.dma_start(cst["ident"][:, :], a["c_ident"]).then_inc(cst["ident_in"], 16)
            sp.dma_start(wp[:, :, :], a["w_proj"].rearrange("(k p) n -> p k n", p=P)).then_inc(sem_wp, 16)
            for dst, src in ((cos[:, :, :], a["c_cos"]), (sin[:, :, :], a["c_sin"]),
                             (gate_add[:, :, :], a["c_gate_add"]), (future[:, :], a["c_future"]),
                             (headmask[:, :, :], a["c_headmask"]), (tri[:, :, :], a["c_tri"]),
                             (ksel[:, :, :], a["c_ksel"]), (ident_b[:, :], a["c_ident_b"]),
                             (onorm[:, :], a["L0_attn_o_norm_w"].unsqueeze(0).broadcast_to([P, DH]))):
                sp.dma_start(dst, src).then_inc(sem_const, 16)
            sp.dma_start(KS[R_BIAS:R_ALL, :, :], spread(a["c_kconst"], 1, H)).then_inc(kconst_ready, 16)

            def load_chunk(s):
                c = s % CH
                if s >= 2:
                    sp.wait_ge(wh_ready, s - 1)
                    sp.wait_ge(wl_ready, s - 1)
                sp.dma_start(wr[:, s % 2, :, :], a["w_chunks"][c]).then_inc(w_in[s % 2], 16)

            def stack_bias(b):
                sp.wait_ge(biasT_read, 2 * (b + 1))
                sp.dma_start(bias_dram[b].rearrange("(f p) t -> p f t", p=P),
                             biasT[:, :, :]).then_inc(bias_out, 16)
                sp.wait_ge(bias_out, 16 * (b + 1))
                sp.dma_start(QS[R_BIAS:R_MAX, :, b * S:(b + 1) * S],
                             bias_dram[b].rearrange("(h n) t -> n h t", n=NBLK)).then_inc(q_stacked[b], 16)

            load_chunk(0)
            load_chunk(1)
            for b in range(B):
                for k in range(4):
                    n = 4 * b + k
                    which, half = k // 2, k % 2
                    sp.wait_ge(H_ready, n + 1)
                    sp.wait_ge(M_ready, n + 1)
                    sp.wait_ge(L_ready, n + 1)
                    sp.dma_start(parts_dram[b, which, :, half * P:(half + 1) * P, :].rearrange("l p t -> p l t"),
                                 parts[:, n % 2, :, :]).then_inc(parts_out[n % 2], 16)
                    if half == 0:
                        continue
                    sp.wait_ge(parts_out[0], 16 * (n // 2 + 1))
                    sp.wait_ge(parts_out[1], 16 * (n // 2 + 1))
                    dst, done = ((QS, q_stacked), (KS, k_stacked))[which]
                    for r, pair in enumerate(STACK):
                        sp.dma_start(dst[r * DH:(r + 1) * DH, :, b * S:(b + 1) * S],
                                     parts_dram[b, which, pair[which]].rearrange("(h d) t -> d h t", d=DH)
                                     ).then_inc(done[b], 16)
                if b == 0:
                    stack_bias(0)
            sp.wait_ge(combT_read, 1)
            sp.dma_start(wo[:, :, :], a["w_o"].rearrange("(k p) n -> p k n", p=P)).then_inc(sem_wo, 16)
            for s in range(2, STEPS):
                load_chunk(s)
                if s == BIAS_STEP + 3:
                    stack_bias(1)
                if s == (B_SLOT + B_SLOTS // 2) // SLOTS + 5:
                    sp.wait_ge(PV_done, NG * TB)
                    sp.dma_start(xr, a["x"].rearrange("(t p) d -> p t d", p=P)).then_inc(x_again, 16)
                for b in range(B):
                    if s == MAX_SLOTS[b] // SLOTS + 4:
                        sp.wait_ge(maxT_read, b + 1)
                        sp.dma_start(max_dram[b], msT[:, b, :]).then_inc(max_out, 16)
                        sp.wait_ge(max_out, 16 * (b + 1))
                        sp.dma_start(QS[R_MAX:R_ALL, :, b * S:(b + 1) * S],
                                     max_dram[b].rearrange("(l h) t -> l h t", l=3)).then_inc(q_stacked[b], 16)

        @block.gpsimd
        def _(pool):
            link = chain(pool, pool_step)
            pool.memset(mhalf[:, :], -0.5).then_inc(half_done, 1)
            link(pool.memset(V[:, :, :, :], 0.0))
            link(pool.memset(V[:, :, :, DH:DH + 1], 1.0))
            link(pool.memset(gates[:, :, :, NBLK:GATE_ROW], SENT))
            link(pool.memset(sc[:, :, E:EROW], SENT))
            pool.memset(cs[:, :, :], 0.0).then_inc(init_done, 1)
            pool.wait_ge(half_done, 1)
            for b in range(B):
                tb = slice(b * TB, (b + 1) * TB)
                pool.wait_ge(var_ready, b + 1)
                pool.tensor_tensor(rstd[:, tb], ve[:, tb], mhalf[:, 0:TB], ALU.pow).then_inc(rstd_ready, 1)
            pool.wait_ge(wph_ready, 1)
            pool.tensor_tensor(wp_l[:, :, :], wp[:, :, :], wp_h[:, :, :].bitcast(F32), ALU.subtract).then_inc(wpl_ready, 1)

            def split_chunk(s):
                pool.wait_ge(wh_ready, s + 1)
                if s >= 3:
                    pool.wait_ge(down_done, s - 2)
                pool.tensor_tensor(wl[:, s % 3, :, :], wr[:, s % 2, :, :], wh[:, s % 3, :, :].bitcast(F32),
                                   ALU.subtract).then_inc(wl_ready, 1)

            def inverse_roots(w):
                pool.wait_ge(rms_in, w + 1)
                pool.tensor_tensor(small[:, 2, :, :], small[:, 1, :, :],
                                   mhalf[:, 0:TB * HG].rearrange("p (i h) -> p i h", h=HG), ALU.pow).then_inc(rms_out, 1)

            def third_parts(b):
                for k in range(4):
                    n = 4 * b + k
                    pool.wait_ge(M_ready, n + 1)
                    pool.wait_ge(R1_ready, n + 1)
                    if n >= 2:
                        pool.wait_ge(parts_out[n % 2], 16 * (n // 2))
                    pool.tensor_tensor(parts[:, n % 2, 2, :], R1[:, n % 2, :], parts[:, n % 2, 1, :],
                                       ALU.subtract).then_inc(L_ready, 1)

            for t in range(T):
                pool.wait_ge(qk_read, t + 1)
                if t >= TB:
                    pool.wait_ge(qkT_ready, 4)
                pool.tensor_tensor(qkr[:, t % TB, :], rot_a[:, :], rot_b[:, :],
                                   ALU.add).then_inc(rope_ready, 1)
                if t == TB - 1:
                    third_parts(0)
            third_parts(1)
            split_chunk(0)
            for s in range(STEPS):
                if s + 1 < STEPS:
                    split_chunk(s + 1)
                pool.wait_ge(gh_ready, s + 1)
                if s >= 2:
                    pool.wait_ge(down_done, s - 1)
                pool.tensor_tensor(gl[:, s % 2, :], gb[:, :], gh[:, s % 2, :].bitcast(F32),
                                   ALU.subtract).then_inc(gl_ready, 1)
                if s == 1:
                    pool.wait_ge(woh_ready, 1)
                    pool.tensor_tensor(wo_l[:, :, :], wo[:, :, :], wo_h[:, :, :].bitcast(F32),
                                       ALU.subtract).then_inc(wol_ready, 1)
                for q in range(s * SLOTS, (s + 1) * SLOTS):
                    if out_unit(q, 4) is not None:
                        inverse_roots(out_unit(q, 4))
            inverse_roots(B * NG - 1)

        @block.scalar
        def _(act):
            act.wait_ge(sem_wp, 16)
            act.copy(wp_h[:, :, :], wp[:, :, :]).then_inc(wph_ready, 1)
            for n in range(2 * B):
                b, c = n // 2, n % 2
                act.wait_ge(xT_ready, n + 1)
                act.copy(xh[:, c, b * S:(b + 1) * S], bank[n][:, :]).then_inc(xh_ready, 1)

            def values(t):
                act.wait_ge(vg_ready, t + 1)
                act.wait_ge(init_done, 1)
                vg = bank[6 + t % 2]
                act.copy(V[:, t, :, 0:DH], vg[:, 0:D].rearrange("p (h d) -> p h d", d=DH))
                act.copy(lg[:, t, :], vg[:, D:D + E]).then_inc(vg_read, 1)

            def first_parts(b):
                for k in range(4):
                    n = 4 * b + k
                    act.wait_ge(X_ready, n + 1)
                    if n >= 2:
                        act.wait_ge(parts_out[n % 2], 16 * (n // 2))
                    act.copy(parts[:, n % 2, 0, :], X[:, n % 4, :]).then_inc(H_ready, 1)
                    act.wait_ge(R1_ready, n + 1)
                    act.copy(parts[:, n % 2, 1, :], R1[:, n % 2, :]).then_inc(M_ready, 1)

            def split_chunk(s):
                act.wait_ge(w_in[s % 2], 16 * (s // 2 + 1))
                if s >= 3:
                    act.wait_ge(down_done, s - 2)
                act.copy(wh[:, s % 3, :, :], wr[:, s % 2, :, :]).then_inc(wh_ready, 1)

            def bias_rows(b):
                for f in range(2):
                    act.wait_ge(biasT_ready, 4 if b else f + 1)
                    src = bank_b[2][:, f * 512:(f + 1) * 512] if b else bank_b[6 + f][:, 0:512]
                    if b:
                        act.wait_ge(bias_out, 16)
                    act.copy(biasT[:, f, :], src).then_inc(biasT_read, 1)

            for t in range(TB):
                values(t)
            first_parts(0)
            for t in range(TB, T):
                values(t)
            bias_rows(0)
            act.wait_ge(e_in, 1)
            act.activation(rt[:, 1, :, :], rt[:, 0, :, :], ACT.Exp).then_inc(e_out, 1)
            first_parts(1)
            split_chunk(0)
            act.wait_ge(combT_ready, 1)
            act.copy(combT[:, :], bank_b[6][0:64, :]).then_inc(combT_read, 1)

            def half_silu(n):
                act.wait_ge(PV_done, NG * TB)
                act.wait_ge(y_read, 2 * (n + 1))
                act.activation(yth[:, n * TB:(n + 1) * TB, :], y[:, n * TB:(n + 1) * TB, :], ACT.Tanh,
                               scale=0.5).then_inc(yth_ready, 1)

            def slot(q):
                v = q - B_SLOT
                if not 0 <= v < B_SLOTS:
                    return
                if v == 0:
                    act.wait_ge(wol_ready, 1)
                for k in (2 * v, 2 * v + 1):
                    u = k // HG
                    n = S - (u % TB) * P
                    act.wait_ge(B_ready, k + 1)
                    if k >= 8:
                        act.wait_ge(PV_done, u - 1)
                    act.activation(PT[:, k % 8, 0:n], bank[k % 2][:, 0:n], ACT.Exp,
                                   scale=float(DH) ** -0.5).then_inc(P_ready, 1)

            for s in range(STEPS):
                act.wait_ge(G_ready, s + 1)
                if s >= 1:
                    act.wait_ge(G_read, s)
                act.activation(th[:, :], bank[3][:, :], ACT.Tanh, scale=0.5).then_inc(th_ready, 1)
                slot(s * SLOTS)
                if s + 1 < STEPS:
                    split_chunk(s + 1)
                slot(s * SLOTS + 1)
                act.wait_ge(g_ready, s + 1)
                if s >= 2:
                    act.wait_ge(down_done, s - 1)
                act.copy(gh[:, s % 2, :], gb[:, :]).then_inc(gh_ready, 1)
                slot(s * SLOTS + 2)
                slot(s * SLOTS + 3)
                if s == 1:
                    act.wait_ge(sem_wo, 16)
                    act.copy(wo_h[:, :, :], wo[:, :, :]).then_inc(woh_ready, 1)
                if s == BIAS_STEP:
                    bias_rows(1)
                for b in range(B):
                    if s == (MAX_SLOTS[b] + 1) // SLOTS:
                        act.wait_ge(maxT_ready, b + 1)
                        act.copy(msT[:, b, :], bank_b[2][0:48, 0:512]).then_inc(maxT_read, 1)
                if s == YTH_STEP:
                    half_silu(0)
            half_silu(1)
            for n in range(2 * B):
                act.wait_ge(onT_ready, n + 1)
                act.copy(xh[:, n % 2, (n // 2) * S:(n // 2 + 1) * S], bank[n][:, :]).then_inc(onh_ready, 1)

        @block.vector
        def _(dve):
            link = chain(dve, dve_step)
            for b in range(B):
                dve.wait_ge(x_in[b], 16)
                for t in range(b * TB, (b + 1) * TB):
                    ins = dve.bn_stats(st[:, t, :], x[:, t, :])
                link(ins)
                for t in range(b * TB, (b + 1) * TB):
                    ins = dve.bn_aggr(mv[:, t, :], st[:, t, :])
                link(ins)
                tb = slice(b * TB, (b + 1) * TB)
                dve.tensor_scalar(ve[:, tb], mv[:, tb, 1], LN_EPS, None, ALU.add).then_inc(var_ready, 1)
            for b in range(B):
                dve.wait_ge(rstd_ready, b + 1)
                for t in range(b * TB, (b + 1) * TB):
                    dve.tensor_scalar(xn[:, t, :], x[:, t, :], mv[:, t, 0:1], rstd[:, t:t + 1],
                                      ALU.subtract, ALU.mult).then_inc(xn_ready, 1)
            for n in range(2 * B):
                b, c = n // 2, n % 2
                dve.wait_ge(xh_ready, n + 1)
                dve.tensor_tensor(xl[:, c, b * S:(b + 1) * S], bank[n][:, :],
                                  xh[:, c, b * S:(b + 1) * S].bitcast(F32), ALU.subtract).then_inc(xl_ready, 1)
            dve.wait_ge(sem_const, 16 * 9)

            def rotate(t):
                i = t % TB
                dve.wait_ge(qk_ready, t + 1)
                if t:
                    dve.wait_ge(rope_ready, t)
                qk = bank[4 + t % 2][:, :].rearrange("p (h s e) -> p h s e", s=2, e=DH // 2)
                rb = rot_b[:, :].rearrange("p (h s e) -> p h s e", s=2, e=DH // 2)
                dve.tensor_tensor(rot_a[:, :].rearrange("p (h d) -> p h d", d=DH),
                                  bank[4 + t % 2][:, :].rearrange("p (h d) -> p h d", d=DH),
                                  spread(cos[:, i, :], 1, 2 * H), ALU.mult)
                dve.tensor_tensor(rb[:, :, 0, :], qk[:, :, 1, :], spread(sin[:, i, 0:DH // 2], 1, 2 * H), ALU.mult)
                dve.tensor_tensor(rb[:, :, 1, :], qk[:, :, 0, :], spread(sin[:, i, DH // 2:DH], 1, 2 * H),
                                  ALU.mult).then_inc(qk_read, 1)

            def key_means_and_rests(b):
                for k in range(4):
                    n = 4 * b + k
                    dve.wait_ge(qkT_ready, n + 1)
                    if n >= 4:
                        dve.wait_ge(gate_ready, 1)
                        dve.wait_ge(H_ready, n - 3)
                    dve.tensor_copy(X[:, k, :], bank[k][:, :]).then_inc(X_ready, 1)
                    dve.wait_ge(H_ready, n + 1)
                    if n >= 2:
                        dve.wait_ge(L_ready, n - 1)
                    dve.tensor_tensor(R1[:, n % 2, :], X[:, k, :], parts[:, n % 2, 0, :],
                                      ALU.subtract).then_inc(R1_ready, 1)
                    if k >= 2:
                        w = 2 * b + k - 2
                        link(dve.tensor_reduce(km[:, w, :], X[:, k, :].rearrange("p (n e) -> p n e", e=BLK),
                                               AX.X, ALU.add))
                        dve.scalar_tensor_tensor(out=kmb[:, w, :, :], in0=spread(km[:, w, :], 1, 8),
                                                 scalar=1.0 / BLK, in1=headmask[:, :, :], op0=ALU.mult,
                                                 op1=ALU.mult).then_inc(kmb_ready, 1)

            def gates_in(b):
                for i in range(1, TB):
                    dve.wait_ge(gate_ready, b + 1)
                    dve.wait_ge(init_done, 1)
                    if b:
                        dve.wait_ge(bias_ready, TB)
                    o = (i - 1) % 2 * H * NBLK
                    dve.tensor_tensor(gates[:, i - 1, :, 0:NBLK],
                                      bank[4 + (i - 1) // 2][:, o:o + H * NBLK].rearrange("p (h n) -> p h n", n=NBLK),
                                      spread(gate_add[:, i, :], 1, H), ALU.add).then_inc(gate_read, 1)

            def select(t):
                b, i = t // TB, t % TB
                if i == 0:
                    dve.tensor_copy(bias[:, t, :, :], spread(future[:, :], 1, H)).then_inc(bias_ready, 1)
                    return
                dve.wait_ge(gate_read, b * (TB - 1) + i)
                dve.wait_ge(bias_ready, t)
                for h in range(H):
                    ins = dve.max(top[:, h, :], gates[:, i - 1, h, :])
                link(ins)
                for h in range(H):
                    ins = dve.match_replace(picked[:, h, :], top[:, h, :], gates[:, i - 1, h, :], SENT)
                link(ins)
                dve.tensor_scalar(bias[:, t, :, :], picked[:, :, 0:NBLK], SENT_TEST, NEG, ALU.is_lt,
                                  ALU.mult).then_inc(bias_ready, 1)

            def router_in():
                dve.wait_ge(vg_read, T)
                link(dve.tensor_reduce(rm[:, 0, :], lg[:, :, :], AX.X, ALU.max))
                dve.tensor_tensor(rt[:, 0, :, :], lg[:, :, :], spread(rm[:, 0, :], 2, E), ALU.subtract).then_inc(e_in, 1)

            def router_out():
                dve.wait_ge(e_out, 1)
                dve.wait_ge(init_done, 1)
                link(dve.tensor_reduce(rm[:, 1, :], rt[:, 1, :, :], AX.X, ALU.add))
                link(dve.reciprocal(rm[:, 2, :], rm[:, 1, :]))
                link(dve.tensor_tensor(sc[:, :, 0:E], rt[:, 1, :, :], spread(rm[:, 2, :], 2, E), ALU.mult))
                for t in range(T):
                    ins = dve.max(rtop[:, t, :], sc[:, t, :])
                link(ins)
                for t in range(T):
                    ins = dve.match_replace(rpick[:, t, :], rtop[:, t, :], sc[:, t, :], SENT)
                link(ins)
                link(dve.scalar_tensor_tensor(out=rt[:, 2, :, :], in0=rpick[:, :, 0:E], scalar=SENT_TEST,
                                              in1=sc[:, :, 0:E], op0=ALU.is_ge, op1=ALU.mult))
                link(dve.tensor_copy(cs[:, :, 0:E], rt[:, 2, :, :]))
                link(dve.tensor_tensor(rt[:, 3, :, :], rt[:, 2, :, :], cs[:, :, 0:E], ALU.subtract))
                link(dve.tensor_copy(cs[:, :, E:2 * E], rt[:, 3, :, :]))
                dve.tensor_tensor(cs[:, :, 2 * E:3 * E], rt[:, 3, :, :], cs[:, :, E:2 * E],
                                  ALU.subtract).then_inc(comb_ready, 1)

            def head_maxima(k):
                b, g = k // (NG * LOADS), k // LOADS % NG
                i, heads = unit_loads(g)[k % LOADS]
                n = (i + 1) * P
                dve.wait_ge(A_ready, k + 1)
                dve.tensor_reduce(mx[:, b * TB + i, heads[0]:heads[-1] + 1],
                                  bank[k % 2][:, 0:len(heads) * n].rearrange("p (h n) -> p h n", n=n),
                                  AX.X, ALU.max).then_inc(A_read, 1)

            def maxima_parts(b):
                tb = slice(b * TB, (b + 1) * TB)
                dve.wait_ge(A_read, (b + 1) * NG * LOADS)
                link(dve.tensor_scalar(mr[:, 0, :, :], mx[:, tb, :], -1.0, None, ALU.mult))
                link(dve.tensor_copy(ms[:, tb, 0, :], mr[:, 0, :, :]))
                link(dve.tensor_tensor(mr[:, 1, :, :], mr[:, 0, :, :], ms[:, tb, 0, :], ALU.subtract))
                link(dve.tensor_copy(ms[:, tb, 1, :], mr[:, 1, :, :]))
                dve.tensor_tensor(ms[:, tb, 2, :], mr[:, 1, :, :], ms[:, tb, 1, :],
                                  ALU.subtract).then_inc(max_ready, 1)

            def out_rows(w):
                dve.wait_ge(PV_done, (w + 1) * TB)
                if w >= 1:
                    dve.wait_ge(oTT_ready, w)
                dve.tensor_copy(oT[:, :], bank[2][:, :]).then_inc(oT_ready, 1)

            def out_tokens(w):
                b, g = w // NG, w % NG
                dve.wait_ge(oTT_ready, w + 1)
                dve.tensor_copy(ob[:, b * TB:(b + 1) * TB, g * HG:(g + 1) * HG, :],
                                bank[5][:, :].rearrange("p (i h d) -> p i h d", i=TB, d=32)[:, :, :, 0:DH + 1]
                                ).then_inc(ob_ready, 1)

            def heads_of(w):
                b, g = w // NG, w % NG
                return slice(b * TB, (b + 1) * TB), slice(g * HG, (g + 1) * HG)

            def rms_sums(w):
                tb, hs = heads_of(w)
                o, l = ob[:, tb, hs, 0:DH], ob[:, tb, hs, DH]
                dve.wait_ge(ob_ready, w + 1)
                if w:
                    dve.wait_ge(on_ready, w)
                link(dve.tensor_tensor(sq, o, o, ALU.mult))
                link(dve.tensor_reduce(small[:, 0, :, :], sq, AX.X, ALU.add))
                link(dve.tensor_tensor(small[:, 1, :, :], l, l, ALU.mult))
                link(dve.scalar_tensor_tensor(out=small[:, 0, :, :], in0=small[:, 1, :, :], scalar=DH * RMS_EPS,
                                              in1=small[:, 0, :, :], op0=ALU.mult, op1=ALU.add))
                dve.tensor_scalar(small[:, 1, :, :], small[:, 0, :, :], 1.0 / DH, None, ALU.mult).then_inc(rms_in, 1)

            def rms_scale(w):
                tb, hs = heads_of(w)
                dve.wait_ge(rms_out, w + 1)
                link(dve.tensor_tensor(sq, ob[:, tb, hs, 0:DH], spread(small[:, 2, :, :], 3, DH), ALU.mult))
                dve.tensor_tensor(xn[:, tb, hs.start * DH:hs.stop * DH].rearrange("p t (h d) -> p t h d", d=DH), sq,
                                  onorm[:, :].unsqueeze(1).unsqueeze(1).broadcast_to([P, TB, HG, DH]),
                                  ALU.mult).then_inc(on_ready, 1)

            def slot(q):
                if q < A_SLOTS:
                    for k in (2 * q, 2 * q + 1):
                        head_maxima(k)
                for b in range(B):
                    if q + 1 == MAX_SLOTS[b]:
                        maxima_parts(b)
                if out_unit(q, 0) is not None:
                    out_rows(out_unit(q, 0))
                if out_unit(q, 1) is not None:
                    out_tokens(out_unit(q, 1))
                if out_unit(q, 3) is not None:
                    rms_sums(out_unit(q, 3))
                if out_unit(q, 5) is not None:
                    rms_scale(out_unit(q, 5))

            def take_y(n):
                dve.wait_ge(down_done, (n + 1) * CH)
                for k in range(2):
                    dve.tensor_copy(y[:, n * TB + 2 * k:n * TB + 2 * k + 2, :],
                                    bank[6 + k][:, :].rearrange("p (t d) -> p t d", d=D)).then_inc(y_read, 1)

            def silu_y(n):
                dve.wait_ge(yth_ready, n + 1)
                half = y[:, n * TB:(n + 1) * TB, :]
                link(dve.scalar_tensor_tensor(out=half, in0=yth[:, n * TB:(n + 1) * TB, :], scalar=1.0, in1=half,
                                              op0=ALU.add, op1=ALU.mult))

            for t in range(TB):
                rotate(t)
            key_means_and_rests(0)
            for t in range(TB, T):
                rotate(t)
            router_in()
            gates_in(0)
            for t in range(TB):
                select(t)
            key_means_and_rests(1)
            router_out()
            gates_in(1)
            select(TB)

            for s in range(STEPS):
                c = s % CH
                dve.wait_ge(th_ready, s + 1)
                if s >= 1:
                    dve.wait_ge(g_ready, s)
                dve.scalar_tensor_tensor(out=s2[:, :], in0=th[:, :], scalar=1.0, in1=bank[3][:, :],
                                         op0=ALU.add, op1=ALU.mult).then_inc(G_read, 1)
                slot(s * SLOTS)
                dve.wait_ge(U_ready, s + 1)
                dve.wait_ge(G_read, s + 1)
                if s >= 1:
                    dve.wait_ge(gh_ready, s)
                    dve.wait_ge(gl_ready, s)
                if c < ECH:
                    link(dve.scalar_tensor_tensor(out=uv[:, :], in0=s2[:, :], scalar=0.5, in1=bank[4][:, :],
                                                  op0=ALU.mult, op1=ALU.mult))
                    dve.tensor_tensor(gb[:, :], uv[:, :], bank[5][:, :], ALU.mult).then_inc(g_ready, 1)
                else:
                    dve.scalar_tensor_tensor(out=gb[:, :], in0=s2[:, :], scalar=0.5, in1=bank[4][:, :],
                                             op0=ALU.mult, op1=ALU.mult).then_inc(g_ready, 1)
                for q in range(s * SLOTS + 1, (s + 1) * SLOTS):
                    slot(q)
                if s < TB - 1:
                    select(TB + 1 + s)
                if s == CH:
                    take_y(0)
                if s == YTH_STEP + 1:
                    silu_y(0)
            take_y(1)
            rms_sums(B * NG - 1)
            rms_scale(B * NG - 1)
            for n in range(2 * B):
                dve.wait_ge(onh_ready, n + 1)
                part = (slice(None), n % 2, slice((n // 2) * S, (n // 2 + 1) * S))
                dve.tensor_tensor(xl[part], bank[n][:, :], xh[part].bitcast(F32), ALU.subtract).then_inc(onl_ready, 1)
            silu_y(1)
            for t in range(T):
                dve.wait_ge(s_ready, t + 1)
                link(dve.scalar_tensor_tensor(out=y[:, t, :], in0=y[:, t, :], scalar=0.5,
                                              in1=bank[4 + t % 2][:, 0:D], op0=ALU.mult, op1=ALU.mult))
                if t == 0:
                    dve.wait_ge(x_again, 16)
                    dve.wait_ge(onT_ready, 2 * B)
                dve.tensor_tensor(x1[:, t, :], xr[:, t, :], y[:, t, :], ALU.add).then_inc(x1_ready, 1)

        @block.tensor
        def _(pe):
            pe.wait_ge(cst["ident_in"], 16)
            for n in range(2 * B):
                b, c = n // 2, n % 2
                for i in range(TB):
                    pe.wait_ge(xn_ready, b * TB + i + 1)
                    ins = pe.transpose(bank[n][:, i * P:(i + 1) * P], xn[:, b * TB + i, c * P:(c + 1) * P], ident[:, :])
                ins.then_inc(xT_ready, 1)
            pe.wait_ge(wph_ready, 1)
            pe.wait_ge(wpl_ready, 1)

            def project(t):
                pe.wait_ge(xl_ready, 2 * (t // TB + 1))
                if t >= 2:
                    pe.wait_ge(qk_read, t - 1)
                    pe.wait_ge(vg_read, t - 1)
                for c in range(KD):
                    ins = split_matmul(pe, bank[4 + t % 2][:, :], xh[:, c, tokens(t)], xl[:, c, tokens(t)],
                                       wp_h[:, c, 0:512], wp_l[:, c, 0:512], c == 0, c == KD - 1)
                ins.then_inc(qk_ready, 1)
                for c in range(KD):
                    ins = split_matmul(pe, bank[6 + t % 2][:, 0:264], xh[:, c, tokens(t)], xl[:, c, tokens(t)],
                                       wp_h[:, c, 512:776], wp_l[:, c, 512:776], c == 0, c == KD - 1)
                ins.then_inc(vg_ready, 1)

            def transpose_qk(b):
                pe.wait_ge(rope_ready, (b + 1) * TB)
                pe.wait_ge(xl_ready, 2 * B)
                for k in range(4):
                    if b:
                        pe.wait_ge(X_ready, k + 1)
                    for i in range(TB):
                        ins = pe.transpose(bank[k][:, i * P:(i + 1) * P], qkr[:, i, k * P:(k + 1) * P], ident[:, :])
                    ins.then_inc(qkT_ready, 1)

            def block_gates(b):
                pe.wait_ge(kmb_ready, 2 * (b + 1))
                pe.wait_ge(qk_read, T)
                if b:
                    pe.wait_ge(gate_read, TB - 1)
                for i in range(1, TB):
                    for f in range(2):
                        o = (i - 1) % 2 * H * NBLK + f * P
                        ins = pe.matmul(bank[4 + (i - 1) // 2][:, o:o + P], X[:, f, i * P:(i + 1) * P],
                                        kmb[:, 2 * b + f, :, :], start=True, stop=True)
                ins.then_inc(gate_ready, 1)

            def transpose_bias(b):
                pe.wait_ge(bias_ready, (b + 1) * TB)
                pe.wait_ge(sem_const, 16 * 9)
                pe.wait_ge(vg_read, T)
                for f in range(2):
                    out = bank_b[2][:, f * 512:(f + 1) * 512] if b else bank_b[6 + f][:, 0:512]
                    for i in range(TB):
                        ins = pe.transpose(out[:, i * P:(i + 1) * P],
                                           bias[:, b * TB + i, f * 8:(f + 1) * 8, :], ident_b[:, :])
                    ins.then_inc(biasT_ready, 1)

            for t in range(TB):
                project(t)
            transpose_qk(0)
            for t in range(TB, T):
                project(t)
            block_gates(0)
            transpose_bias(0)
            transpose_qk(1)
            block_gates(1)
            pe.wait_ge(comb_ready, 1)
            pe.wait_ge(biasT_read, 2)
            for t in range(T):
                ins = pe.transpose(bank_b[6][0:64, t * P:(t + 1) * P], cs[:, t, :], ident_b[:, :])
            ins.then_inc(combT_ready, 1)
            pe.wait_ge(combT_read, 1)
            pe.wait_ge(X_ready, 8)
            pe.wait_ge(gate_read, B * (TB - 1))

            def scores_by_query(k):
                b, g, r = k // (NG * LOADS), k // LOADS % NG, k % LOADS
                if g == 0 and r == 0:
                    pe.wait_ge(q_stacked[b], 16 * (len(STACK) + 1))
                    pe.wait_ge(k_stacked[b], 16 * len(STACK))
                    pe.wait_ge(kconst_ready, 16)
                i, heads = unit_loads(g)[r]
                n = (i + 1) * P
                if k >= 2:
                    pe.wait_ge(A_read, k - 1)
                for o, h in enumerate(heads):
                    out = bank[k % 2][:, o * n:(o + 1) * n]
                    pe.matmul(out, QS[0:R_MAX, h, b * S + i * P:b * S + (i + 1) * P],
                              KS[0:R_MAX, h, b * S:b * S + n], start=True, stop=False)
                    ins = pe.matmul(out[:, n - P:n], ident_b[:, :], tri[:, 0, :], start=False, stop=True)
                ins.then_inc(A_ready, 1)

            def scores_by_key(k):
                b, g, j = unit_of(k // HG)
                h = HG * g + k % HG
                n = S - j * P
                if k % (HG * NG * TB) == 0:
                    pe.wait_ge(q_stacked[b], 16 * (len(STACK) + 2))
                if k == 0:
                    pe.wait_ge(A_read, B * NG * LOADS)
                if k >= 2:
                    pe.wait_ge(P_ready, k - 1)
                out = bank[k % 2]
                pe.matmul(out[:, 0:n], KS[0:R_ALL, h, b * S + j * P:b * S + (j + 1) * P],
                          QS[0:R_ALL, h, b * S + j * P:(b + 1) * S], start=True, stop=False)
                pe.matmul(out[:, 0:P], ident_b[:, :], tri[:, 1, :], start=False, stop=True).then_inc(B_ready, 1)

            def transpose_maxima(b):
                pe.wait_ge(max_ready, b + 1)
                pe.wait_ge(biasT_read, 4)
                for i in range(TB):
                    ins = pe.transpose(bank_b[2][0:48, i * P:(i + 1) * P],
                                       ms[:, b * TB + i, :, :].rearrange("p l h -> p (l h)"), ident_b[:, :])
                ins.then_inc(maxT_ready, 1)

            def values_sum(u):
                b, g, j = unit_of(u)
                q = u // TB
                pe.wait_ge(P_ready, HG * (u + 1))
                if j == 0 and q >= 1:
                    pe.wait_ge(oT_ready, q)
                if u == 0:
                    pe.wait_ge(maxT_read, B)
                for c in range(HG):
                    k = HG * u + c
                    ins = pe.matmul(bank[2][32 * c:32 * (c + 1), j * P:S], V[:, b * TB + j, HG * g + c, :],
                                    PT[:, k % 8, 0:S - j * P], start=(j == 0), stop=(j == TB - 1))
                ins.then_inc(PV_done, 1)

            def transpose_out(q):
                pe.wait_ge(oT_ready, q + 1)
                pe.wait_ge(g_ready, (B_SLOT + (q + 1) * UNIT_SLOTS) // SLOTS + 1)
                for i in range(TB):
                    ins = pe.transpose(bank[5][:, i * P:(i + 1) * P], oT[:, i * P:(i + 1) * P], ident[:, :])
                ins.then_inc(oTT_ready, 1)

            def gate_product(s):
                part = slice(s // CH * S, (s // CH + 1) * S)
                w = s % 3
                pe.wait_ge(wl_ready, s + 1)
                if s >= 1:
                    pe.wait_ge(G_read, s)
                for k in range(KD):
                    ins = split_matmul(pe, bank[3][:, :], wh[:, w, k, 0:P], wl[:, w, k, 0:P],
                                       xh[:, k, part], xl[:, k, part], k == 0, k == KD - 1)
                ins.then_inc(G_ready, 1)

            def up_product(s):
                n, c = s // CH, s % CH
                part = slice(n * S, (n + 1) * S)
                w = s % 3
                if s >= 1:
                    pe.wait_ge(g_ready, s)
                for k in range(KD):
                    ins = split_matmul(pe, bank[4][:, :], wh[:, w, k, P:2 * P], wl[:, w, k, P:2 * P],
                                       xh[:, k, part], xl[:, k, part], k == 0, k == KD - 1)
                if c < ECH:
                    if out_unit(s * SLOTS - 1, 1) is not None:
                        pe.wait_ge(ob_ready, out_unit(s * SLOTS - 1, 1) + 1)
                    ins = pe.matmul(bank[5][:, :], ksel[:, c, :], combT[:, part], start=True, stop=True)
                ins.then_inc(U_ready, 1)

            def down(s, k):
                c, w = s % CH, s % 3
                pe.wait_ge(gl_ready, s + 1)
                if c == 0 and s:
                    pe.wait_ge(y_read, 2)
                for o in range(2):
                    ins = split_matmul(pe, bank[6 + k][:, o * D:(o + 1) * D],
                                       gh[:, s % 2, tokens(2 * k + o)], gl[:, s % 2, tokens(2 * k + o)],
                                       wh[:, w, 2, :], wl[:, w, 2, :], c == 0 and o == 0, c == CH - 1, skip=True)
                if k:
                    ins.then_inc(down_done, 1)

            def slot(q):
                if q < A_SLOTS:
                    for k in (2 * q, 2 * q + 1):
                        scores_by_query(k)
                for b in range(B):
                    if q == MAX_SLOTS[b] + 1:
                        transpose_maxima(b)
                v = q - B_SLOT
                if 0 <= v < B_SLOTS:
                    for k in (2 * v, 2 * v + 1):
                        scores_by_key(k)
                if v > 0 and v * 2 % HG == 0 and v <= B_SLOTS:
                    values_sum(v * 2 // HG - 1)
                if out_unit(q, 1) is not None:
                    transpose_out(out_unit(q, 1))

            for s in range(STEPS):
                gate_product(s)
                slot(s * SLOTS)
                up_product(s)
                slot(s * SLOTS + 1)
                if s >= 1:
                    down(s - 1, 0)
                slot(s * SLOTS + 2)
                if s >= 1:
                    down(s - 1, 1)
                slot(s * SLOTS + 3)
                if s == BIAS_STEP:
                    transpose_bias(1)
            down(STEPS - 1, 0)
            down(STEPS - 1, 1)
            for n in range(2 * B):
                b, c = n // 2, n % 2
                pe.wait_ge(on_ready, (b + 1) * NG)
                for i in range(TB):
                    ins = pe.transpose(bank[n][:, i * P:(i + 1) * P], xn[:, b * TB + i, c * P:(c + 1) * P], ident[:, :])
                ins.then_inc(onT_ready, 1)
            pe.wait_ge(woh_ready, 1)
            pe.wait_ge(wol_ready, 1)
            for t in range(T):
                pe.wait_ge(onl_ready, 2 * (t // TB + 1))
                if t >= 2:
                    pe.wait_ge(x1_ready, t - 1)
                for c in range(KD):
                    ins = split_matmul(pe, bank[4 + t % 2][:, 0:D], xh[:, c, tokens(t)], xl[:, c, tokens(t)],
                                       wo_h[:, c, :], wo_l[:, c, :], c == 0, c == KD - 1)
                ins.then_inc(s_ready, 1)


def layer1(nc, a, x1, out, cst):
    ctx = ExitStack()
    with ctx:
        m = Mem(nc, ctx)
        ident = cst["ident"]
        w_lr = m.sb("w_lr", [P, KD, 2 * HP])
        w_lr_h = m.sb("w_lr_h", [P, KD, 2 * HP], F32R)
        w_lr_l = m.sb("w_lr_l", [P, KD, 2 * HP], F32R)
        w_ai = m.sb("w_ai", [P, HT, 2 * HP])
        w_ai_h = m.sb("w_ai_h", [P, HT, 2 * HP], F32R)
        w_ai_l = m.sb("w_ai_l", [P, HT, 2 * HP], F32R)
        w_o = m.sb("w_o", [P, HT, D])
        w_o_h = m.sb("w_o_h", [P, HT, D], F32R)
        w_o_l = m.sb("w_o_l", [P, HT, D], F32R)
        w_f = m.sb("w_f", [P, KD, FW])
        md = m.sb("md", [P, KD, 2 * N_SEL])
        w_g = m.sb("w_g", [OW, D])
        vec = m.sb("vec", [P, 10, HT])
        vec2 = m.sb("vec2", [P, 10, HT])
        sel_vec = m.sb("sel_vec", [P, 3, N_SEL])
        bo = m.sb("bo", [P, D])
        fmask = m.sb("fmask", [2 * N_SEL, FW])
        ones16 = m.sb("ones16", [2 * N_SEL, P])
        st = m.sb("st1", [P, T, 6])
        mv = m.sb("mv1", [P, T, 2])
        ve = m.sb("ve1", [P, T])
        mhalf = m.sb("mhalf1", [P, T])
        rstd = m.sb("rstd1", [P, T])
        xn = m.sb("xn1", [P, T, D])
        xsq = m.sb("xsq", [P, D])
        nsq = m.sb("nsq", [P, T])
        xh = m.sb("xh1", [P, KD, T * P], F32R)
        xl = m.sb("xl1", [P, KD, T * P], F32R)
        xT = m.sb("xT1", [P, KD, T * P])
        rin = m.sb("rin", [P, 2, TAPS - 1 + S])
        cv = m.sb("cv", [P, 2, S])
        u = m.sb("u", [P, HT, S])
        uh = m.sb("uh", [P, HT, S], F32R)
        ul = m.sb("ul", [P, HT, S], F32R)
        left = m.sb("left", [P, HT, S])
        ta = m.sb("ta", [P, HT, S])
        ti = m.sb("ti", [P, HT, S])
        dec = m.sb("dec", [P, HT, S])
        sqd = m.sb("sqd", [P, HT, S])
        drv = m.sb("drv", [P, HT, S])
        Y = m.sb("Y", [P, T, FW])
        fc = m.sb("fc", [2 * N_SEL, FW])
        fcm = m.sb("fcm", [2 * N_SEL, FW])
        fb = m.sb("fb", [P, FW])
        f1 = m.sb("f1", [P, T, N_SEL * S_SEL])
        z = m.sb("z", [P, 6, T, N_SEL])
        zm = m.sb("zm", [P, 3, T])
        ZO = m.sb("ZO", [P, T, OW])
        ZT = m.sb("ZT", [OW, T * P])
        ed = m.sb("ed", [P, T, D])
        o1 = m.sb("o1", [P, T, D])

        bank = [m.ps(f"lbank{i}") for i in range(8)]

        sems = {}

        def sem(name):
            if name not in sems:
                sems[name] = m.sem("l1_" + name)
            return sems[name]

        w_in = {n: m.sem("in_" + n) for n in ("lr", "ai", "o", "f", "vec", "selc")}
        var_ready, rstd_ready, xn_ready, nsq_ready = (sem(n) for n in ("var", "rstd", "xn", "nsq"))
        xT_ready, xh_ready, xl_ready = sem("xT"), sem("xh"), sem("xl")
        wh_ready, wl_ready = sem("wh"), sem("wl")
        R_ready, rin_ready, u_ready, uh_ready, ul_ready = (
            sem(n) for n in ("R", "rin", "u", "uh", "ul"))
        vec_ready, vec_exp, vec_dve, vec_ln, half_done = (sem(n) for n in ("vecr", "vexp", "vdve", "vln", "half"))
        A_ready, I_ready, ta_ready, ti_ready, dec_ready, sqd_ready, om_ready, beta_ready = (
            sem(n) for n in ("A", "I", "ta", "ti", "dec", "sqd", "om", "beta"))
        L_ready, left_ready, prod_ready, ph_ready, pl_ready, O_ready = (
            sem(n) for n in ("L", "left", "prod", "ph", "pl", "O"))
        F_ready, F_read, fc_ready, fcm_ready, fb_ready, fb_read = (
            sem(n) for n in ("F", "Fread", "fc", "fcm", "fb", "fbread"))
        z_ready, ez_ready, ZO_ready, ZT_ready, ZT_read, D_ready, ed_ready, eth_ready, out_ready = (
            sem(n) for n in ("z", "ez", "ZO", "ZT", "ZTread", "Dg", "ed", "eth", "out"))
        o_read = sem("o_read")
        dve_step, act_step, pool_step, stored = sem("dve_step"), sem("act_step"), sem("pool_step"), sem("stored")

        def tokens(t):
            return slice(t * P, (t + 1) * P)

        block = ctx.enter_context(nc.Block())

        @block.sync
        def _(sp):
            def load(dst, src, s):
                sp.dma_start(dst, src).then_inc(w_in[s], 16)
            load(w_lr[:, :, :], a["w_lr"].rearrange("(k p) n -> p k n", p=P), "lr")
            load(w_f[:, :, :], a["w_f"].rearrange("(k p) n -> p k n", p=P), "f")
            load(md[:, :, :], a["w_md"].rearrange("(k p) n -> p k n", p=P), "f")
            load(fmask[:, :], a["c_fmask"], "f")
            load(ones16[:, :], a["c_ones16"], "f")
            load(vec[:, :, :], a["vecs"], "vec")
            load(w_ai[:, :, :], a["w_ai"].rearrange("(k p) n -> p k n", p=P), "ai")
            load(w_o[:, :, :], a["w_o1"].rearrange("(k p) n -> p k n", p=P), "o")
            load(w_g[:, :], a["w_g"], "selc")
            load(sel_vec[:, 0, :], a["L1_ffn_imp_center"].unsqueeze(0).broadcast_to([P, N_SEL]), "selc")
            load(sel_vec[:, 1, :], a["L1_ffn_imp_slope"].unsqueeze(0).broadcast_to([P, N_SEL]), "selc")
            load(sel_vec[:, 2, :], a["c_rank"], "selc")
            load(bo[:, :], a["L1_attn_bo"].unsqueeze(0).broadcast_to([P, D]), "selc")
            dst = out.rearrange("(t p) d -> p t d", p=P)
            for t in range(T):
                sp.wait_ge(out_ready, t + 1)
                sp.dma_start(dst[:, t, :], ed[:, t, :]).then_inc(stored, 16)
            sp.wait_ge(stored, 16 * T)

        @block.gpsimd
        def _(pool):
            pool.memset(mhalf[:, :], -0.5).then_inc(half_done, 1)
            pool.memset(rin[:, :, 0:TAPS - 1], 0.0).then_inc(half_done, 1)
            pool.wait_ge(half_done, 1)
            for b in range(B):
                tb = slice(b * TB, (b + 1) * TB)
                pool.wait_ge(var_ready, b + 1)
                pool.tensor_tensor(rstd[:, tb], ve[:, tb], mhalf[:, tb], ALU.pow).then_inc(rstd_ready, 1)
            for k, (lo, raw, hi) in enumerate(((w_lr_l, w_lr, w_lr_h), (w_ai_l, w_ai, w_ai_h), (w_o_l, w_o, w_o_h))):
                pool.wait_ge(wh_ready, k + 1)
                pool.tensor_tensor(lo[:, :, :], raw[:, :, :], hi[:, :, :].bitcast(F32), ALU.subtract).then_inc(wl_ready, 1)
            for b in range(B):
                pool.wait_ge(uh_ready, b + 1)
                if b:
                    pool.wait_ge(O_ready, TB)
                pool.tensor_tensor(ul[:, :, :], u[:, :, :], uh[:, :, :].bitcast(F32), ALU.subtract).then_inc(ul_ready, 1)
                pool.wait_ge(ph_ready, b + 1)
                pool.wait_ge(I_ready, (b + 1) * HT)
                pool.tensor_tensor(ul[:, :, :], drv[:, :, :], uh[:, :, :].bitcast(F32), ALU.subtract).then_inc(pl_ready, 1)

        @block.scalar
        def _(act):
            link = chain(act, act_step)
            act.wait_ge(w_in["lr"], 16)
            act.copy(w_lr_h[:, :, :], w_lr[:, :, :]).then_inc(wh_ready, 1)
            act.wait_ge(vec_dve, 1)
            act.activation(vec2[:, 1, :], vec2[:, 0, :], ACT.Exp, scale=-1.0).then_inc(vec_exp, 1)
            act.wait_ge(vec_dve, 2)
            act.activation(vec2[:, 3, :], vec2[:, 2, :], ACT.Ln).then_inc(vec_ln, 1)
            for t in range(T):
                act.wait_ge(xn_ready, t + 1)
                if t:
                    act.wait_ge(nsq_ready, t)
                act.activation(xsq[:, :], xn[:, t, :], ACT.Square, accum_out=nsq[:, t:t + 1]).then_inc(nsq_ready, 1)
            for n in range(2 * B):
                b, c = n // 2, n % 2
                act.wait_ge(xT_ready, n + 1)
                act.copy(xh[:, c, b * S:(b + 1) * S], bank[n][:, :]).then_inc(xh_ready, 1)
            act.wait_ge(w_in["ai"], 16)
            act.copy(w_ai_h[:, :, :], w_ai[:, :, :]).then_inc(wh_ready, 1)
            act.wait_ge(w_in["o"], 16)
            act.copy(w_o_h[:, :, :], w_o[:, :, :]).then_inc(wh_ready, 1)
            act.wait_ge(half_done, 2)
            for b in range(B):
                for p in range(HT):
                    n = b * HT + p
                    act.wait_ge(R_ready, n + 1)
                    if n >= 2:
                        act.wait_ge(u_ready, n - 1)
                    act.activation(rin[:, n % 2, TAPS - 1:], bank[4 + n % 2][:, :], ACT.Identity,
                                   bias=vec[:, 1, p:p + 1]).then_inc(rin_ready, 1)
                act.wait_ge(u_ready, (b + 1) * HT)
                if b:
                    act.wait_ge(O_ready, TB)
                act.copy(uh[:, :, :], u[:, :, :]).then_inc(uh_ready, 1)
                act.wait_ge(vec_ready, 1)
                if b:
                    act.wait_ge(prod_ready, 1)
                for p in range(HT):
                    act.wait_ge(A_ready, b * HT + p + 1)
                    act.activation(ta[:, p, :], bank[0][:, :], ACT.Tanh, scale=0.5,
                                   bias=vec2[:, 4, p:p + 1]).then_inc(ta_ready, 1)
                    act.wait_ge(I_ready, b * HT + p + 1)
                    act.activation(ti[:, p, :], bank[1][:, :], ACT.Tanh, scale=0.5,
                                   bias=vec2[:, 5, p:p + 1]).then_inc(ti_ready, 1)
                    act.wait_ge(ta_ready, b * HT + p + 1)
                    act.activation(dec[:, p, :], ta[:, p, :], ACT.Exp, scale=vec2[:, 6, p:p + 1],
                                   bias=vec2[:, 6, p:p + 1]).then_inc(dec_ready, 1)
                    act.activation(sqd[:, p, :], ta[:, p, :], ACT.Exp, scale=vec2[:, 7, p:p + 1],
                                   bias=vec2[:, 7, p:p + 1]).then_inc(sqd_ready, 1)
                act.wait_ge(om_ready, b + 1)
                act.activation(sqd[:, :, :], sqd[:, :, :], ACT.Sqrt, scale=-1.0).then_inc(beta_ready, 1)
                for p in range(HT):
                    act.wait_ge(L_ready, b * HT + p + 1)
                    act.activation(left[:, p, :], bank[2 + (b * HT + p) % 2][:, :], ACT.Gelu_apprx_tanh,
                                   bias=vec[:, 0, p:p + 1]).then_inc(left_ready, 1)
                act.wait_ge(prod_ready, b + 1)
                act.wait_ge(I_ready, (b + 1) * HT)
                act.copy(uh[:, :, :], drv[:, :, :]).then_inc(ph_ready, 1)
            act.wait_ge(z_ready, 1)
            act.activation(z[:, 2, :, :], z[:, 1, :, :], ACT.Exp, scale=-1.0).then_inc(ez_ready, 1)
            for t in range(T):
                act.wait_ge(ZT_ready, t + 1)
                act.copy(ZT[:, tokens(t)], bank[6][0:OW, 0:P]).then_inc(ZT_read, 1)
            for t in range(T):
                act.wait_ge(ed_ready, t + 1)
                act.activation(xn[:, t, :], ed[:, t, :], ACT.Tanh, scale=0.5).then_inc(eth_ready, 1)

        @block.vector
        def _(dve):
            link = chain(dve, dve_step)
            for b in range(B):
                for t in range(b * TB, (b + 1) * TB):
                    ins = dve.bn_stats(st[:, t, :], x1[:, t, :])
                link(ins)
                for t in range(b * TB, (b + 1) * TB):
                    ins = dve.bn_aggr(mv[:, t, :], st[:, t, :])
                link(ins)
                tb = slice(b * TB, (b + 1) * TB)
                dve.tensor_scalar(ve[:, tb], mv[:, tb, 1], LN_EPS, None, ALU.add).then_inc(var_ready, 1)
            for b in range(B):
                dve.wait_ge(rstd_ready, b + 1)
                for t in range(b * TB, (b + 1) * TB):
                    dve.tensor_scalar(xn[:, t, :], x1[:, t, :], mv[:, t, 0:1], rstd[:, t:t + 1],
                                      ALU.subtract, ALU.mult).then_inc(xn_ready, 1)
            dve.wait_ge(w_in["vec"], 16)
            link(dve.tensor_scalar(vec2[:, 8, :], vec[:, 5, :], -1.0, None, ALU.mult))
            dve.tensor_tensor(vec2[:, 0, :], vec[:, 5, :], vec2[:, 8, :], ALU.max).then_inc(vec_dve, 1)
            dve.wait_ge(vec_exp, 1)
            dve.tensor_scalar(vec2[:, 2, :], vec2[:, 1, :], 1.0, None, ALU.add).then_inc(vec_dve, 1)
            dve.wait_ge(vec_dve, 2)
            link(dve.tensor_scalar(vec2[:, 6, :], vec2[:, 2, :], 1.0, None, ALU.subtract))
            link(dve.tensor_scalar(vec2[:, 7, :], vec2[:, 6, :], 0.0, None, ALU.is_equal))
            link(dve.tensor_tensor(vec2[:, 6, :], vec2[:, 6, :], vec2[:, 7, :], ALU.add))
            link(dve.reciprocal(vec2[:, 6, :], vec2[:, 6, :]))
            dve.wait_ge(vec_ln, 1)
            link(dve.tensor_tensor(vec2[:, 6, :], vec2[:, 6, :], vec2[:, 3, :], ALU.mult))
            link(dve.tensor_tensor(vec2[:, 6, :], vec2[:, 6, :], vec2[:, 7, :], ALU.add))
            link(dve.tensor_tensor(vec2[:, 6, :], vec2[:, 6, :], vec2[:, 1, :], ALU.mult))
            link(dve.scalar_tensor_tensor(out=vec2[:, 8, :], in0=vec2[:, 8, :], scalar=0.0, in1=vec2[:, 6, :],
                                          op0=ALU.max, op1=ALU.add))
            dve.tensor_scalar(vec2[:, 6, :], vec2[:, 8, :], -4.0, None, ALU.mult)
            dve.tensor_scalar(vec2[:, 7, :], vec2[:, 8, :], -8.0, None, ALU.mult)
            dve.tensor_scalar(vec2[:, 4:6, :], vec[:, 3:5, :], 0.5, None, ALU.mult).then_inc(vec_ready, 1)
            for n in range(2 * B):
                b, c = n // 2, n % 2
                part = (slice(None), c, slice(b * S, (b + 1) * S))
                dve.wait_ge(xh_ready, n + 1)
                dve.tensor_copy(xT[part], bank[n][:, :])
                dve.tensor_tensor(xl[part], bank[n][:, :], xh[part].bitcast(F32), ALU.subtract).then_inc(xl_ready, 1)

            def conv(b, p):
                n = b * HT + p
                dve.wait_ge(rin_ready, n + 1)
                if n:
                    dve.wait_ge(u_ready, n)
                if b and p == 0:
                    dve.wait_ge(ul_ready, 1)
                r = rin[:, n % 2, :]
                link(dve.tensor_scalar(cv[:, 0, :], r[:, 0:S], vec[:, 6, p:p + 1], vec[:, 2, p:p + 1],
                                       ALU.mult, ALU.add))
                link(dve.scalar_tensor_tensor(out=cv[:, 1, :], in0=r[:, 1:S + 1], scalar=vec[:, 7, p:p + 1],
                                              in1=cv[:, 0, :], op0=ALU.mult, op1=ALU.add))
                link(dve.scalar_tensor_tensor(out=cv[:, 0, :], in0=r[:, 2:S + 2], scalar=vec[:, 8, p:p + 1],
                                              in1=cv[:, 1, :], op0=ALU.mult, op1=ALU.add))
                dve.scalar_tensor_tensor(out=u[:, p, :], in0=r[:, 3:S + 3], scalar=vec[:, 9, p:p + 1],
                                         in1=cv[:, 0, :], op0=ALU.mult, op1=ALU.add).then_inc(u_ready, 1)

            def edit_in():
                dve.wait_ge(fc_ready, 1)
                dve.tensor_tensor(fcm[:, :], bank[6][0:2 * N_SEL, 0:FW], fmask[:, :], ALU.mult).then_inc(fcm_ready, 1)
                dve.wait_ge(fb_ready, 1)
                dve.tensor_copy(fb[:, :], bank[6][:, 0:FW]).then_inc(fb_read, 1)
                for t in range(T):
                    dve.wait_ge(F_ready, t + 1)
                    dve.tensor_copy(Y[:, t, :], bank[6 + t % 2][:, 0:FW]).then_inc(F_read, 1)
                dve.wait_ge(F_read, T)
                dve.wait_ge(fb_read, 1)
                dve.wait_ge(nsq_ready, T)
                NS = N_SEL * S_SEL
                link(dve.tensor_tensor(f1[:, :, :], Y[:, :, 0:NS], spread(fb[:, 0:NS], 1, T), ALU.subtract))
                link(dve.tensor_tensor(f1[:, :, :], f1[:, :, :], f1[:, :, :], ALU.mult))
                link(dve.tensor_reduce(z[:, 0, :, :].rearrange("p t n -> p (t n)"),
                                       f1[:, :, :].rearrange("p t (n s) -> p (t n) s", s=S_SEL), AX.X, ALU.add))
                link(dve.scalar_tensor_tensor(out=z[:, 1, :, :], in0=Y[:, :, 2 * NS:FW], scalar=-2.0,
                                              in1=spread(fb[:, 2 * NS:FW], 1, T), op0=ALU.mult, op1=ALU.add))
                link(dve.tensor_tensor(z[:, 1, :, :], z[:, 1, :, :], spread(nsq[:, :], 2, N_SEL), ALU.add))
                link(dve.reciprocal(z[:, 2, :, :], z[:, 1, :, :]))
                link(dve.tensor_tensor(z[:, 0, :, :], z[:, 0, :, :], z[:, 2, :, :], ALU.mult))
                dve.wait_ge(w_in["selc"], 16 * 5)
                link(dve.tensor_tensor(z[:, 0, :, :], z[:, 0, :, :], spread(sel_vec[:, 0, :], 1, T), ALU.subtract))
                link(dve.tensor_tensor(z[:, 1, :, :], z[:, 0, :, :], spread(sel_vec[:, 1, :], 1, T), ALU.mult))
                dve.tensor_scalar(z[:, 1, :, :], z[:, 1, :, :], -88.0, None, ALU.max).then_inc(z_ready, 1)

            def edit_select():
                NS = N_SEL * S_SEL
                dve.wait_ge(ez_ready, 1)
                link(dve.tensor_scalar(z[:, 3, :, :], z[:, 2, :, :], 1.0, None, ALU.add))
                link(dve.reciprocal(z[:, 0, :, :], z[:, 3, :, :]))
                link(dve.tensor_reduce(zm[:, 1, :], z[:, 0, :, :], AX.X, ALU.max))
                link(dve.tensor_tensor(z[:, 3, :, :], z[:, 0, :, :], spread(zm[:, 1, :], 2, N_SEL), ALU.is_equal))
                link(dve.tensor_tensor(z[:, 4, :, :], z[:, 3, :, :], spread(sel_vec[:, 2, :], 1, T), ALU.mult))
                link(dve.tensor_reduce(zm[:, 2, :], z[:, 4, :, :], AX.X, ALU.max))
                link(dve.tensor_tensor(ZO[:, :, NS:OW], z[:, 4, :, :], spread(zm[:, 2, :], 2, N_SEL), ALU.is_equal))
                link(dve.tensor_tensor(f1[:, :, :], Y[:, :, NS:2 * NS], spread(fb[:, NS:2 * NS], 1, T), ALU.subtract))
                for t in range(T):
                    ins = dve.tensor_tensor(ZO[:, t, 0:NS].rearrange("p (n h) -> p n h", h=H_SEL),
                                            f1[:, t, :].rearrange("p (n h) -> p n h", h=H_SEL),
                                            spread(ZO[:, t, NS:OW], 2, H_SEL), ALU.mult)
                ins.then_inc(ZO_ready, 1)

            for p in range(HT):
                conv(0, p)
            edit_in()
            for b in range(B):
                if b:
                    for p in range(HT):
                        conv(1, p)
                dve.wait_ge(sqd_ready, (b + 1) * HT)
                dve.tensor_scalar(sqd[:, :, :], sqd[:, :, :], 1.0, -1e-12, ALU.subtract, ALU.min).then_inc(om_ready, 1)
                dve.wait_ge(ti_ready, (b + 1) * HT)
                if b:
                    dve.wait_ge(pl_ready, 1)
                link(dve.scalar_tensor_tensor(out=ti[:, :, :], in0=ti[:, :, :], scalar=1.0, in1=u[:, :, :],
                                              op0=ALU.add, op1=ALU.mult))
                dve.wait_ge(beta_ready, b + 1)
                link(dve.scalar_tensor_tensor(out=drv[:, :, :], in0=ti[:, :, :], scalar=0.5, in1=sqd[:, :, :],
                                              op0=ALU.mult, op1=ALU.mult))
                dve.wait_ge(dec_ready, (b + 1) * HT)
                for p in range(HT):
                    ins = dve.tensor_tensor_scan(ti[:, p, :], dec[:, p, :], drv[:, p, :], 0.0, ALU.mult, ALU.add)
                link(ins)
                dve.wait_ge(left_ready, (b + 1) * HT)
                dve.tensor_tensor(drv[:, :, :], ti[:, :, :], left[:, :, :], ALU.mult).then_inc(prod_ready, 1)
                for t in range(b * TB, (b + 1) * TB):
                    dve.wait_ge(O_ready, t + 1)
                    dve.tensor_tensor(o1[:, t, :], bank[6 + t % 2][:, 0:D], bo[:, :], ALU.add).then_inc(o_read, 1)
            dve.wait_ge(o_read, T)
            edit_select()
            for t in range(T):
                dve.wait_ge(D_ready, t + 1)
                link(dve.tensor_tensor(ed[:, t, :], bank[4 + t % 2][:, 0:D], xn[:, t, :], ALU.subtract))
                dve.scalar_tensor_tensor(out=ed[:, t, :], in0=ed[:, t, :], scalar=zm[:, 1, t:t + 1],
                                         in1=xn[:, t, :], op0=ALU.mult, op1=ALU.add).then_inc(ed_ready, 1)
            for t in range(T):
                dve.wait_ge(eth_ready, t + 1)
                link(dve.scalar_tensor_tensor(out=ed[:, t, :], in0=xn[:, t, :], scalar=1.0, in1=ed[:, t, :],
                                              op0=ALU.add, op1=ALU.mult))
                link(dve.scalar_tensor_tensor(out=xn[:, t, :], in0=o1[:, t, :], scalar=0.5, in1=ed[:, t, :],
                                              op0=ALU.mult, op1=ALU.mult))
                dve.tensor_tensor(ed[:, t, :], xn[:, t, :], x1[:, t, :], ALU.add).then_inc(out_ready, 1)

        @block.tensor
        def _(pe):
            for n in range(2 * B):
                b, c = n // 2, n % 2
                for i in range(TB):
                    pe.wait_ge(xn_ready, b * TB + i + 1)
                    ins = pe.transpose(bank[n][:, i * P:(i + 1) * P], xn[:, b * TB + i, c * P:(c + 1) * P], ident[:, :])
                ins.then_inc(xT_ready, 1)

            def right_in(b):
                pe.wait_ge(wl_ready, 1)
                pe.wait_ge(xl_ready, 2 * (b + 1))
                for p in range(HT):
                    n = b * HT + p
                    if n >= 2:
                        pe.wait_ge(rin_ready, n - 1)
                    for k in range(KD):
                        w = slice(HP + p * P, HP + (p + 1) * P)
                        ins = split_matmul(pe, bank[4 + n % 2][:, :], w_lr_h[:, k, w], w_lr_l[:, k, w],
                                           xh[:, k, b * S:(b + 1) * S], xl[:, k, b * S:(b + 1) * S],
                                           k == 0, k == KD - 1)
                    ins.then_inc(R_ready, 1)

            def left_in(b):
                for p in range(HT):
                    n = b * HT + p
                    if n >= 2:
                        pe.wait_ge(left_ready, n - 1)
                    w = slice(p * P, (p + 1) * P)
                    for k in range(KD):
                        ins = split_matmul(pe, bank[2 + n % 2][:, :], w_lr_h[:, k, w], w_lr_l[:, k, w],
                                           xh[:, k, b * S:(b + 1) * S], xl[:, k, b * S:(b + 1) * S],
                                           k == 0, k == KD - 1)
                    ins.then_inc(L_ready, 1)

            def gates(b):
                pe.wait_ge(wl_ready, 2)
                pe.wait_ge(ul_ready, b + 1)
                for p in range(HT):
                    n = b * HT + p
                    if n:
                        pe.wait_ge(ta_ready, n)
                    for g, done in ((0, A_ready), (1, I_ready)):
                        if g and n:
                            pe.wait_ge(ti_ready, n)
                        w = slice(g * HP + p * P, g * HP + (p + 1) * P)
                        for k in range(HT):
                            ins = split_matmul(pe, bank[g][:, :], w_ai_h[:, k, w], w_ai_l[:, k, w],
                                               uh[:, k, :], ul[:, k, :], k == 0, k == HT - 1)
                        ins.then_inc(done, 1)

            def mix_out(b):
                pe.wait_ge(wl_ready, 3)
                pe.wait_ge(pl_ready, b + 1)
                for i in range(TB):
                    t = b * TB + i
                    if t >= 2:
                        pe.wait_ge(o_read, t - 1)
                    if t == 0:
                        pe.wait_ge(F_read, T)
                    for k in range(HT):
                        ins = split_matmul(pe, bank[6 + t % 2][:, 0:D],
                                           uh[:, k, tokens(i)], ul[:, k, tokens(i)], w_o_h[:, k, :], w_o_l[:, k, :],
                                           k == 0, k == HT - 1)
                    ins.then_inc(O_ready, 1)

            def edit_products():
                pe.wait_ge(w_in["f"], 64)
                for k in range(KD):
                    ins = pe.matmul(bank[6][0:2 * N_SEL, 0:FW], md[:, k, :], w_f[:, k, :],
                                    start=(k == 0), stop=(k == KD - 1))
                ins.then_inc(fc_ready, 1)
                pe.wait_ge(fcm_ready, 1)
                pe.matmul(bank[6][:, 0:FW], ones16[:, :], fcm[:, :], start=True, stop=True).then_inc(fb_ready, 1)
                pe.wait_ge(fb_read, 1)
                for t in range(T):
                    if t >= 2:
                        pe.wait_ge(F_read, t - 1)
                    for k in range(KD):
                        ins = pe.matmul(bank[6 + t % 2][:, 0:FW], xT[:, k, tokens(t)], w_f[:, k, :],
                                        start=(k == 0), stop=(k == KD - 1))
                    ins.then_inc(F_ready, 1)

            right_in(0)
            pe.wait_ge(xl_ready, 2 * B)
            edit_products()
            gates(0)
            left_in(0)
            right_in(1)
            mix_out(0)
            gates(1)
            left_in(1)
            mix_out(1)
            pe.wait_ge(ZO_ready, 1)
            pe.wait_ge(o_read, T)
            for t in range(T):
                if t:
                    pe.wait_ge(ZT_read, t)
                pe.transpose(bank[6][0:OW, 0:P], ZO[:, t, :], ident[:, :]).then_inc(ZT_ready, 1)
            pe.wait_ge(w_in["selc"], 16 * 5)
            pe.wait_ge(ZT_read, T)
            for t in range(T):
                if t >= 2:
                    pe.wait_ge(ed_ready, t - 1)
                pe.matmul(bank[4 + t % 2][:, 0:D], ZT[:, tokens(t)], w_g[:, :], start=True, stop=True).then_inc(D_ready, 1)


_OUTS = [((2, 512, 256), 'float32')]


def _constants():
    f, bf = np.float32, np.dtype("bfloat16")
    pos = np.arange(S, dtype=f)
    inv = (1.0 / 10000.0 ** (np.arange(0, DH, 2).astype(f) / f(DH))).astype(f)
    ang = (pos[:, None] * inv).astype(f)
    cos, sin = np.cos(ang).astype(f), np.sin(ang).astype(f)
    tok = np.arange(P)

    def by_tile(v):
        return np.ascontiguousarray(v.reshape(TB, P, -1).transpose(1, 0, 2))
    own = np.arange(S)[:, None] // BLK
    blk = np.arange(NBLK)[None, :]
    gate_add = np.where(blk > own, f(NEG), np.where(blk == own, f(-NEG), f(0))).astype(f)
    later = (tok[None, :] > tok[:, None])
    ksel = np.zeros((64, ECH, P), f)
    unit = np.arange(ECH * P).reshape(ECH, P)
    for level in range(3):
        for e in range(E):
            ksel[level * E + e] = (unit // EH == e)
    kconst = np.ones((R_ALL - R_BIAS, T * P), f)
    kconst[:NBLK] = (np.arange(T * P)[None, :] % S // BLK) == np.arange(NBLK)[:, None]
    fmask = np.zeros((2 * N_SEL, FW), f)
    for n in range(N_SEL):
        fmask[n, n * S_SEL:(n + 1) * S_SEL] = 1
        fmask[N_SEL + n, N_SEL * S_SEL + n * H_SEL:N_SEL * S_SEL + (n + 1) * H_SEL] = 1
        fmask[n, 2 * N_SEL * S_SEL + n] = 1
    return {
        "c_ident": np.eye(P, dtype=f),
        "c_cos": by_tile(np.concatenate([cos, cos], 1)),
        "c_sin": by_tile(np.concatenate([-sin, sin], 1)),
        "c_gate_add": by_tile(gate_add),
        "c_future": np.where(blk > tok[:, None] // BLK, f(NEG), f(0)).astype(f),
        "c_headmask": np.repeat((tok[:, None] // DH == np.arange(8)[None, :]).astype(f)[:, :, None], NBLK, 2),
        "c_tri": np.stack([np.where(later, f(NEG), f(0)), np.where(later.T, f(NEG), f(0))], 1).astype(bf),
        "c_ksel": ksel.astype(bf),
        "c_kconst": kconst.astype(bf),
        "c_ident_b": np.eye(P, dtype=f).astype(bf),
        "c_fmask": fmask,
        "c_ones16": np.ones((2 * N_SEL, P), f),
        "c_rank": np.tile(np.arange(N_SEL, 0, -1, dtype=f), (P, 1)),
    }


def _layout(v):
    def pad(w, rows, cols):
        return np.pad(w, ((0, rows - w.shape[0]), (0, cols - w.shape[1])))

    def wide(w):
        return w.transpose(1, 0, 2).reshape(D, E * EH)
    gate = np.concatenate([wide(v["L0_ffn_w_gate"]), pad(v["L0_ffn_sw_gate"], D, SCH * P)], 1)
    up = np.concatenate([wide(v["L0_ffn_w_up"]), pad(v["L0_ffn_sw_up"], D, SCH * P)], 1)
    down = np.concatenate([v["L0_ffn_w_down"].reshape(E * EH, D), pad(v["L0_ffn_sw_down"], SCH * P, D)], 0)
    chunks = np.empty((CH, P, 3, 2 * P), np.float32)
    for w, o in ((gate, 0), (up, P)):
        chunks[:, :, 0:KD, o:o + P] = w.reshape(KD, P, CH, P).transpose(2, 1, 0, 3)
    chunks[:, :, 2, :] = down.reshape(CH, P, D)
    vecs = [v["L1_attn_" + n] for n in ("bl", "br", "conv_b", "ba", "bi", "lam")] + list(v["L1_attn_conv_w"][:, 0])
    vecs = np.stack([np.pad(w, (0, HP - HID)).reshape(HT, P) for w in vecs])

    def side(w):
        return w.transpose(1, 0, 2).reshape(D, -1)
    return {
        "x": v["L0_attn_hidden_states"].reshape(B * S, D),
        "w_proj": np.concatenate([v["L0_attn_Wq"].T, v["L0_attn_Wk"].T, v["L0_attn_Wv"].T, v["L0_ffn_gate_w"]], 1),
        "w_o": v["L0_attn_Wo"].T,
        "w_chunks": chunks,
        "w_lr": np.concatenate([pad(v["L1_attn_Wl"], D, HP), pad(v["L1_attn_Wr"], D, HP)], 1),
        "w_ai": np.concatenate([pad(v["L1_attn_Wa"], HP, HP), pad(v["L1_attn_Wi"], HP, HP)], 1),
        "w_o1": pad(v["L1_attn_Wo"], HP, D),
        "w_f": np.concatenate([side(v["L1_ffn_select_weight"]), side(v["L1_ffn_lora_update"]),
                               v["L1_ffn_select_mean_diff"].T], 1),
        "w_md": np.concatenate([v["L1_ffn_select_mean_diff"].T, v["L1_ffn_debias_w"].T], 1),
        "w_g": np.concatenate([v["L1_ffn_lora_degen"].transpose(0, 2, 1).reshape(N_SEL * H_SEL, D),
                               v["L1_ffn_bias_w"]], 0),
        "vecs": vecs.transpose(2, 0, 1),
        "L0_attn_o_norm_w": v["L0_attn_o_norm_w"],
        "L1_ffn_imp_center": v["L1_ffn_imp_center"],
        "L1_ffn_imp_slope": v["L1_ffn_imp_slope"],
        "L1_attn_bo": v["L1_attn_bo"],
    }


def program(nc, a, out):
    with ExitStack() as ctx:
        m = Mem(nc, ctx)
        x1 = m.sb("x1", [P, T, D])
        cst = {"ident": m.sb("ident", [P, P]), "ident_b": m.sb("ident_b", [P, P], BF16),
               "ident_in": m.sem("ident_in")}
        layer0(nc, a, x1, cst)
        layer1(nc, a, x1, out, cst)


def kernel(**inputs):
    import numpy as _np
    import concourse.bacc as _bacc
    from concourse import mybir as _mybir
    from concourse.bass_utils import run_bass_kernel_spmd as _run

    nc = _bacc.Bacc("TRN2", target_bir_lowering=False, num_devices=1)
    data = _layout({k: _np.asarray(v) for k, v in inputs.items()})
    data.update(_constants())
    arrays, args = {}, {}
    for name, v in data.items():
        v = _np.ascontiguousarray(v)
        arrays[f"in_{name}_dram"] = v
        args[name] = nc.dram_tensor(f"in_{name}_dram", v.shape, _mybir.dt.from_np(v.dtype), kind="ExternalInput").ap()
    (shape, dtype), = _OUTS
    out = nc.dram_tensor("out_0_dram", shape, _mybir.dt.from_np(_np.dtype(dtype)), kind="ExternalOutput").ap()
    program(nc, args, out.rearrange("b s d -> (b s) d"))
    r = _run(nc, [arrays], core_ids=[0])
    return r.results[0]["out_0_dram"]
```

```python
from contextlib import ExitStack

import numpy as np

import concourse.bass as bass
from concourse import mybir

ALU = mybir.AluOpType
ACT = mybir.ActivationFunctionType
AX = mybir.AxisListType
F32 = mybir.dt.float32
F32R = mybir.dt.float32r
BF16 = mybir.dt.bfloat16

P = 128
B, S, D = 2, 512, 256
T = B * S // P
TB = S // P
KD = D // P
LN_EPS = 1e-5
NEG = -1e30

H, DH, BLK, TOPK = 16, 16, 32, 4
NBLK = S // BLK
GATE_ROW = NBLK + TOPK
HG = 4
NG = H // HG
RMS_EPS = 1e-6
E, EK, EH, SH = 8, 2, 176, 352
ECH = E * EH // P
SCH = -(-SH // P)
CH = ECH + SCH
EROW = E + 8 - EK
HALVES = 2
STEPS = HALVES * CH
SENT, SENT_TEST = 3e38, 1e38
STACK = [(0, 0), (0, 1), (1, 0), (1, 1), (0, 2), (2, 0)]
R_BIAS = len(STACK) * DH
R_MAX = R_BIAS + NBLK
R_ALL = R_MAX + 3
SLOTS = 4

HID = 320
HT = -(-HID // P)
HP = HT * P
TAPS = 4
N_SEL, S_SEL, H_SEL = 8, 8, 8
FW = N_SEL * S_SEL + N_SEL * H_SEL + N_SEL
OW = N_SEL * H_SEL + N_SEL


def unit_loads(g):
    heads = list(range(HG * g, HG * g + HG))
    loads = [(0, heads), (1, heads[:2]), (1, heads[2:])]
    loads += [(i, [h]) for i in (2, 3) for h in heads]
    return loads


LOADS = len(unit_loads(0))


def exp_loads(g):
    heads = list(range(HG * g, HG * g + HG))
    loads = [(j, [h]) for j in (0, 1) for h in heads]
    return loads + [(2, heads[:2]), (2, heads[2:]), (3, heads)]


LAST_LOAD = [max(r for r, (j, _) in enumerate(exp_loads(0)) if j == tile) for tile in range(TB)]

PREP_SLOT = [0, 12]
GATE_SLOT = [6, 18]
SELECT_SLOTS = [range(6, 12), range(20, 32, 2)]
BIAS_SLOT = [14, 34]
A_SLOT = 20
PASS_SLOTS = B * NG * LOADS // 2
MAX_SLOTS = [A_SLOT + PASS_SLOTS // B, A_SLOT + PASS_SLOTS]
B_SLOT = A_SLOT + PASS_SLOTS
SUM_SLOT = [[B_SLOT + (w * LOADS + r) // 2 + 1 for r in LAST_LOAD] for w in range(B * NG)]
OUT_SLOT = [next(q for q in range(v[-1] + 1, v[-1] + 4) if q % SLOTS >= 2) for v in SUM_SLOT]
SLOT_END = OUT_SLOT[-1] + 1
WO_STEP = 6
DVE_STEP = B_SLOT // SLOTS
YTH_STEP = (B_SLOT + PASS_SLOTS // 2) // SLOTS + 2


def pool_weighs(s):
    return A_SLOT // SLOTS <= s < DVE_STEP and s % CH < ECH


def out_unit(q, lag):
    return OUT_SLOT.index(q - lag) if q - lag in OUT_SLOT else None


def spread(ap, axis, n):
    v = ap.unsqueeze(axis)
    shape = list(v.shape)
    shape[axis] = n
    return v.broadcast_to(shape)


class Mem:
    def __init__(self, nc, ctx):
        self.nc, self.ctx = nc, ctx

    def sb(self, name, shape, dt=F32):
        return self.ctx.enter_context(self.nc.sbuf_tensor(name, shape, dt))

    def ps(self, name, dt=F32):
        return self.ctx.enter_context(self.nc.psum_tensor(name, [P, 2048 // (4 if dt == F32 else 2)], dt))

    def sem(self, name):
        return self.ctx.enter_context(self.nc.semaphore(name))


def chain(eng, sem):
    done = [0]

    def link(ins):
        done[0] += 1
        ins.then_inc(sem, 1)
        eng.wait_ge(sem, done[0])
    return link


def split_matmul(pe, out, l_hi, l_lo, r_hi, r_lo, start, stop, skip=False):
    pe.matmul(out, l_hi, r_hi, start=start, stop=False, skip_group_check=skip)
    pe.matmul(out, l_hi, r_lo, start=False, stop=False, skip_group_check=skip)
    return pe.matmul(out, l_lo, r_hi, start=False, stop=stop, skip_group_check=skip)


def layer0(nc, a, x1, cst):
    ctx = ExitStack()
    with ctx:
        m = Mem(nc, ctx)
        ident, ident_b = cst["ident"], cst["ident_b"]
        tri = m.sb("tri", [P, 2, P], BF16)
        ksel = m.sb("ksel", [64, ECH, P], BF16)
        onorm = m.sb("onorm", [P, DH])
        mhalf = m.sb("mhalf", [P, P])
        x = xn = x1
        xh = m.sb("xh", [P, KD, T * P], F32R)
        xl = m.sb("xl", [P, KD, T * P], F32R)
        bias = m.sb("bias", [P, T, H, NBLK], BF16)
        biasT = m.sb("biasT", [P, 2, 512], BF16)
        QS = m.sb("QS", [P, H, T * P], BF16)
        KS = m.sb("KS", [P, H, T * P], BF16)
        V = m.sb("V", [P, T, H, 32])
        mx = m.sb("mx", [P, T, H])
        mr = m.sb("mr", [P, 2, TB, H])
        ms = m.sb("ms", [P, T, 3, H], BF16)
        lg = m.sb("lg", [P, T, E])
        rt = m.sb("rt", [P, 4, T, E])
        rm = m.sb("rm", [P, 3, T])
        sc = m.sb("sc", [P, T, EROW])
        cs = m.sb("cs", [P, T, 64], BF16)
        combT = m.sb("combT", [64, T * P], BF16)
        wr = m.sb("wr", [P, 2, 3, 256])
        wh = m.sb("wh", [P, 3, 3, 256], F32R)
        wl = m.sb("wl", [P, 3, 3, 256], F32R)
        gates = m.sb("gates", [P, TB - 1, H, GATE_ROW])
        top = m.sb("top", [P, H, 8])
        picked = m.sb("picked", [P, H, GATE_ROW])

        early_ctx = ExitStack()
        early = Mem(nc, early_ctx)
        wp_h = early.sb("wp_h", [P, KD, 776], F32R)
        wp_l = early.sb("wp_l", [P, KD, 776], F32R)
        rot_b = early.sb("rot_b", [P, 2, 512])
        rot_a = early.sb("rot_a", [P, 2, 512])
        wp = early.sb("wp", [P, KD, 776])
        qkr = early.sb("qkr", [P, T, 512])
        X = early.sb("X", [P, 4, 512])
        R1 = rot_a
        parts_in = [w.rearrange("p k n -> p (k n)")[:, 0:1536].bitcast(BF16).rearrange("p (i l t) -> p i l t", i=2, l=3)
                    for w in (wp[:, :, :], x1[:, :, :])]
        parts = [parts_in[i // 2][:, i % 2] for i in range(4)]
        km = early.sb("km", [P, 4, NBLK])
        kmb = early.sb("kmb", [P, 4, 8, NBLK])
        cos = early.sb("cos", [P, TB, DH])
        sin = early.sb("sin", [P, TB, DH])
        gate_add = early.sb("gate_add", [P, TB, NBLK])
        future = early.sb("future", [P, NBLK])
        headmask = early.sb("headmask", [P, 8, NBLK])
        st = early.sb("st", [P, T, 6])
        mv = early.sb("mv", [P, T, 2])
        ve = early.sb("ve", [P, T])
        rstd = early.sb("rstd", [P, T])
        rpick = early.sb("rpick", [P, T, EROW])
        rtop = early.sb("rtop", [P, T, 8])
        early_ctx.close()
        th = m.sb("th", [P, 512])
        s2 = m.sb("s2", [P, 512])
        uv = m.sb("uv", [P, 512])
        gb = m.sb("gb", [P, 512])
        gh = m.sb("gh", [P, 2, 512], F32R)
        gl = m.sb("gl", [P, 2, 512], F32R)
        PT = m.sb("PT", [P, 8, 512])
        oT = m.sb("oT", [P, 512])
        y = m.sb("y", [P, T, D])
        ob = m.sb("ob", [P, T, H, DH + 1])
        small = m.sb("small", [P, 3, TB, HG])
        msT = m.sb("msT", [48, 2, 512], BF16)
        wo = PT[:, 0, :].rearrange("p (k n) -> p k n", n=D)
        wo_h = m.sb("wo_h", [P, KD, D], F32R)
        wo_l = m.sb("wo_l", [P, KD, D], F32R)

        bank = [m.ps(f"bank{i}") for i in range(8)]
        bank_b = [bank[i][:, :].bitcast(BF16) for i in range(8)]

        parts_dram = nc.dram_tensor("parts_dram", (B, 2, 3, D, S), BF16, kind="Internal").ap()
        bias_dram = nc.dram_tensor("bias_dram", (B, D, S), BF16, kind="Internal").ap()
        max_dram = nc.dram_tensor("max_dram", (B, 3 * H, S), BF16, kind="Internal").ap()

        x_in = [m.sem(f"x_in{b}") for b in range(B)]
        sem_wp, sem_wo, sem_const, x_again = (m.sem(n) for n in ("wp_in", "wo_in", "const_in", "x_again"))
        init_done = m.sem("init_done")
        half_done = m.sem("half_done")
        var_ready, rstd_ready, xn_ready = m.sem("var_ready"), m.sem("rstd_ready"), m.sem("xn_ready")
        xT_ready, xh_ready, xl_ready = m.sem("xT_ready"), m.sem("xh_ready"), m.sem("xl_ready")
        wph_ready, wpl_ready, woh_ready, wol_ready = (m.sem(n) for n in ("wph", "wpl", "woh", "wol"))
        qk_ready, vg_ready, qk_read, vg_read = (m.sem(n) for n in ("qk_ready", "vg_ready", "qk_read", "vg_read"))
        rope_ready = m.sem("rope_ready")
        qkT_ready, X_ready, H_ready, R1_ready, M_ready, L_ready = (
            m.sem(n) for n in ("qkT_ready", "X_ready", "H_ready", "R1_ready", "M_ready", "L_ready"))
        parts_out = [m.sem(f"parts_out{i}") for i in range(4)]
        q_stacked = [m.sem(f"q_stacked{b}") for b in range(B)]
        k_stacked = [m.sem(f"k_stacked{b}") for b in range(B)]
        kconst_ready = m.sem("kconst_ready")
        kmb_ready, gate_ready, gate_read, bias_ready = (
            m.sem(n) for n in ("kmb_ready", "gate_ready", "gate_read", "bias_ready"))
        biasT_ready, biasT_read, bias_out = m.sem("biasT_ready"), m.sem("biasT_read"), m.sem("bias_out")
        e_in, e_out, comb_ready, combT_ready, combT_read = (
            m.sem(n) for n in ("e_in", "e_out", "comb_ready", "combT_ready", "combT_read"))
        w_in = [m.sem("w_in0"), m.sem("w_in1")]
        wh_ready, wl_ready = m.sem("wh_ready"), m.sem("wl_ready")
        G_ready, U_ready, th_ready, G_read, g_ready, gh_ready, gl_ready, down_done = (
            m.sem(n) for n in ("G_ready", "U_ready", "th_ready", "G_read", "g_ready", "gh_ready", "gl_ready",
                               "down_done"))
        uv_ready, weights_read = m.sem("uv_ready"), m.sem("weights_read")
        y_read = m.sem("y_read")
        A_ready, A_read, max_ready, maxT_ready, maxT_read, max_out = (
            m.sem(n) for n in ("A_ready", "A_read", "max_ready", "maxT_ready", "maxT_read", "max_out"))
        B_ready, P_ready, PV_done, oT_ready, oTT_ready, ob_ready = (
            m.sem(n) for n in ("B_ready", "P_ready", "PV_done", "oT_ready", "oTT_ready", "ob_ready"))
        rms_in, rms_out, on_ready, onT_ready, onh_ready, onl_ready = (
            m.sem(n) for n in ("rms_in", "rms_out", "on_ready", "onT_ready", "onh_ready", "onl_ready"))
        yth_ready, s_ready, gated_ready = m.sem("yth_ready"), m.sem("s_ready"), m.sem("gated_ready")
        dve_step, act_step, pool_step = m.sem("dve_step"), m.sem("act_step"), m.sem("pool_step")

        def tokens(t, n=1):
            return slice(t * P, (t + n) * P)

        def unit_of(u):
            return u // (NG * TB), (u // TB) % NG, u % TB

        xr = KS[:, 4:12, 0:S].bitcast(F32)
        yth = QS[:, 0:8, 0:S].bitcast(F32)
        sq = KS[:, 0, 0:S].bitcast(F32).rearrange("p (i h d) -> p i h d", i=TB, d=DH)

        block = ctx.enter_context(nc.Block())

        @block.sync
        def _(sp):
            for b in range(B):
                sp.dma_start(x[:, b * TB:(b + 1) * TB, :],
                             a["x"].rearrange("(t p) d -> p t d", p=P)[:, b * TB:(b + 1) * TB, :]).then_inc(x_in[b], 16)
            sp.dma_start(cst["ident"][:, :], a["c_ident"]).then_inc(cst["ident_in"], 16)
            sp.dma_start(wp[:, :, :], a["w_proj"].rearrange("(k p) n -> p k n", p=P)).then_inc(sem_wp, 16)
            for dst, src in ((cos[:, :, :], a["c_cos"]), (sin[:, :, :], a["c_sin"]),
                             (gate_add[:, :, :], a["c_gate_add"]), (future[:, :], a["c_future"]),
                             (headmask[:, :, :], a["c_headmask"]), (tri[:, :, :], a["c_tri"]),
                             (ksel[:, :, :], a["c_ksel"]), (ident_b[:, :], a["c_ident_b"]),
                             (onorm[:, :], a["L0_attn_o_norm_w"].unsqueeze(0).broadcast_to([P, DH]))):
                sp.dma_start(dst, src).then_inc(sem_const, 16)
            sp.dma_start(KS[R_BIAS:R_ALL, :, :], spread(a["c_kconst"], 1, H)).then_inc(kconst_ready, 16)

            def stack_bias(b):
                sp.wait_ge(biasT_read, b + 1)
                sp.dma_start(bias_dram[b].rearrange("(f p) t -> p f t", p=P),
                             biasT[:, :, :]).then_inc(bias_out, 16)
                sp.wait_ge(bias_out, 16 * (b + 1))
                sp.dma_start(QS[R_BIAS:R_MAX, :, b * S:(b + 1) * S],
                             bias_dram[b].rearrange("(h n) t -> n h t", n=NBLK)).then_inc(q_stacked[b], 16)

            def stack_parts(b, halves):
                for k in halves:
                    n = 4 * b + k
                    which, half = k // 2, k % 2
                    sp.wait_ge(H_ready, n + 1)
                    sp.wait_ge(M_ready, n + 1)
                    sp.wait_ge(L_ready, n + 1)
                    sp.dma_start(parts_dram[b, which, :, half * P:(half + 1) * P, :].rearrange("l p t -> p l t"),
                                 parts[n % 4]).then_inc(parts_out[n % 4], 16)
                    if half == 0:
                        continue
                    sp.wait_ge(parts_out[(n - 1) % 4], 16 * (b + 1))
                    sp.wait_ge(parts_out[n % 4], 16 * (b + 1))
                    dst, done = ((QS, q_stacked), (KS, k_stacked))[which]
                    for r, pair in enumerate(STACK):
                        sp.dma_start(dst[r * DH:(r + 1) * DH, :, b * S:(b + 1) * S],
                                     parts_dram[b, which, pair[which]].rearrange("(h d) t -> d h t", d=DH)
                                     ).then_inc(done[b], 16)

            def stack_maxima(b):
                sp.wait_ge(maxT_read, b + 1)
                sp.dma_start(max_dram[b], msT[:, b, :]).then_inc(max_out, 16)
                sp.wait_ge(max_out, 16 * (b + 1))
                sp.dma_start(QS[R_MAX:R_ALL, :, b * S:(b + 1) * S],
                             max_dram[b].rearrange("(l h) t -> l h t", l=3)).then_inc(q_stacked[b], 16)

            stack_parts(0, range(4))
            stack_bias(0)
            stack_parts(1, range(4))
            sp.dma_start(wo[:, :, :], a["w_o"].rearrange("(k p) n -> p k n", p=P)).then_inc(sem_wo, 16)
            stack_bias(1)
            for b in range(B):
                stack_maxima(b)
            sp.wait_ge(PV_done, NG * TB)
            sp.dma_start(xr, a["x"].rearrange("(t p) d -> p t d", p=P)).then_inc(x_again, 16)

        @block.gpsimd
        def _(pool):
            link = chain(pool, pool_step)
            pool.memset(mhalf[:, :], -0.5).then_inc(half_done, 1)
            link(pool.memset(V[:, :, :, :], 0.0))
            link(pool.memset(V[:, :, :, DH:DH + 1], 1.0))
            link(pool.memset(gates[:, :, :, NBLK:GATE_ROW], SENT))
            link(pool.memset(sc[:, :, E:EROW], SENT))
            pool.memset(cs[:, :, :], 0.0).then_inc(init_done, 1)
            pool.wait_ge(half_done, 1)
            for b in range(B):
                tb = slice(b * TB, (b + 1) * TB)
                pool.wait_ge(var_ready, b + 1)
                pool.tensor_tensor(rstd[:, tb], ve[:, tb], mhalf[:, 0:TB], ALU.pow).then_inc(rstd_ready, 1)
            pool.wait_ge(wph_ready, 1)
            pool.tensor_tensor(wp_l[:, :, :], wp[:, :, :], wp_h[:, :, :].bitcast(F32), ALU.subtract).then_inc(wpl_ready, 1)

            def split_chunk(s):
                pool.wait_ge(wh_ready, s + 1)
                if s >= 3:
                    pool.wait_ge(down_done, s - 2)
                pool.tensor_tensor(wl[:, s % 3, :, :], wr[:, s % 2, :, :], wh[:, s % 3, :, :].bitcast(F32),
                                   ALU.subtract).then_inc(wl_ready, 1)

            def inverse_roots(w):
                pool.wait_ge(rms_in, w + 1)
                pool.tensor_tensor(small[:, 2, :, :], small[:, 1, :, :],
                                   mhalf[:, 0:TB * HG].rearrange("p (i h) -> p i h", h=HG), ALU.pow).then_inc(rms_out, 1)

            def slot(q):
                for b in range(B):
                    if PREP_SLOT[b] < q <= PREP_SLOT[b] + 4:
                        n = 4 * b + q - PREP_SLOT[b] - 1
                        pool.wait_ge(M_ready, n + 1)
                        pool.wait_ge(R1_ready, n + 1)
                        if n >= 4:
                            pool.wait_ge(parts_out[n % 4], 16)
                        pool.tensor_tensor(parts[n % 4][:, 2, :], R1[:, n % 2, :], parts[n % 4][:, 1, :],
                                           ALU.subtract).then_inc(L_ready, 1)
            split_chunk(0)
            for t in range(T):
                pool.wait_ge(qk_read, t + 1)
                pool.tensor_tensor(qkr[:, t, :], rot_a[:, t % 2, :], rot_b[:, t % 2, :],
                                   ALU.add).then_inc(rope_ready, 1)
            for s in range(STEPS):
                if s + 1 < STEPS:
                    split_chunk(s + 1)
                slot(s * SLOTS)
                slot(s * SLOTS + 1)
                if pool_weighs(s):
                    done = sum(pool_weighs(r) for r in range(s + 1))
                    pool.wait_ge(uv_ready, done)
                    pool.wait_ge(weights_read, done)
                    pool.wait_ge(gh_ready, s)
                    pool.wait_ge(gl_ready, s)
                    pool.tensor_tensor(gb[:, :], uv[:, :], th[:, :], ALU.mult).then_inc(g_ready, 1)
                pool.wait_ge(gh_ready, s + 1)
                if s >= 2:
                    pool.wait_ge(down_done, s - 1)
                pool.tensor_tensor(gl[:, s % 2, :], gb[:, :], gh[:, s % 2, :].bitcast(F32),
                                   ALU.subtract).then_inc(gl_ready, 1)
                if s == WO_STEP:
                    pool.wait_ge(woh_ready, 1)
                    pool.tensor_tensor(wo_l[:, :, :], wo[:, :, :], wo_h[:, :, :].bitcast(F32),
                                       ALU.subtract).then_inc(wol_ready, 1)
                slot(s * SLOTS + 2)
                slot(s * SLOTS + 3)
                for q in range(s * SLOTS, (s + 1) * SLOTS):
                    if out_unit(q, 1) is not None:
                        inverse_roots(out_unit(q, 1))
            if OUT_SLOT[-1] + 1 >= STEPS * SLOTS:
                inverse_roots(B * NG - 1)
            pool.wait_ge(x_again, 16)
            pool.wait_ge(onT_ready, 2 * B)
            for n in range(T // 2):
                pair = slice(2 * n, 2 * n + 2)
                pool.wait_ge(gated_ready, n + 1)
                pool.tensor_tensor(x1[:, pair, :], xr[:, pair, :], y[:, pair, :], ALU.add)

        @block.scalar
        def _(act):
            def load_chunk(s):
                if s >= 2:
                    act.wait_ge(wh_ready, s - 1)
                    act.wait_ge(wl_ready, s - 1)
                act.dma_start(wr[:, s % 2, :, :], a["w_chunks"][s % CH]).then_inc(w_in[s % 2], 16)

            load_chunk(0)
            load_chunk(1)
            act.wait_ge(sem_wp, 16)
            act.copy(wp_h[:, :, :], wp[:, :, :]).then_inc(wph_ready, 1)
            for n in range(2 * B):
                b, c = n // 2, n % 2
                act.wait_ge(xT_ready, n + 1)
                act.copy(xh[:, c, b * S:(b + 1) * S], bank[n][:, :]).then_inc(xh_ready, 1)

            def values(t):
                act.wait_ge(vg_ready, t + 1)
                act.wait_ge(init_done, 1)
                vg = bank[6 + t % 2]
                act.copy(V[:, t, :, 0:DH], vg[:, 0:D].rearrange("p (h d) -> p h d", d=DH))
                act.copy(lg[:, t, :], vg[:, D:D + E]).then_inc(vg_read, 1)

            def split_chunk(s):
                act.wait_ge(w_in[s % 2], 16 * (s // 2 + 1))
                if s >= 3:
                    act.wait_ge(down_done, s - 2)
                act.copy(wh[:, s % 3, :, :], wr[:, s % 2, :, :]).then_inc(wh_ready, 1)

            def bias_rows(b):
                act.wait_ge(biasT_ready, b + 1)
                if b:
                    act.wait_ge(bias_out, 16)
                act.copy(biasT[:, :, :].rearrange("p f t -> p (f t)"), bank_b[2][:, :]).then_inc(biasT_read, 1)

            split_chunk(0)
            for t in range(T):
                values(t)
            act.wait_ge(e_in, 1)
            act.activation(rt[:, 1, :, :], rt[:, 0, :, :], ACT.Exp).then_inc(e_out, 1)

            def half_silu(n):
                act.wait_ge(PV_done, NG * TB)
                act.wait_ge(y_read, 2 * (n + 1))
                act.activation(yth[:, n * TB:(n + 1) * TB, :], y[:, n * TB:(n + 1) * TB, :], ACT.Tanh,
                               scale=0.5).then_inc(yth_ready, 1)

            def slot(q):
                for b in range(B):
                    if PREP_SLOT[b] <= q < PREP_SLOT[b] + 4:
                        k = q - PREP_SLOT[b]
                        n = 4 * b + k
                        act.wait_ge(qkT_ready, n + 1)
                        if b:
                            act.wait_ge(gate_ready, 1)
                            act.wait_ge(kmb_ready, 2)
                            act.wait_ge(R1_ready, 4)
                        act.copy(X[:, k, :], bank[n % 2][:, :]).then_inc(X_ready, 1)
                        if n >= 4:
                            act.wait_ge(parts_out[n % 4], 16)
                        act.wait_ge(X_ready, n + 1)
                        act.copy(parts[n % 4][:, 0, :], X[:, k, :]).then_inc(H_ready, 1)
                    if PREP_SLOT[b] < q <= PREP_SLOT[b] + 4:
                        n = 4 * b + q - PREP_SLOT[b] - 1
                        act.wait_ge(R1_ready, n + 1)
                        act.copy(parts[n % 4][:, 1, :], R1[:, n % 2, :]).then_inc(M_ready, 1)
                    if q == BIAS_SLOT[b]:
                        bias_rows(b)
                    if q == MAX_SLOTS[b] + 1:
                        act.wait_ge(maxT_ready, b + 1)
                        act.copy(msT[:, b, :], bank_b[2][0:48, 0:512]).then_inc(maxT_read, 1)
                if not B_SLOT <= q < B_SLOT + PASS_SLOTS:
                    return
                if q == B_SLOT:
                    act.wait_ge(wol_ready, 1)
                for k in (2 * (q - B_SLOT), 2 * (q - B_SLOT) + 1):
                    j, heads = exp_loads(0)[k % LOADS]
                    n = (S - j * P) * len(heads)
                    act.wait_ge(B_ready, k + 1)
                    if k >= 8:
                        act.wait_ge(PV_done, (k - 8) // LOADS * TB + exp_loads(0)[(k - 8) % LOADS][0] + 1)
                    act.activation(PT[:, k % 8, 0:n], bank[k % 2][:, 0:n], ACT.Exp,
                                   scale=float(DH) ** -0.5).then_inc(P_ready, 1)

            for s in range(STEPS):
                act.wait_ge(G_ready, s + 1)
                if s >= 1:
                    act.wait_ge(G_read, s)
                act.activation(th[:, :], bank[3][:, :], ACT.Tanh, scale=0.5).then_inc(th_ready, 1)
                if s == 0:
                    act.wait_ge(combT_ready, 1)
                    act.copy(combT[:, :], bank_b[6][0:64, :]).then_inc(combT_read, 1)
                slot(s * SLOTS)
                if s < DVE_STEP:
                    split_chunk(s + 1)
                if s + 2 < STEPS:
                    load_chunk(s + 2)
                slot(s * SLOTS + 1)
                if pool_weighs(s):
                    act.wait_ge(U_ready, s + 1)
                    act.wait_ge(G_read, s + 1)
                    act.copy(th[:, :], bank[5][:, :]).then_inc(weights_read, 1)
                if s < DVE_STEP:
                    act.wait_ge(g_ready, s + 1)
                    if s >= 2:
                        act.wait_ge(down_done, s - 1)
                    act.copy(gh[:, s % 2, :], gb[:, :]).then_inc(gh_ready, 1)
                slot(s * SLOTS + 2)
                slot(s * SLOTS + 3)
                if s == WO_STEP:
                    act.wait_ge(sem_wo, 16)
                    act.copy(wo_h[:, :, :], wo[:, :, :]).then_inc(woh_ready, 1)
                if s == YTH_STEP:
                    half_silu(0)
            for q in range(STEPS * SLOTS, SLOT_END):
                slot(q)
            half_silu(1)
            for n in range(2 * B):
                act.wait_ge(onT_ready, n + 1)
                act.copy(xh[:, n % 2, (n // 2) * S:(n // 2 + 1) * S], bank[n][:, :]).then_inc(onh_ready, 1)

        @block.vector
        def _(dve):
            link = chain(dve, dve_step)
            for b in range(B):
                dve.wait_ge(x_in[b], 16)
                for t in range(b * TB, (b + 1) * TB):
                    ins = dve.bn_stats(st[:, t, :], x[:, t, :])
                link(ins)
                for t in range(b * TB, (b + 1) * TB):
                    ins = dve.bn_aggr(mv[:, t, :], st[:, t, :])
                link(ins)
                tb = slice(b * TB, (b + 1) * TB)
                dve.tensor_scalar(ve[:, tb], mv[:, tb, 1], LN_EPS, None, ALU.add).then_inc(var_ready, 1)
            for b in range(B):
                dve.wait_ge(rstd_ready, b + 1)
                for t in range(b * TB, (b + 1) * TB):
                    dve.tensor_scalar(xn[:, t, :], x[:, t, :], mv[:, t, 0:1], rstd[:, t:t + 1],
                                      ALU.subtract, ALU.mult).then_inc(xn_ready, 1)
            for n in range(2 * B):
                b, c = n // 2, n % 2
                dve.wait_ge(xh_ready, n + 1)
                dve.tensor_tensor(xl[:, c, b * S:(b + 1) * S], bank[n][:, :],
                                  xh[:, c, b * S:(b + 1) * S].bitcast(F32), ALU.subtract).then_inc(xl_ready, 1)
            dve.wait_ge(sem_const, 16 * 9)

            def rotate(t):
                i = t % TB
                dve.wait_ge(qk_ready, t + 1)
                if t >= 2:
                    dve.wait_ge(rope_ready, t - 1)
                qk = bank[4 + t % 2][:, :].rearrange("p (h s e) -> p h s e", s=2, e=DH // 2)
                rb = rot_b[:, t % 2, :].rearrange("p (h s e) -> p h s e", s=2, e=DH // 2)
                dve.tensor_tensor(rot_a[:, t % 2, :].rearrange("p (h d) -> p h d", d=DH),
                                  bank[4 + t % 2][:, :].rearrange("p (h d) -> p h d", d=DH),
                                  spread(cos[:, i, :], 1, 2 * H), ALU.mult)
                dve.tensor_tensor(rb[:, :, 0, :], qk[:, :, 1, :], spread(sin[:, i, 0:DH // 2], 1, 2 * H), ALU.mult)
                dve.tensor_tensor(rb[:, :, 1, :], qk[:, :, 0, :], spread(sin[:, i, DH // 2:DH], 1, 2 * H),
                                  ALU.mult).then_inc(qk_read, 1)

            def key_means_and_rest(b, k):
                n = 4 * b + k
                dve.wait_ge(X_ready, n + 1)
                dve.wait_ge(H_ready, n + 1)
                if n >= 2:
                    dve.wait_ge(L_ready, n - 1)
                else:
                    dve.wait_ge(rope_ready, T)
                dve.tensor_tensor(R1[:, n % 2, :], X[:, k, :], parts[n % 4][:, 0, :],
                                  ALU.subtract).then_inc(R1_ready, 1)
                if k >= 2:
                    w = 2 * b + k - 2
                    link(dve.tensor_reduce(km[:, w, :], X[:, k, :].rearrange("p (n e) -> p n e", e=BLK),
                                           AX.X, ALU.add))
                    dve.scalar_tensor_tensor(out=kmb[:, w, :, :], in0=spread(km[:, w, :], 1, 8),
                                             scalar=1.0 / BLK, in1=headmask[:, :, :], op0=ALU.mult,
                                             op1=ALU.mult).then_inc(kmb_ready, 1)

            def gates_in(b):
                for i in range(1, TB):
                    dve.wait_ge(gate_ready, b + 1)
                    dve.wait_ge(init_done, 1)
                    if b:
                        dve.wait_ge(bias_ready, TB)
                    o = (i - 1) % 2 * H * NBLK
                    dve.tensor_tensor(gates[:, i - 1, :, 0:NBLK],
                                      bank[(i - 1) // 2][:, o:o + H * NBLK].rearrange("p (h n) -> p h n", n=NBLK),
                                      spread(gate_add[:, i, :], 1, H), ALU.add).then_inc(gate_read, 1)

            def select(t, heads):
                b, i = t // TB, t % TB
                if i == 0:
                    dve.tensor_copy(bias[:, t, :, :], spread(future[:, :], 1, H)).then_inc(bias_ready, 1)
                    return
                dve.wait_ge(gate_read, b * (TB - 1) + i)
                dve.wait_ge(bias_ready, t)
                for h in heads:
                    ins = dve.max(top[:, h, :], gates[:, i - 1, h, :])
                link(ins)
                for h in heads:
                    ins = dve.match_replace(picked[:, h, :], top[:, h, :], gates[:, i - 1, h, :], SENT)
                link(ins)
                hs = slice(heads.start, heads.stop)
                ins = dve.tensor_scalar(bias[:, t, hs, :], picked[:, hs, 0:NBLK], SENT_TEST, NEG, ALU.is_lt, ALU.mult)
                if heads.stop == H:
                    ins.then_inc(bias_ready, 1)

            def router_in():
                dve.wait_ge(vg_read, T)
                link(dve.tensor_reduce(rm[:, 0, :], lg[:, :, :], AX.X, ALU.max))
                dve.tensor_tensor(rt[:, 0, :, :], lg[:, :, :], spread(rm[:, 0, :], 2, E), ALU.subtract).then_inc(e_in, 1)

            def router_out():
                dve.wait_ge(e_out, 1)
                dve.wait_ge(init_done, 1)
                link(dve.tensor_reduce(rm[:, 1, :], rt[:, 1, :, :], AX.X, ALU.add))
                link(dve.reciprocal(rm[:, 2, :], rm[:, 1, :]))
                link(dve.tensor_tensor(sc[:, :, 0:E], rt[:, 1, :, :], spread(rm[:, 2, :], 2, E), ALU.mult))
                for t in range(T):
                    ins = dve.max(rtop[:, t, :], sc[:, t, :])
                link(ins)
                for t in range(T):
                    ins = dve.match_replace(rpick[:, t, :], rtop[:, t, :], sc[:, t, :], SENT)
                link(ins)
                link(dve.scalar_tensor_tensor(out=rt[:, 2, :, :], in0=rpick[:, :, 0:E], scalar=SENT_TEST,
                                              in1=sc[:, :, 0:E], op0=ALU.is_ge, op1=ALU.mult))
                link(dve.tensor_copy(cs[:, :, 0:E], rt[:, 2, :, :]))
                link(dve.tensor_tensor(rt[:, 3, :, :], rt[:, 2, :, :], cs[:, :, 0:E], ALU.subtract))
                link(dve.tensor_copy(cs[:, :, E:2 * E], rt[:, 3, :, :]))
                dve.tensor_tensor(cs[:, :, 2 * E:3 * E], rt[:, 3, :, :], cs[:, :, E:2 * E],
                                  ALU.subtract).then_inc(comb_ready, 1)

            def head_maxima(k):
                b, g = k // (NG * LOADS), k // LOADS % NG
                i, heads = unit_loads(g)[k % LOADS]
                n = (i + 1) * P
                dve.wait_ge(A_ready, k + 1)
                dve.tensor_reduce(mx[:, b * TB + i, heads[0]:heads[-1] + 1],
                                  bank[k % 2][:, 0:len(heads) * n].rearrange("p (h n) -> p h n", n=n),
                                  AX.X, ALU.max).then_inc(A_read, 1)

            def maxima_parts(b):
                tb = slice(b * TB, (b + 1) * TB)
                dve.wait_ge(A_read, (b + 1) * NG * LOADS)
                link(dve.tensor_scalar(mr[:, 0, :, :], mx[:, tb, :], -1.0, None, ALU.mult))
                link(dve.tensor_copy(ms[:, tb, 0, :], mr[:, 0, :, :]))
                link(dve.tensor_tensor(mr[:, 1, :, :], mr[:, 0, :, :], ms[:, tb, 0, :], ALU.subtract))
                link(dve.tensor_copy(ms[:, tb, 1, :], mr[:, 1, :, :]))
                dve.tensor_tensor(ms[:, tb, 2, :], mr[:, 1, :, :], ms[:, tb, 1, :],
                                  ALU.subtract).then_inc(max_ready, 1)

            def out_rows(w):
                dve.wait_ge(PV_done, (w + 1) * TB)
                if w >= 1:
                    dve.wait_ge(oTT_ready, w)
                dve.tensor_copy(oT[:, :], bank[2][:, :]).then_inc(oT_ready, 1)

            def out_tokens(w):
                b, g = w // NG, w % NG
                dve.wait_ge(oTT_ready, w + 1)
                dve.tensor_copy(ob[:, b * TB:(b + 1) * TB, g * HG:(g + 1) * HG, :],
                                bank[5][:, :].rearrange("p (i h d) -> p i h d", i=TB, d=32)[:, :, :, 0:DH + 1]
                                ).then_inc(ob_ready, 1)

            def heads_of(w):
                b, g = w // NG, w % NG
                return slice(b * TB, (b + 1) * TB), slice(g * HG, (g + 1) * HG)

            def rms_sums(w):
                tb, hs = heads_of(w)
                o, l = ob[:, tb, hs, 0:DH], ob[:, tb, hs, DH]
                dve.wait_ge(ob_ready, w + 1)
                if w:
                    dve.wait_ge(on_ready, w)
                link(dve.tensor_tensor(sq, o, o, ALU.mult))
                link(dve.tensor_reduce(small[:, 0, :, :], sq, AX.X, ALU.add))
                link(dve.tensor_tensor(small[:, 1, :, :], l, l, ALU.mult))
                link(dve.scalar_tensor_tensor(out=small[:, 0, :, :], in0=small[:, 1, :, :], scalar=DH * RMS_EPS,
                                              in1=small[:, 0, :, :], op0=ALU.mult, op1=ALU.add))
                dve.tensor_scalar(small[:, 1, :, :], small[:, 0, :, :], 1.0 / DH, None, ALU.mult).then_inc(rms_in, 1)

            def rms_scale(w):
                tb, hs = heads_of(w)
                dve.wait_ge(rms_out, w + 1)
                link(dve.tensor_tensor(sq, ob[:, tb, hs, 0:DH], spread(small[:, 2, :, :], 3, DH), ALU.mult))
                dve.tensor_tensor(xn[:, tb, hs.start * DH:hs.stop * DH].rearrange("p t (h d) -> p t h d", d=DH), sq,
                                  onorm[:, :].unsqueeze(1).unsqueeze(1).broadcast_to([P, TB, HG, DH]),
                                  ALU.mult).then_inc(on_ready, 1)

            def slot(q):
                for b in range(B):
                    if PREP_SLOT[b] <= q < PREP_SLOT[b] + 4:
                        key_means_and_rest(b, q - PREP_SLOT[b])
                    if q == GATE_SLOT[b]:
                        gates_in(b)
                if A_SLOT <= q < A_SLOT + PASS_SLOTS:
                    for k in (2 * (q - A_SLOT), 2 * (q - A_SLOT) + 1):
                        head_maxima(k)
                for b in range(B):
                    if q in SELECT_SLOTS[b]:
                        n = SELECT_SLOTS[b].index(q)
                        if n == 0:
                            select(b * TB, range(H))
                        select(b * TB + 1 + n // 2, range(n % 2 * H // 2, (n % 2 + 1) * H // 2))
                    if q + 1 == MAX_SLOTS[b]:
                        maxima_parts(b)
                for w in range(B * NG):
                    if q == SUM_SLOT[w][-1]:
                        out_rows(w)
                if out_unit(q, 0) is not None:
                    out_tokens(out_unit(q, 0))
                if out_unit(q, 1) is not None:
                    rms_sums(out_unit(q, 1))
                if out_unit(q, 3) is not None:
                    rms_scale(out_unit(q, 3))

            def take_y(n):
                dve.wait_ge(down_done, (n + 1) * CH)
                for k in range(2):
                    dve.tensor_copy(y[:, n * TB + 2 * k:n * TB + 2 * k + 2, :],
                                    bank[6 + k][:, :].rearrange("p (t d) -> p t d", d=D)).then_inc(y_read, 1)

            def silu_y(n):
                dve.wait_ge(yth_ready, n + 1)
                half = y[:, n * TB:(n + 1) * TB, :]
                link(dve.scalar_tensor_tensor(out=half, in0=yth[:, n * TB:(n + 1) * TB, :], scalar=1.0, in1=half,
                                              op0=ALU.add, op1=ALU.mult))

            for t in range(T):
                rotate(t)
            router_in()
            router_out()

            for s in range(STEPS):
                c = s % CH
                if s >= DVE_STEP and s + 1 < STEPS:
                    dve.wait_ge(w_in[(s + 1) % 2], 16 * ((s + 1) // 2 + 1))
                    dve.wait_ge(wl_ready, s + 1)
                    dve.wait_ge(down_done, s - 1)
                    dve.tensor_copy(wh[:, (s + 1) % 3, :, :], wr[:, (s + 1) % 2, :, :]).then_inc(wh_ready, 1)
                dve.wait_ge(th_ready, s + 1)
                if s >= 1:
                    dve.wait_ge(g_ready, s)
                dve.scalar_tensor_tensor(out=s2[:, :], in0=th[:, :], scalar=1.0, in1=bank[3][:, :],
                                         op0=ALU.add, op1=ALU.mult).then_inc(G_read, 1)
                slot(s * SLOTS)
                dve.wait_ge(U_ready, s + 1)
                dve.wait_ge(G_read, s + 1)
                if s >= 1:
                    dve.wait_ge(gh_ready, s)
                    dve.wait_ge(gl_ready, s)
                if pool_weighs(s):
                    dve.scalar_tensor_tensor(out=uv[:, :], in0=s2[:, :], scalar=0.5, in1=bank[4][:, :],
                                             op0=ALU.mult, op1=ALU.mult).then_inc(uv_ready, 1)
                elif c < ECH:
                    link(dve.scalar_tensor_tensor(out=uv[:, :], in0=s2[:, :], scalar=0.5, in1=bank[4][:, :],
                                                  op0=ALU.mult, op1=ALU.mult))
                    dve.tensor_tensor(gb[:, :], uv[:, :], bank[5][:, :], ALU.mult).then_inc(g_ready, 1)
                else:
                    dve.scalar_tensor_tensor(out=gb[:, :], in0=s2[:, :], scalar=0.5, in1=bank[4][:, :],
                                             op0=ALU.mult, op1=ALU.mult).then_inc(g_ready, 1)
                if s >= DVE_STEP:
                    dve.wait_ge(g_ready, s + 1)
                    dve.wait_ge(down_done, s - 1)
                    dve.tensor_copy(gh[:, s % 2, :], gb[:, :]).then_inc(gh_ready, 1)
                for q in range(s * SLOTS + 1, (s + 1) * SLOTS):
                    slot(q)
                if s == CH:
                    take_y(0)
                if s == YTH_STEP + 1:
                    silu_y(0)
            take_y(1)
            for q in range(STEPS * SLOTS, SLOT_END):
                slot(q)
            if OUT_SLOT[-1] + 1 >= max(SLOT_END, STEPS * SLOTS):
                rms_sums(B * NG - 1)
            if OUT_SLOT[-1] + 3 >= max(SLOT_END, STEPS * SLOTS):
                rms_scale(B * NG - 1)
            for n in range(2 * B):
                dve.wait_ge(onh_ready, n + 1)
                part = (slice(None), n % 2, slice((n // 2) * S, (n // 2 + 1) * S))
                dve.tensor_tensor(xl[part], bank[n][:, :], xh[part].bitcast(F32), ALU.subtract).then_inc(onl_ready, 1)
            silu_y(1)
            for n in range(T // 2):
                pair = slice(2 * n, 2 * n + 2)
                dve.wait_ge(s_ready, n + 1)
                dve.scalar_tensor_tensor(out=y[:, pair, :], in0=y[:, pair, :], scalar=0.5,
                                         in1=bank[4 + n % 2][:, :].rearrange("p (t d) -> p t d", d=D),
                                         op0=ALU.mult, op1=ALU.mult).then_inc(gated_ready, 1)

        @block.tensor
        def _(pe):
            pe.wait_ge(cst["ident_in"], 16)
            for n in range(2 * B):
                b, c = n // 2, n % 2
                for i in range(TB):
                    pe.wait_ge(xn_ready, b * TB + i + 1)
                    ins = pe.transpose(bank[n][:, i * P:(i + 1) * P], xn[:, b * TB + i, c * P:(c + 1) * P], ident[:, :])
                ins.then_inc(xT_ready, 1)
            pe.wait_ge(wph_ready, 1)
            pe.wait_ge(wpl_ready, 1)

            def project(t):
                pe.wait_ge(xl_ready, 2 * (t // TB + 1))
                if t >= 2:
                    pe.wait_ge(qk_read, t - 1)
                    pe.wait_ge(vg_read, t - 1)
                for c in range(KD):
                    ins = split_matmul(pe, bank[4 + t % 2][:, :], xh[:, c, tokens(t)], xl[:, c, tokens(t)],
                                       wp_h[:, c, 0:512], wp_l[:, c, 0:512], c == 0, c == KD - 1)
                ins.then_inc(qk_ready, 1)
                for c in range(KD):
                    ins = split_matmul(pe, bank[6 + t % 2][:, 0:264], xh[:, c, tokens(t)], xl[:, c, tokens(t)],
                                       wp_h[:, c, 512:776], wp_l[:, c, 512:776], c == 0, c == KD - 1)
                ins.then_inc(vg_ready, 1)

            def transpose_qk(b, k):
                n = 4 * b + k
                if k == 0:
                    pe.wait_ge(rope_ready, (b + 1) * TB)
                if b and k < 2:
                    pe.wait_ge(gate_read, TB - 1)
                if n >= 2:
                    pe.wait_ge(X_ready, n - 1)
                for i in range(TB):
                    ins = pe.transpose(bank[n % 2][:, i * P:(i + 1) * P], qkr[:, b * TB + i, k * P:(k + 1) * P],
                                       ident[:, :])
                ins.then_inc(qkT_ready, 1)

            def block_gates(b):
                pe.wait_ge(kmb_ready, 2 * (b + 1))
                pe.wait_ge(X_ready, 4 * (b + 1))
                for i in range(1, TB):
                    for f in range(2):
                        o = (i - 1) % 2 * H * NBLK + f * P
                        ins = pe.matmul(bank[(i - 1) // 2][:, o:o + P], X[:, f, i * P:(i + 1) * P],
                                        kmb[:, 2 * b + f, :, :], start=True, stop=True)
                ins.then_inc(gate_ready, 1)

            def transpose_bias(b):
                pe.wait_ge(bias_ready, (b + 1) * TB)
                if b:
                    pe.wait_ge(biasT_read, 1)
                for f in range(2):
                    for i in range(TB):
                        ins = pe.transpose(bank_b[2][:, f * 512 + i * P:f * 512 + (i + 1) * P],
                                           bias[:, b * TB + i, f * 8:(f + 1) * 8, :], ident_b[:, :])
                ins.then_inc(biasT_ready, 1)

            def transpose_comb():
                pe.wait_ge(sem_const, 16 * 9)
                pe.wait_ge(comb_ready, 1)
                for t in range(T):
                    ins = pe.transpose(bank_b[6][0:64, t * P:(t + 1) * P], cs[:, t, :], ident_b[:, :])
                ins.then_inc(combT_ready, 1)
                pe.wait_ge(combT_read, 1)

            for t in range(T):
                project(t)
            pe.wait_ge(xl_ready, 2 * B)
            pe.wait_ge(qk_read, T)
            pe.wait_ge(vg_read, T)

            def scores_by_query(k):
                b, g, r = k // (NG * LOADS), k // LOADS % NG, k % LOADS
                if g == 0 and r == 0:
                    pe.wait_ge(q_stacked[b], 16 * (len(STACK) + 1))
                    pe.wait_ge(k_stacked[b], 16 * len(STACK))
                    pe.wait_ge(kconst_ready, 16)
                i, heads = unit_loads(g)[r]
                n = (i + 1) * P
                if k < 2:
                    pe.wait_ge(gate_read, B * (TB - 1))
                else:
                    pe.wait_ge(A_read, k - 1)
                for o, h in enumerate(heads):
                    out = bank[k % 2][:, o * n:(o + 1) * n]
                    pe.matmul(out, QS[0:R_MAX, h, b * S + i * P:b * S + (i + 1) * P],
                              KS[0:R_MAX, h, b * S:b * S + n], start=True, stop=False)
                    ins = pe.matmul(out[:, n - P:n], ident_b[:, :], tri[:, 0, :], start=False, stop=True)
                ins.then_inc(A_ready, 1)

            def scores_by_key(k):
                w, r = k // LOADS, k % LOADS
                b = w // NG
                j, heads = exp_loads(w % NG)[r]
                n = S - j * P
                if w % NG == 0 and r == 0:
                    pe.wait_ge(q_stacked[b], 16 * (len(STACK) + 2))
                if k == 0:
                    pe.wait_ge(A_read, B * NG * LOADS)
                if k >= 2:
                    pe.wait_ge(P_ready, k - 1)
                for o, h in enumerate(heads):
                    out = bank[k % 2][:, o * n:(o + 1) * n]
                    pe.matmul(out, KS[0:R_ALL, h, b * S + j * P:b * S + (j + 1) * P],
                              QS[0:R_ALL, h, b * S + j * P:(b + 1) * S], start=True, stop=False)
                    ins = pe.matmul(out[:, 0:P], ident_b[:, :], tri[:, 1, :], start=False, stop=True)
                ins.then_inc(B_ready, 1)

            def transpose_maxima(b):
                pe.wait_ge(max_ready, b + 1)
                pe.wait_ge(biasT_read, 2)
                for i in range(TB):
                    ins = pe.transpose(bank_b[2][0:48, i * P:(i + 1) * P],
                                       ms[:, b * TB + i, :, :].rearrange("p l h -> p (l h)"), ident_b[:, :])
                ins.then_inc(maxT_ready, 1)

            def values_sum(u):
                b, g, j = unit_of(u)
                q = u // TB
                pe.wait_ge(P_ready, q * LOADS + LAST_LOAD[j] + 1)
                if j == 0 and q >= 1:
                    pe.wait_ge(oT_ready, q)
                if u == 0:
                    pe.wait_ge(maxT_read, B)
                n = S - j * P
                loads = [(r, o, h) for r, (tile, heads) in enumerate(exp_loads(g)) if tile == j
                         for o, h in enumerate(heads)]
                for c, (r, o, h) in enumerate(loads):
                    ins = pe.matmul(bank[2][32 * c:32 * (c + 1), j * P:S], V[:, b * TB + j, h, :],
                                    PT[:, (q * LOADS + r) % 8, o * n:(o + 1) * n], start=(j == 0), stop=(j == TB - 1))
                ins.then_inc(PV_done, 1)

            def transpose_out(q):
                pe.wait_ge(oT_ready, q + 1)
                pe.wait_ge(g_ready, min(OUT_SLOT[q] // SLOTS + 1, STEPS))
                for i in range(TB):
                    ins = pe.transpose(bank[5][:, i * P:(i + 1) * P], oT[:, i * P:(i + 1) * P], ident[:, :])
                ins.then_inc(oTT_ready, 1)

            def gate_product(s):
                part = slice(s // CH * S, (s // CH + 1) * S)
                w = s % 3
                pe.wait_ge(wl_ready, s + 1)
                if s >= 1:
                    pe.wait_ge(G_read, s)
                for k in range(KD):
                    ins = split_matmul(pe, bank[3][:, :], wh[:, w, k, 0:P], wl[:, w, k, 0:P],
                                       xh[:, k, part], xl[:, k, part], k == 0, k == KD - 1)
                ins.then_inc(G_ready, 1)

            def up_product(s):
                n, c = s // CH, s % CH
                part = slice(n * S, (n + 1) * S)
                w = s % 3
                if s >= 1:
                    pe.wait_ge(g_ready, s)
                for k in range(KD):
                    ins = split_matmul(pe, bank[4][:, :], wh[:, w, k, P:2 * P], wl[:, w, k, P:2 * P],
                                       xh[:, k, part], xl[:, k, part], k == 0, k == KD - 1)
                if c < ECH:
                    if any(q < s * SLOTS for q in OUT_SLOT):
                        pe.wait_ge(ob_ready, sum(q < s * SLOTS for q in OUT_SLOT))
                    ins = pe.matmul(bank[5][:, :], ksel[:, c, :], combT[:, part], start=True, stop=True)
                ins.then_inc(U_ready, 1)

            def down(s, k):
                c, w = s % CH, s % 3
                pe.wait_ge(gl_ready, s + 1)
                if c == 0 and s:
                    pe.wait_ge(y_read, 2)
                for o in range(2):
                    ins = split_matmul(pe, bank[6 + k][:, o * D:(o + 1) * D],
                                       gh[:, s % 2, tokens(2 * k + o)], gl[:, s % 2, tokens(2 * k + o)],
                                       wh[:, w, 2, :], wl[:, w, 2, :], c == 0 and o == 0, c == CH - 1, skip=True)
                if k:
                    ins.then_inc(down_done, 1)

            def slot(q):
                for b in range(B):
                    if PREP_SLOT[b] <= q < PREP_SLOT[b] + 4:
                        transpose_qk(b, q - PREP_SLOT[b])
                    if q == GATE_SLOT[b]:
                        block_gates(b)
                    if q == BIAS_SLOT[b]:
                        transpose_bias(b)
                if A_SLOT <= q < A_SLOT + PASS_SLOTS:
                    for k in (2 * (q - A_SLOT), 2 * (q - A_SLOT) + 1):
                        scores_by_query(k)
                for b in range(B):
                    if q == MAX_SLOTS[b] + 1:
                        transpose_maxima(b)
                if B_SLOT <= q < B_SLOT + PASS_SLOTS:
                    for k in (2 * (q - B_SLOT), 2 * (q - B_SLOT) + 1):
                        scores_by_key(k)
                for w in range(B * NG):
                    for j in range(TB):
                        if q == SUM_SLOT[w][j]:
                            values_sum(w * TB + j)
                if out_unit(q, 0) is not None:
                    transpose_out(out_unit(q, 0))

            for s in range(STEPS):
                gate_product(s)
                slot(s * SLOTS)
                if s == 0:
                    transpose_comb()
                up_product(s)
                slot(s * SLOTS + 1)
                if s >= 1:
                    down(s - 1, 0)
                slot(s * SLOTS + 2)
                if s >= 1:
                    down(s - 1, 1)
                slot(s * SLOTS + 3)
            down(STEPS - 1, 0)
            down(STEPS - 1, 1)
            for q in range(STEPS * SLOTS, SLOT_END):
                slot(q)
            for n in range(2 * B):
                b, c = n // 2, n % 2
                pe.wait_ge(on_ready, (b + 1) * NG)
                for i in range(TB):
                    ins = pe.transpose(bank[n][:, i * P:(i + 1) * P], xn[:, b * TB + i, c * P:(c + 1) * P], ident[:, :])
                ins.then_inc(onT_ready, 1)
            pe.wait_ge(woh_ready, 1)
            pe.wait_ge(wol_ready, 1)
            for n in range(T // 2):
                pe.wait_ge(onl_ready, 2 * (2 * n // TB + 1))
                if n >= 2:
                    pe.wait_ge(gated_ready, n - 1)
                for t in (2 * n, 2 * n + 1):
                    for c in range(KD):
                        ins = split_matmul(pe, bank[4 + n % 2][:, t % 2 * D:(t % 2 + 1) * D],
                                           xh[:, c, tokens(t)], xl[:, c, tokens(t)],
                                           wo_h[:, c, :], wo_l[:, c, :], c == 0, c == KD - 1, skip=True)
                ins.then_inc(s_ready, 1)


def layer1(nc, a, x1, out, cst):
    ctx = ExitStack()
    with ctx:
        m = Mem(nc, ctx)
        ident = cst["ident"]
        w_lr_h = m.sb("w_lr_h", [P, KD, 2 * HP], F32R)
        w_lr_l = m.sb("w_lr_l", [P, KD, 2 * HP], F32R)
        w_ai_h = m.sb("w_ai_h", [P, HT, 2 * HP], F32R)
        w_ai_l = m.sb("w_ai_l", [P, HT, 2 * HP], F32R)
        w_o_h = m.sb("w_o_h", [P, HT, D], F32R)
        w_o_l = m.sb("w_o_l", [P, HT, D], F32R)
        w_f = m.sb("w_f", [P, KD, FW])
        md = m.sb("md", [P, KD, 2 * N_SEL])
        w_g = m.sb("w_g", [OW, D])
        vec = m.sb("vec", [P, 10, HT])
        vec2 = m.sb("vec2", [P, 10, HT])
        sel_vec = m.sb("sel_vec", [P, 3, N_SEL])
        bo = m.sb("bo", [P, D])
        fmask = m.sb("fmask", [2 * N_SEL, FW])
        ones16 = m.sb("ones16", [2 * N_SEL, P])
        st = m.sb("st1", [P, T, 6])
        mv = m.sb("mv1", [P, T, 2])
        ve = m.sb("ve1", [P, T])
        mhalf = m.sb("mhalf1", [P, T])
        rstd = m.sb("rstd1", [P, T])
        xn = m.sb("xn1", [P, T, D])
        xsq = m.sb("xsq", [P, D])
        nsq = m.sb("nsq", [P, T])
        xh = m.sb("xh1", [P, KD, T * P], F32R)
        xl = m.sb("xl1", [P, KD, T * P], F32R)
        xT = m.sb("xT1", [P, KD, T * P])
        rin = m.sb("rin", [P, 2, TAPS - 1 + S])
        cv = m.sb("cv", [P, 2, S])
        u = m.sb("u", [P, B, HT, S])
        uh = m.sb("uh", [P, B, HT, S], F32R)
        ul = m.sb("ul", [P, B, HT, S], F32R)
        left = m.sb("left", [P, B, HT, S])
        acts = m.sb("acts", [P, 4, HT * S])
        ta, ti, dec, sqd = (acts[:, i, :].rearrange("p (k n) -> p k n", n=S) for i in range(4))
        drv = m.sb("drv", [P, HT, S])
        ph = m.sb("ph", [P, HT, S], F32R)
        pl = m.sb("pl", [P, HT, S], F32R)
        w_lr = drv[:, :, :].rearrange("p k n -> p (k n)").rearrange("p (k n) -> p k n", n=2 * HP)
        w_ai = acts[:, 0:2, :].rearrange("p a n -> p (a n)")[:, 0:HT * 2 * HP].rearrange("p (k n) -> p k n", n=2 * HP)
        w_o = acts[:, 2, 0:HT * D].rearrange("p (k n) -> p k n", n=D)
        Y = m.sb("Y", [P, T, FW])
        fc = m.sb("fc", [2 * N_SEL, FW])
        fcm = m.sb("fcm", [2 * N_SEL, FW])
        fb = m.sb("fb", [P, FW])
        f1 = m.sb("f1", [P, T, N_SEL * S_SEL])
        z = m.sb("z", [P, 6, T, N_SEL])
        zm = m.sb("zm", [P, 3, T])
        ZO = m.sb("ZO", [P, T, OW])
        ZT = m.sb("ZT", [OW, T * P])
        ed = m.sb("ed", [P, T, D])
        eth = xT[:, :, :].rearrange("p k n -> p (k n)").rearrange("p (t d) -> p t d", d=D)
        o1 = [left[:, b, 0:2, :].rearrange("p a (i d) -> p (a i) d", d=D) for b in range(B)]

        bank = [m.ps(f"lbank{i}") for i in range(8)]

        sems = {}

        def sem(name):
            if name not in sems:
                sems[name] = m.sem("l1_" + name)
            return sems[name]

        w_in = {n: m.sem("in_" + n) for n in ("lr", "ai", "o", "f", "vec", "selc")}
        var_ready, rstd_ready, xn_ready, nsq_ready = (sem(n) for n in ("var", "rstd", "xn", "nsq"))
        xT_ready, xh_ready, xl_ready = sem("xT"), sem("xh"), sem("xl")
        wh_ready, wl_ready = sem("wh"), sem("wl")
        R_ready, rin_ready, u_ready, uh_ready, ul_ready = (
            sem(n) for n in ("R", "rin", "u", "uh", "ul"))
        vec_ready, vec_exp, vec_dve, vec_ln, half_done = (sem(n) for n in ("vecr", "vexp", "vdve", "vln", "half"))
        A_ready, I_ready, ta_ready, ti_ready, dec_ready, sqd_ready, om_ready, beta_ready = (
            sem(n) for n in ("A", "I", "ta", "ti", "dec", "sqd", "om", "beta"))
        L_ready, left_ready, prod_ready, ph_ready, pl_ready, O_ready = (
            sem(n) for n in ("L", "left", "prod", "ph", "pl", "O"))
        F_ready, F_read, fc_ready, fcm_ready, fb_ready, fb_read = (
            sem(n) for n in ("F", "Fread", "fc", "fcm", "fb", "fbread"))
        z_ready, ez_ready, ZO_ready, ZT_ready, ZT_read, D_ready, ed_ready, eth_ready, out_ready = (
            sem(n) for n in ("z", "ez", "ZO", "ZT", "ZTread", "Dg", "ed", "eth", "out"))
        o_read, gated_ready = sem("o_read"), sem("gated")
        xT_copied = sem("xTc")
        tap_ready, edited, D_read = sem("tap"), sem("edited"), sem("Dread")
        dve_step, act_step, pool_step, stored = sem("dve_step"), sem("act_step"), sem("pool_step"), sem("stored")

        def tokens(t):
            return slice(t * P, (t + 1) * P)

        block = ctx.enter_context(nc.Block())

        @block.sync
        def _(sp):
            def load(dst, src, s):
                sp.dma_start(dst, src).then_inc(w_in[s], 16)
            load(w_lr, a["w_lr"].rearrange("(k p) n -> p k n", p=P), "lr")
            load(w_f[:, :, :], a["w_f"].rearrange("(k p) n -> p k n", p=P), "f")
            load(md[:, :, :], a["w_md"].rearrange("(k p) n -> p k n", p=P), "f")
            load(fmask[:, :], a["c_fmask"], "f")
            load(ones16[:, :], a["c_ones16"], "f")
            load(vec[:, :, :], a["vecs"], "vec")
            load(w_ai, a["w_ai"].rearrange("(k p) n -> p k n", p=P), "ai")
            load(w_o, a["w_o1"].rearrange("(k p) n -> p k n", p=P), "o")
            load(w_g[:, :], a["w_g"], "selc")
            load(sel_vec[:, 0, :], a["L1_ffn_imp_center"].unsqueeze(0).broadcast_to([P, N_SEL]), "selc")
            load(sel_vec[:, 1, :], a["L1_ffn_imp_slope"].unsqueeze(0).broadcast_to([P, N_SEL]), "selc")
            load(sel_vec[:, 2, :], a["c_rank"], "selc")
            load(bo[:, :], a["L1_attn_bo"].unsqueeze(0).broadcast_to([P, D]), "selc")
            dst = out.rearrange("(t p) d -> p t d", p=P)
            for t in range(T):
                sp.wait_ge(out_ready, t + 1)
                sp.dma_start(dst[:, t, :], o1[t // TB][:, t % TB, :]).then_inc(stored, 16)
            sp.wait_ge(stored, 16 * T)

        @block.gpsimd
        def _(pool):
            pool.memset(mhalf[:, :], -0.5).then_inc(half_done, 1)
            pool.memset(rin[:, :, 0:TAPS - 1], 0.0).then_inc(half_done, 1)
            pool.wait_ge(half_done, 1)
            for b in range(B):
                tb = slice(b * TB, (b + 1) * TB)
                pool.wait_ge(var_ready, b + 1)
                pool.tensor_tensor(rstd[:, tb], ve[:, tb], mhalf[:, tb], ALU.pow).then_inc(rstd_ready, 1)
            for k, (lo, raw, hi) in enumerate(((w_lr_l, w_lr, w_lr_h), (w_ai_l, w_ai, w_ai_h), (w_o_l, w_o, w_o_h))):
                pool.wait_ge(wh_ready, k + 1)
                pool.tensor_tensor(lo[:, :, :], raw, hi[:, :, :].bitcast(F32), ALU.subtract).then_inc(wl_ready, 1)
            def rests_of_u(b):
                for p in range(HT):
                    n = b * HT + p
                    pool.wait_ge(uh_ready, n + 1)
                    pool.tensor_tensor(ul[:, b, p, :], u[:, b, p, :], uh[:, b, p, :].bitcast(F32),
                                       ALU.subtract).then_inc(ul_ready, 1)

            def rests_of_products(b):
                for p in range(HT):
                    pool.wait_ge(ph_ready, b * HT + p + 1)
                    if b:
                        pool.wait_ge(O_ready, 1)
                    pool.tensor_tensor(pl[:, p, :], drv[:, p, :], ph[:, p, :].bitcast(F32),
                                       ALU.subtract).then_inc(pl_ready, 1)

            rests_of_u(0)
            rests_of_u(1)
            rests_of_products(0)
            rests_of_products(1)
            for t in range(T):
                pool.wait_ge(gated_ready, t + 1)
                pool.tensor_tensor(o1[t // TB][:, t % TB, :], xn[:, t, :], x1[:, t, :], ALU.add).then_inc(out_ready, 1)

        @block.scalar
        def _(act):
            link = chain(act, act_step)
            act.wait_ge(w_in["lr"], 16)
            act.copy(w_lr_h[:, :, :], w_lr).then_inc(wh_ready, 1)
            for n in range(2 * B):
                b, c = n // 2, n % 2
                act.wait_ge(xT_ready, n + 1)
                act.copy(xh[:, c, b * S:(b + 1) * S], bank[n][:, :]).then_inc(xh_ready, 1)
            act.wait_ge(half_done, 2)

            def convolution_in(b):
                for p in range(HT):
                    n = b * HT + p
                    act.wait_ge(R_ready, n + 1)
                    if n >= 2:
                        act.wait_ge(u_ready, n - 1)
                    act.activation(rin[:, n % 2, TAPS - 1:], bank[4 + p][:, :], ACT.Identity,
                                   bias=vec[:, 1, p:p + 1]).then_inc(rin_ready, 1)
                    act.wait_ge(rin_ready, n + 1)
                    act.activation(cv[:, n % 2, :], rin[:, n % 2, 0:S], ACT.Identity, scale=vec[:, 6, p:p + 1],
                                   bias=vec[:, 2, p:p + 1]).then_inc(tap_ready, 1)

            def split_u(b):
                for p in range(HT):
                    act.wait_ge(u_ready, b * HT + p + 1)
                    act.copy(uh[:, b, p, :], u[:, b, p, :]).then_inc(uh_ready, 1)

            def left_gelu(b):
                for p in range(HT):
                    act.wait_ge(L_ready, b * HT + p + 1)
                    act.activation(left[:, b, p, :], bank[p][:, :], ACT.Gelu_apprx_tanh,
                                   bias=vec[:, 0, p:p + 1]).then_inc(left_ready, 1)

            def decays(b):
                act.wait_ge(vec_ready, 1)
                act.wait_ge(wl_ready, 3)
                if b:
                    act.wait_ge(prod_ready, HT)
                for p in range(HT):
                    n = b * HT + p
                    act.wait_ge(A_ready, n + 1)
                    act.activation(ta[:, p, :], bank[p][:, :], ACT.Tanh, scale=0.5,
                                   bias=vec2[:, 4, p:p + 1]).then_inc(ta_ready, 1)
                    act.wait_ge(ta_ready, n + 1)
                    act.activation(sqd[:, p, :], ta[:, p, :], ACT.Exp, scale=vec2[:, 7, p:p + 1],
                                   bias=vec2[:, 7, p:p + 1]).then_inc(sqd_ready, 1)
                    act.activation(dec[:, p, :], ta[:, p, :], ACT.Exp, scale=vec2[:, 6, p:p + 1],
                                   bias=vec2[:, 6, p:p + 1]).then_inc(dec_ready, 1)

            def roots_and_inputs(b):
                for p in range(HT):
                    act.wait_ge(om_ready, b * HT + p + 1)
                    act.activation(sqd[:, p, :], sqd[:, p, :], ACT.Sqrt, scale=-1.0).then_inc(beta_ready, 1)
                for p in range(HT):
                    act.wait_ge(I_ready, b * HT + p + 1)
                    act.activation(ti[:, p, :], bank[3 + p][:, :], ACT.Tanh, scale=0.5,
                                   bias=vec2[:, 5, p:p + 1]).then_inc(ti_ready, 1)

            def split_products(b):
                for p in range(HT):
                    act.wait_ge(prod_ready, b * HT + p + 1)
                    if b:
                        act.wait_ge(O_ready, 1)
                    act.copy(ph[:, p, :], drv[:, p, :]).then_inc(ph_ready, 1)

            def transposed_selection():
                for n in range(2):
                    act.wait_ge(ZT_ready, n + 1)
                    act.copy(ZT[:, n * 512:(n + 1) * 512], bank[6 + n][0:OW, :]).then_inc(ZT_read, 1)

            act.wait_ge(w_in["vec"], 16)
            convolution_in(0)
            act.wait_ge(w_in["ai"], 16)
            act.copy(w_ai_h[:, :, :], w_ai).then_inc(wh_ready, 1)
            split_u(0)
            act.wait_ge(vec_dve, 1)
            act.activation(vec2[:, 1, :], vec2[:, 0, :], ACT.Exp, scale=-1.0).then_inc(vec_exp, 1)
            for t in range(T):
                act.wait_ge(xn_ready, t + 1)
                if t:
                    act.wait_ge(nsq_ready, t)
                act.activation(xsq[:, :], xn[:, t, :], ACT.Square, accum_out=nsq[:, t:t + 1]).then_inc(nsq_ready, 1)
            act.wait_ge(w_in["o"], 16)
            act.copy(w_o_h[:, :, :], w_o).then_inc(wh_ready, 1)
            left_gelu(0)
            convolution_in(1)
            left_gelu(1)
            split_u(1)
            act.wait_ge(vec_dve, 2)
            act.activation(vec2[:, 3, :], vec2[:, 2, :], ACT.Ln).then_inc(vec_ln, 1)
            act.wait_ge(z_ready, 1)
            act.activation(z[:, 2, :, :], z[:, 1, :, :], ACT.Exp, scale=-1.0).then_inc(ez_ready, 1)
            decays(0)
            roots_and_inputs(0)
            transposed_selection()
            split_products(0)
            decays(1)
            for t in range(T):
                act.wait_ge(ed_ready, t + 1)
                act.activation(eth[:, t, :], ed[:, t, :], ACT.Tanh, scale=0.5).then_inc(eth_ready, 1)
            roots_and_inputs(1)
            split_products(1)

        @block.vector
        def _(dve):
            link = chain(dve, dve_step)
            for b in range(B):
                for t in range(b * TB, (b + 1) * TB):
                    ins = dve.bn_stats(st[:, t, :], x1[:, t, :])
                link(ins)
                for t in range(b * TB, (b + 1) * TB):
                    ins = dve.bn_aggr(mv[:, t, :], st[:, t, :])
                link(ins)
                tb = slice(b * TB, (b + 1) * TB)
                dve.tensor_scalar(ve[:, tb], mv[:, tb, 1], LN_EPS, None, ALU.add).then_inc(var_ready, 1)
            for b in range(B):
                dve.wait_ge(rstd_ready, b + 1)
                for t in range(b * TB, (b + 1) * TB):
                    dve.tensor_scalar(xn[:, t, :], x1[:, t, :], mv[:, t, 0:1], rstd[:, t:t + 1],
                                      ALU.subtract, ALU.mult).then_inc(xn_ready, 1)
            for n in range(2 * B):
                b, c = n // 2, n % 2
                part = (slice(None), c, slice(b * S, (b + 1) * S))
                dve.wait_ge(xh_ready, n + 1)
                dve.tensor_tensor(xl[part], bank[n][:, :], xh[part].bitcast(F32), ALU.subtract).then_inc(xl_ready, 1)
            for n in range(2 * B):
                b, c = n // 2, n % 2
                dve.tensor_copy(xT[:, c, b * S:(b + 1) * S], bank[n][:, :]).then_inc(xT_copied, 1)
            dve.wait_ge(w_in["vec"], 16)
            link(dve.tensor_scalar(vec2[:, 8, :], vec[:, 5, :], -1.0, None, ALU.mult))
            dve.tensor_tensor(vec2[:, 0, :], vec[:, 5, :], vec2[:, 8, :], ALU.max).then_inc(vec_dve, 1)

            def decay_constants():
                dve.wait_ge(vec_exp, 1)
                dve.tensor_scalar(vec2[:, 2, :], vec2[:, 1, :], 1.0, None, ALU.add).then_inc(vec_dve, 1)
                dve.wait_ge(vec_dve, 2)
                link(dve.tensor_scalar(vec2[:, 6, :], vec2[:, 2, :], 1.0, None, ALU.subtract))
                link(dve.tensor_scalar(vec2[:, 7, :], vec2[:, 6, :], 0.0, None, ALU.is_equal))
                link(dve.tensor_tensor(vec2[:, 6, :], vec2[:, 6, :], vec2[:, 7, :], ALU.add))
                link(dve.reciprocal(vec2[:, 6, :], vec2[:, 6, :]))
                dve.wait_ge(vec_ln, 1)
                link(dve.tensor_tensor(vec2[:, 6, :], vec2[:, 6, :], vec2[:, 3, :], ALU.mult))
                link(dve.tensor_tensor(vec2[:, 6, :], vec2[:, 6, :], vec2[:, 7, :], ALU.add))
                link(dve.tensor_tensor(vec2[:, 6, :], vec2[:, 6, :], vec2[:, 1, :], ALU.mult))
                link(dve.scalar_tensor_tensor(out=vec2[:, 8, :], in0=vec2[:, 8, :], scalar=0.0, in1=vec2[:, 6, :],
                                              op0=ALU.max, op1=ALU.add))
                dve.tensor_scalar(vec2[:, 6, :], vec2[:, 8, :], -4.0, None, ALU.mult)
                dve.tensor_scalar(vec2[:, 7, :], vec2[:, 8, :], -8.0, None, ALU.mult)
                dve.tensor_scalar(vec2[:, 4:6, :], vec[:, 3:5, :], 0.5, None, ALU.mult).then_inc(vec_ready, 1)

            def conv(b, p):
                n = b * HT + p
                dve.wait_ge(tap_ready, n + 1)
                r, c = rin[:, n % 2, :], cv[:, n % 2, :]
                for k in (1, 2):
                    link(dve.scalar_tensor_tensor(out=c, in0=r[:, k:S + k], scalar=vec[:, 6 + k, p:p + 1],
                                                  in1=c, op0=ALU.mult, op1=ALU.add))
                dve.scalar_tensor_tensor(out=u[:, b, p, :], in0=r[:, 3:S + 3], scalar=vec[:, 9, p:p + 1],
                                         in1=c, op0=ALU.mult, op1=ALU.add).then_inc(u_ready, 1)

            def edit_in():
                dve.wait_ge(fc_ready, 1)
                dve.tensor_tensor(fcm[:, :], bank[7][0:2 * N_SEL, 0:FW], fmask[:, :], ALU.mult).then_inc(fcm_ready, 1)
                dve.wait_ge(fb_ready, 1)
                dve.tensor_copy(fb[:, :], bank[7][:, 0:FW]).then_inc(fb_read, 1)
                for t in range(T):
                    dve.wait_ge(F_ready, t + 1)
                    dve.tensor_copy(Y[:, t, :], bank[3 + t % 2 * 4][:, 0:FW]).then_inc(F_read, 1)
                dve.wait_ge(F_read, T)
                dve.wait_ge(fb_read, 1)
                dve.wait_ge(nsq_ready, T)
                NS = N_SEL * S_SEL
                link(dve.tensor_tensor(f1[:, :, :], Y[:, :, 0:NS], spread(fb[:, 0:NS], 1, T), ALU.subtract))
                link(dve.tensor_tensor(f1[:, :, :], f1[:, :, :], f1[:, :, :], ALU.mult))
                link(dve.tensor_reduce(z[:, 0, :, :].rearrange("p t n -> p (t n)"),
                                       f1[:, :, :].rearrange("p t (n s) -> p (t n) s", s=S_SEL), AX.X, ALU.add))
                link(dve.scalar_tensor_tensor(out=z[:, 1, :, :], in0=Y[:, :, 2 * NS:FW], scalar=-2.0,
                                              in1=spread(fb[:, 2 * NS:FW], 1, T), op0=ALU.mult, op1=ALU.add))
                link(dve.tensor_tensor(z[:, 1, :, :], z[:, 1, :, :], spread(nsq[:, :], 2, N_SEL), ALU.add))
                link(dve.reciprocal(z[:, 2, :, :], z[:, 1, :, :]))
                link(dve.tensor_tensor(z[:, 0, :, :], z[:, 0, :, :], z[:, 2, :, :], ALU.mult))
                dve.wait_ge(w_in["selc"], 16 * 5)
                link(dve.tensor_tensor(z[:, 0, :, :], z[:, 0, :, :], spread(sel_vec[:, 0, :], 1, T), ALU.subtract))
                link(dve.tensor_tensor(z[:, 1, :, :], z[:, 0, :, :], spread(sel_vec[:, 1, :], 1, T), ALU.mult))
                dve.tensor_scalar(z[:, 1, :, :], z[:, 1, :, :], -88.0, None, ALU.max).then_inc(z_ready, 1)

            def edit_select():
                NS = N_SEL * S_SEL
                dve.wait_ge(ez_ready, 1)
                link(dve.tensor_scalar(z[:, 3, :, :], z[:, 2, :, :], 1.0, None, ALU.add))
                link(dve.reciprocal(z[:, 0, :, :], z[:, 3, :, :]))
                link(dve.tensor_reduce(zm[:, 1, :], z[:, 0, :, :], AX.X, ALU.max))
                link(dve.tensor_tensor(z[:, 3, :, :], z[:, 0, :, :], spread(zm[:, 1, :], 2, N_SEL), ALU.is_equal))
                link(dve.tensor_tensor(z[:, 4, :, :], z[:, 3, :, :], spread(sel_vec[:, 2, :], 1, T), ALU.mult))
                link(dve.tensor_reduce(zm[:, 2, :], z[:, 4, :, :], AX.X, ALU.max))
                link(dve.tensor_tensor(ZO[:, :, NS:OW], z[:, 4, :, :], spread(zm[:, 2, :], 2, N_SEL), ALU.is_equal))
                link(dve.tensor_tensor(f1[:, :, :], Y[:, :, NS:2 * NS], spread(fb[:, NS:2 * NS], 1, T), ALU.subtract))
                for t in range(T):
                    ins = dve.tensor_tensor(ZO[:, t, 0:NS].rearrange("p (n h) -> p n h", h=H_SEL),
                                            f1[:, t, :].rearrange("p (n h) -> p n h", h=H_SEL),
                                            spread(ZO[:, t, NS:OW], 2, H_SEL), ALU.mult)
                ins.then_inc(ZO_ready, 1)

            def root_arguments(b):
                for p in range(HT):
                    dve.wait_ge(sqd_ready, b * HT + p + 1)
                    dve.tensor_scalar(sqd[:, p, :], sqd[:, p, :], 1.0, -1e-12, ALU.subtract,
                                      ALU.min).then_inc(om_ready, 1)

            def recurrence(b):
                for p in range(HT):
                    n = b * HT + p
                    dve.wait_ge(ti_ready, n + 1)
                    link(dve.scalar_tensor_tensor(out=ti[:, p, :], in0=ti[:, p, :], scalar=1.0, in1=u[:, b, p, :],
                                                  op0=ALU.add, op1=ALU.mult))
                    dve.wait_ge(beta_ready, n + 1)
                    if b:
                        dve.wait_ge(pl_ready, p + 1)
                    link(dve.scalar_tensor_tensor(out=drv[:, p, :], in0=ti[:, p, :], scalar=0.5, in1=sqd[:, p, :],
                                                  op0=ALU.mult, op1=ALU.mult))
                    dve.wait_ge(dec_ready, n + 1)
                    link(dve.tensor_tensor_scan(ti[:, p, :], dec[:, p, :], drv[:, p, :], 0.0, ALU.mult, ALU.add))
                    dve.wait_ge(left_ready, n + 1)
                    dve.tensor_tensor(drv[:, p, :], ti[:, p, :], left[:, b, p, :], ALU.mult).then_inc(prod_ready, 1)

            def gated_out(b):
                for k in range(2):
                    dve.wait_ge(O_ready, b + 1)
                    dve.tensor_tensor(o1[b][:, 2 * k:2 * k + 2, :], bank[6 + k][:, :].rearrange("p (t d) -> p t d", d=D),
                                      spread(bo[:, :], 1, 2), ALU.add).then_inc(o_read, 1)
                for t in range(b * TB, (b + 1) * TB):
                    dve.wait_ge(o_read, 2 * b + (t % TB) // 2 + 1)
                    dve.wait_ge(edited, t + 1)
                    dve.scalar_tensor_tensor(out=xn[:, t, :], in0=o1[b][:, t % TB, :], scalar=0.5, in1=ed[:, t, :],
                                             op0=ALU.mult, op1=ALU.mult).then_inc(gated_ready, 1)

            for p in range(HT):
                conv(0, p)
            edit_in()
            for p in range(HT):
                conv(1, p)
            decay_constants()
            dve.wait_ge(w_in["selc"], 16 * 5)
            edit_select()
            root_arguments(0)
            recurrence(0)
            for t in range(T):
                dve.wait_ge(D_ready, t // 2 + 1)
                if t >= 2:
                    dve.wait_ge(ed_ready, t - 1)
                dve.tensor_tensor(ed[:, t, :], bank[6 + t // 2 % 2][:, t % 2 * D:(t % 2 + 1) * D], xn[:, t, :],
                                  ALU.subtract).then_inc(D_read, 1)
                dve.wait_ge(D_read, t + 1)
                dve.scalar_tensor_tensor(out=ed[:, t, :], in0=ed[:, t, :], scalar=zm[:, 1, t:t + 1],
                                         in1=xn[:, t, :], op0=ALU.mult, op1=ALU.add).then_inc(ed_ready, 1)
            root_arguments(1)
            for t in range(T):
                dve.wait_ge(eth_ready, t + 1)
                dve.scalar_tensor_tensor(out=ed[:, t, :], in0=eth[:, t, :], scalar=1.0, in1=ed[:, t, :],
                                         op0=ALU.add, op1=ALU.mult).then_inc(edited, 1)
            gated_out(0)
            recurrence(1)
            gated_out(1)

        @block.tensor
        def _(pe):
            for n in range(2 * B):
                b, c = n // 2, n % 2
                for i in range(TB):
                    pe.wait_ge(xn_ready, b * TB + i + 1)
                    ins = pe.transpose(bank[n][:, i * P:(i + 1) * P], xn[:, b * TB + i, c * P:(c + 1) * P], ident[:, :])
                ins.then_inc(xT_ready, 1)

            def branch_in(b, side, first_bank, done):
                for p in range(HT):
                    w = slice(side * HP + p * P, side * HP + (p + 1) * P)
                    if b and side:
                        pe.wait_ge(rin_ready, p + 1)
                    if b and not side:
                        pe.wait_ge(left_ready, p + 1)
                    for k in range(KD):
                        ins = split_matmul(pe, bank[first_bank + p][:, :], w_lr_h[:, k, w], w_lr_l[:, k, w],
                                           xh[:, k, b * S:(b + 1) * S], xl[:, k, b * S:(b + 1) * S],
                                           k == 0, k == KD - 1)
                    ins.then_inc(done, 1)

            def gates(b, which):
                pe.wait_ge(wl_ready, 2)
                if b == 0:
                    pe.wait_ge(left_ready, B * HT)
                    pe.wait_ge(rin_ready, B * HT)
                    pe.wait_ge(F_read, T)
                for g in which:
                    done, read = ((A_ready, ta_ready), (I_ready, ti_ready))[g]
                    for p in range(HT):
                        if b:
                            pe.wait_ge(read, p + 1)
                        w = slice(g * HP + p * P, g * HP + (p + 1) * P)
                        for k in range(HT):
                            pe.wait_ge(ul_ready, b * HT + k + 1)
                            ins = split_matmul(pe, bank[3 * g + p][:, :], w_ai_h[:, k, w], w_ai_l[:, k, w],
                                               uh[:, b, k, :], ul[:, b, k, :], k == 0, k == HT - 1)
                        ins.then_inc(done, 1)

            def mix_out(b):
                pe.wait_ge(wl_ready, 3)
                pe.wait_ge(D_read, T)
                if b:
                    pe.wait_ge(o_read, 2)
                for k in range(HT):
                    pe.wait_ge(pl_ready, b * HT + k + 1)
                    for i in range(TB):
                        ins = split_matmul(pe, bank[6 + i // 2][:, i % 2 * D:(i % 2 + 1) * D],
                                           ph[:, k, tokens(i)], pl[:, k, tokens(i)], w_o_h[:, k, :], w_o_l[:, k, :],
                                           k == 0 and i % 2 == 0, k == HT - 1, skip=True)
                ins.then_inc(O_ready, 1)

            def edit_products():
                pe.wait_ge(w_in["f"], 64)
                for k in range(KD):
                    ins = pe.matmul(bank[7][0:2 * N_SEL, 0:FW], md[:, k, :], w_f[:, k, :],
                                    start=(k == 0), stop=(k == KD - 1))
                ins.then_inc(fc_ready, 1)
                pe.wait_ge(fcm_ready, 1)
                pe.matmul(bank[7][:, 0:FW], ones16[:, :], fcm[:, :], start=True, stop=True).then_inc(fb_ready, 1)
                pe.wait_ge(fb_read, 1)
                for t in range(T):
                    if t >= 2:
                        pe.wait_ge(F_read, t - 1)
                    for k in range(KD):
                        ins = pe.matmul(bank[3 + t % 2 * 4][:, 0:FW], xT[:, k, tokens(t)], w_f[:, k, :],
                                        start=(k == 0), stop=(k == KD - 1))
                    ins.then_inc(F_ready, 1)

            def edit_update():
                pe.wait_ge(ZO_ready, 1)
                for t in range(T):
                    ins = pe.transpose(bank[6 + t // TB][0:OW, t % TB * P:(t % TB + 1) * P], ZO[:, t, :], ident[:, :])
                    if t % TB == TB - 1:
                        ins.then_inc(ZT_ready, 1)
                pe.wait_ge(w_in["selc"], 16 * 5)
                pe.wait_ge(ZT_read, 2)
                for n in range(TB):
                    if n >= 2:
                        pe.wait_ge(D_read, 2 * (n - 1))
                    for t in (2 * n, 2 * n + 1):
                        ins = pe.matmul(bank[6 + n % 2][:, t % 2 * D:(t % 2 + 1) * D], ZT[:, tokens(t)], w_g[:, :],
                                        start=True, stop=True)
                    ins.then_inc(D_ready, 1)

            pe.wait_ge(wl_ready, 1)
            pe.wait_ge(xl_ready, 2)
            branch_in(0, 1, 4, R_ready)
            pe.wait_ge(xT_copied, 2 * B)
            branch_in(0, 0, 0, L_ready)
            edit_products()
            branch_in(1, 1, 4, R_ready)
            branch_in(1, 0, 0, L_ready)
            gates(0, (0, 1))
            gates(1, (0,))
            edit_update()
            mix_out(0)
            gates(1, (1,))
            mix_out(1)


_OUTS = [((2, 512, 256), 'float32')]


def _constants():
    f, bf = np.float32, np.dtype("bfloat16")
    pos = np.arange(S, dtype=f)
    inv = (1.0 / 10000.0 ** (np.arange(0, DH, 2).astype(f) / f(DH))).astype(f)
    ang = (pos[:, None] * inv).astype(f)
    cos, sin = np.cos(ang).astype(f), np.sin(ang).astype(f)
    tok = np.arange(P)

    def by_tile(v):
        return np.ascontiguousarray(v.reshape(TB, P, -1).transpose(1, 0, 2))
    own = np.arange(S)[:, None] // BLK
    blk = np.arange(NBLK)[None, :]
    gate_add = np.where(blk > own, f(NEG), np.where(blk == own, f(-NEG), f(0))).astype(f)
    later = (tok[None, :] > tok[:, None])
    ksel = np.zeros((64, ECH, P), f)
    unit = np.arange(ECH * P).reshape(ECH, P)
    for level in range(3):
        for e in range(E):
            ksel[level * E + e] = (unit // EH == e)
    kconst = np.ones((R_ALL - R_BIAS, T * P), f)
    kconst[:NBLK] = (np.arange(T * P)[None, :] % S // BLK) == np.arange(NBLK)[:, None]
    fmask = np.zeros((2 * N_SEL, FW), f)
    for n in range(N_SEL):
        fmask[n, n * S_SEL:(n + 1) * S_SEL] = 1
        fmask[N_SEL + n, N_SEL * S_SEL + n * H_SEL:N_SEL * S_SEL + (n + 1) * H_SEL] = 1
        fmask[n, 2 * N_SEL * S_SEL + n] = 1
    return {
        "c_ident": np.eye(P, dtype=f),
        "c_cos": by_tile(np.concatenate([cos, cos], 1)),
        "c_sin": by_tile(np.concatenate([-sin, sin], 1)),
        "c_gate_add": by_tile(gate_add),
        "c_future": np.where(blk > tok[:, None] // BLK, f(NEG), f(0)).astype(f),
        "c_headmask": np.repeat((tok[:, None] // DH == np.arange(8)[None, :]).astype(f)[:, :, None], NBLK, 2),
        "c_tri": np.stack([np.where(later, f(NEG), f(0)), np.where(later.T, f(NEG), f(0))], 1).astype(bf),
        "c_ksel": ksel.astype(bf),
        "c_kconst": kconst.astype(bf),
        "c_ident_b": np.eye(P, dtype=f).astype(bf),
        "c_fmask": fmask,
        "c_ones16": np.ones((2 * N_SEL, P), f),
        "c_rank": np.tile(np.arange(N_SEL, 0, -1, dtype=f), (P, 1)),
    }


def _layout(v):
    def pad(w, rows, cols):
        return np.pad(w, ((0, rows - w.shape[0]), (0, cols - w.shape[1])))

    def wide(w):
        return w.transpose(1, 0, 2).reshape(D, E * EH)
    gate = np.concatenate([wide(v["L0_ffn_w_gate"]), pad(v["L0_ffn_sw_gate"], D, SCH * P)], 1)
    up = np.concatenate([wide(v["L0_ffn_w_up"]), pad(v["L0_ffn_sw_up"], D, SCH * P)], 1)
    down = np.concatenate([v["L0_ffn_w_down"].reshape(E * EH, D), pad(v["L0_ffn_sw_down"], SCH * P, D)], 0)
    chunks = np.empty((CH, P, 3, 2 * P), np.float32)
    for w, o in ((gate, 0), (up, P)):
        chunks[:, :, 0:KD, o:o + P] = w.reshape(KD, P, CH, P).transpose(2, 1, 0, 3)
    chunks[:, :, 2, :] = down.reshape(CH, P, D)
    vecs = [v["L1_attn_" + n] for n in ("bl", "br", "conv_b", "ba", "bi", "lam")] + list(v["L1_attn_conv_w"][:, 0])
    vecs = np.stack([np.pad(w, (0, HP - HID)).reshape(HT, P) for w in vecs])

    def side(w):
        return w.transpose(1, 0, 2).reshape(D, -1)
    return {
        "x": v["L0_attn_hidden_states"].reshape(B * S, D),
        "w_proj": np.concatenate([v["L0_attn_Wq"].T, v["L0_attn_Wk"].T, v["L0_attn_Wv"].T, v["L0_ffn_gate_w"]], 1),
        "w_o": v["L0_attn_Wo"].T,
        "w_chunks": chunks,
        "w_lr": np.concatenate([pad(v["L1_attn_Wl"], D, HP), pad(v["L1_attn_Wr"], D, HP)], 1),
        "w_ai": np.concatenate([pad(v["L1_attn_Wa"], HP, HP), pad(v["L1_attn_Wi"], HP, HP)], 1),
        "w_o1": pad(v["L1_attn_Wo"], HP, D),
        "w_f": np.concatenate([side(v["L1_ffn_select_weight"]), side(v["L1_ffn_lora_update"]),
                               v["L1_ffn_select_mean_diff"].T], 1),
        "w_md": np.concatenate([v["L1_ffn_select_mean_diff"].T, v["L1_ffn_debias_w"].T], 1),
        "w_g": np.concatenate([v["L1_ffn_lora_degen"].transpose(0, 2, 1).reshape(N_SEL * H_SEL, D),
                               v["L1_ffn_bias_w"]], 0),
        "vecs": vecs.transpose(2, 0, 1),
        "L0_attn_o_norm_w": v["L0_attn_o_norm_w"],
        "L1_ffn_imp_center": v["L1_ffn_imp_center"],
        "L1_ffn_imp_slope": v["L1_ffn_imp_slope"],
        "L1_attn_bo": v["L1_attn_bo"],
    }


def program(nc, a, out):
    with ExitStack() as ctx:
        m = Mem(nc, ctx)
        x1 = m.sb("x1", [P, T, D])
        cst = {"ident": m.sb("ident", [P, P]), "ident_b": m.sb("ident_b", [P, P], BF16),
               "ident_in": m.sem("ident_in")}
        layer0(nc, a, x1, cst)
        layer1(nc, a, x1, out, cst)


def kernel(**inputs):
    import numpy as _np
    import concourse.bacc as _bacc
    from concourse import mybir as _mybir
    from concourse.bass_utils import run_bass_kernel_spmd as _run

    nc = _bacc.Bacc("TRN2", target_bir_lowering=False, num_devices=1)
    data = _layout({k: _np.asarray(v) for k, v in inputs.items()})
    data.update(_constants())
    arrays, args = {}, {}
    for name, v in data.items():
        v = _np.ascontiguousarray(v)
        arrays[f"in_{name}_dram"] = v
        args[name] = nc.dram_tensor(f"in_{name}_dram", v.shape, _mybir.dt.from_np(v.dtype), kind="ExternalInput").ap()
    (shape, dtype), = _OUTS
    out = nc.dram_tensor("out_0_dram", shape, _mybir.dt.from_np(_np.dtype(dtype)), kind="ExternalOutput").ap()
    program(nc, args, out.rearrange("b s d -> (b s) d"))
    r = _run(nc, [arrays], core_ids=[0])
    return r.results[0]["out_0_dram"]
```
